# Optimizing a Trainium2 kernel written in Bass

```python
import numpy as np
import jax
import jax.numpy as jnp

def _softmax(x, axis=-1):
    return jax.nn.softmax(x, axis=axis)

def _gelu(x):
    return jax.nn.gelu(x, approximate=True)

def _silu(x):
    return jax.nn.silu(x)

def _sigmoid(x):
    return jax.nn.sigmoid(x)

def _layernorm(x, axis=-1, eps=1e-05):
    m = jnp.mean(x, axis=axis, keepdims=True)
    v = jnp.var(x, axis=axis, keepdims=True)
    return (x - m) / jnp.sqrt(v + eps)

def _scatter_add(tgt, idx, src, axis=0):
    return tgt.at[idx].add(src)

def _segment_sum(src, seg, n):
    return jax.ops.segment_sum(src, seg, n)
kernel_name = 'mk_flamingo_gated_d2_seqx_r4_00c1f3'

def setup_inputs(seed: int=0):
    np.random.seed(seed)
    _w = jnp.asarray

    def _rec_inputs():
        import jax
        import jax.numpy as jnp
        _rk = jax.random.key(seed)
        x = -0.0003929 + 0.9999 * jax.random.normal(jax.random.fold_in(_rk, 1), (4, 1024, 256), jnp.float32)
        _lenS = 1024 - jax.random.randint(jax.random.fold_in(_rk, 7), (4,), 0, max(1, 1024 // 4) + 1, jnp.int32)
        _lenS2 = 77 - jax.random.randint(jax.random.fold_in(_rk, 8), (4,), 0, max(1, 77 // 4) + 1, jnp.int32)
        _ctx_512P = jax.random.normal(jax.random.fold_in(_rk, 11), (4, 16, 128), jnp.float32)
        _ctx_512c = jax.random.dirichlet(jax.random.fold_in(_rk, 511), 0.3 * jnp.ones((16,), jnp.float32), (4, 77))
        _ctx_512t = jnp.einsum('bsk,bkd->bsd', _ctx_512c, _ctx_512P)
        _ctx_512t = _ctx_512t * jax.lax.rsqrt(jnp.mean(jnp.square(_ctx_512t)) + 1e-12) * 0.953939
        ctx_512 = -1.39393e-06 + 0.999914 * (_ctx_512t + 0.3 * jax.random.normal(jax.random.fold_in(_rk, 611), (4, 77, 128), jnp.float32))
        _g = jax.random.normal(jax.random.fold_in(_rk, 9001), (2, 2), jnp.float32)
        _g = jnp.sign(_g) * jnp.maximum(jnp.abs(_g), 1.0) + (_g == 0) * 1.0
        g_xattn = _g[0]
        g_ffn = _g[1]
        return (x, ctx_512, g_xattn, g_ffn)
    x, ctx_512, g_xattn, g_ffn = _rec_inputs()

    def _L0_xattn_setup():
        import jax, jax.numpy as jnp
        import numpy as np
        HEADS = 16
        D_MODEL = 256
        IMG_MODEL = 128
        D_K = D_MODEL // HEADS
        key = jax.random.key(seed)
        ks = jax.random.split(key, 12)
        B, LQ, LKV = (8, 512, 256)
        s_dm = 1.0 / np.sqrt(D_MODEL)
        s_im = 1.0 / np.sqrt(IMG_MODEL)
        return {'q': jax.random.normal(ks[0], (B, LQ, D_MODEL), jnp.float32), 'k': jax.random.normal(ks[1], (B, LKV, IMG_MODEL), jnp.float32), 'v': jax.random.normal(ks[2], (B, LKV, IMG_MODEL), jnp.float32), 'Wq': jax.random.normal(ks[3], (D_MODEL, D_MODEL), jnp.float32) * s_dm, 'bq': jnp.zeros((D_MODEL,), jnp.float32), 'Wk': jax.random.normal(ks[4], (IMG_MODEL, D_MODEL), jnp.float32) * s_im, 'bk': jnp.zeros((D_MODEL,), jnp.float32), 'Wv': jax.random.normal(ks[5], (IMG_MODEL, D_MODEL), jnp.float32) * s_im, 'bv': jnp.zeros((D_MODEL,), jnp.float32), 'Wo': jax.random.normal(ks[6], (D_MODEL, D_MODEL), jnp.float32) * s_dm, 'bo': jnp.zeros((D_MODEL,), jnp.float32)}
    _L0_xattn_all = _L0_xattn_setup()
    _L0_xattn_in = {k: v for k, v in _L0_xattn_all.items() if k in ('Wq', 'bq', 'Wk', 'bk', 'Wv', 'bv', 'Wo', 'bo')}
    del _L0_xattn_all

    def _L0_ffn_setup():
        import jax, jax.numpy as jnp
        import numpy as np
        import math
        D_IN = 256
        FEATURES = (1024, 1024, 256)
        BATCH, SEQ = (8, 512)

        def _conn_dense(kernel_bool, x):
            w = jnp.where(kernel_bool, jnp.float32(1.0), jnp.float32(-1.0))
            return x @ w
        key = jax.random.key(seed)
        kx, kk0, kk1, kk2 = jax.random.split(key, 4)
        x = jax.random.normal(kx, (BATCH, SEQ, D_IN), dtype=jnp.float32)
        k0 = jax.random.randint(kk0, (2 * D_IN, FEATURES[0]), 0, 2).astype(jnp.bool_)
        k1 = jax.random.randint(kk1, (FEATURES[0], FEATURES[1]), 0, 2).astype(jnp.bool_)
        k2 = jax.random.randint(kk2, (FEATURES[1], FEATURES[2]), 0, 2).astype(jnp.bool_)
        s0 = jnp.asarray(1.0 / math.sqrt(2 * D_IN), dtype=jnp.float32)
        s1 = jnp.asarray(1.0 / math.sqrt(FEATURES[0]), dtype=jnp.float32)
        s2 = jnp.asarray(1.0 / math.sqrt(FEATURES[1]), dtype=jnp.float32)
        return {'x': x, 'k0': k0, 'k1': k1, 'k2': k2, 's0': s0, 's1': s1, 's2': s2}
    _L0_ffn_all = _L0_ffn_setup()
    _L0_ffn_in = {k: v for k, v in _L0_ffn_all.items() if k in ('k0', 'k1', 'k2', 's0', 's1', 's2')}
    del _L0_ffn_all

    def _L1_xattn_setup():
        import jax, jax.numpy as jnp
        import numpy as np
        DIM = 256
        LATENT_DIM = 128
        NUM_HEADS = 16
        HEAD_DIM = DIM // NUM_HEADS
        SCALE = HEAD_DIM ** (-0.5)
        key = jax.random.key(seed)
        k1, k2, k3, k4, k5 = jax.random.split(key, 5)
        B, xN, zN = (2, 512, 512)
        x = jax.random.normal(k1, (B, xN, DIM), dtype=jnp.float32)
        z = jax.random.normal(k2, (B, zN, LATENT_DIM), dtype=jnp.float32)
        Wq = jax.random.normal(k3, (DIM, DIM), dtype=jnp.float32) * DIM ** (-0.5)
        Wkv = jax.random.normal(k4, (2 * DIM, LATENT_DIM), dtype=jnp.float32) * LATENT_DIM ** (-0.5)
        Wo = jax.random.normal(k5, (DIM, DIM), dtype=jnp.float32) * DIM ** (-0.5)
        return {'x': x, 'z': z, 'Wq': Wq, 'Wkv': Wkv, 'Wo': Wo}
    _L1_xattn_all = _L1_xattn_setup()
    _L1_xattn_in = {k: v for k, v in _L1_xattn_all.items() if k in ('Wq', 'Wkv', 'Wo')}
    del _L1_xattn_all

    def _L1_ffn_setup():
        import jax, jax.numpy as jnp
        import numpy as np
        from jax import lax
        T, B, I, M, O = (64, 64, 256, 256, 256)

        def _xavier(key, shape):
            fan_out, fan_in = shape
            limit = float(np.sqrt(6.0 / (fan_in + fan_out)))
            return jax.random.uniform(key, shape, jnp.float32, -limit, limit)
        key = jax.random.key(seed)
        ks = jax.random.split(key, 9)
        x = jax.random.normal(ks[0], (T, B, I), jnp.float32)
        return {'x': x, 'wf': _xavier(ks[1], (M, I)), 'uf': _xavier(ks[2], (M, M)), 'bf': jnp.zeros((M,), jnp.float32), 'wi': _xavier(ks[3], (M, I)), 'ui': _xavier(ks[4], (M, M)), 'bi': jnp.zeros((M,), jnp.float32), 'wc': _xavier(ks[5], (M, I)), 'uc': _xavier(ks[6], (M, M)), 'bc': jnp.zeros((M,), jnp.float32), 'wo': _xavier(ks[7], (O, I)), 'uo': _xavier(ks[8], (O, M)), 'bo': jnp.zeros((O,), jnp.float32), 'in_c': jnp.zeros((M,), jnp.float32)}
    _L1_ffn_all = _L1_ffn_setup()
    _L1_ffn_in = {k: v for k, v in _L1_ffn_all.items() if k in ('wf', 'uf', 'bf', 'wi', 'ui', 'bi', 'wc', 'uc', 'bc', 'wo', 'uo', 'bo', 'in_c')}
    del _L1_ffn_all
    return {'x': x, 'ctx_512': ctx_512, 'g_xattn': g_xattn, 'g_ffn': g_ffn, 'L0_xattn_Wq': _L0_xattn_in['Wq'], 'L0_xattn_bq': _L0_xattn_in['bq'], 'L0_xattn_Wk': _L0_xattn_in['Wk'], 'L0_xattn_bk': _L0_xattn_in['bk'], 'L0_xattn_Wv': _L0_xattn_in['Wv'], 'L0_xattn_bv': _L0_xattn_in['bv'], 'L0_xattn_Wo': _L0_xattn_in['Wo'], 'L0_xattn_bo': _L0_xattn_in['bo'], 'L0_ffn_k0': _L0_ffn_in['k0'], 'L0_ffn_k1': _L0_ffn_in['k1'], 'L0_ffn_k2': _L0_ffn_in['k2'], 'L0_ffn_s0': _L0_ffn_in['s0'], 'L0_ffn_s1': _L0_ffn_in['s1'], 'L0_ffn_s2': _L0_ffn_in['s2'], 'L1_xattn_Wq': _L1_xattn_in['Wq'], 'L1_xattn_Wkv': _L1_xattn_in['Wkv'], 'L1_xattn_Wo': _L1_xattn_in['Wo'], 'L1_ffn_wf': _L1_ffn_in['wf'], 'L1_ffn_uf': _L1_ffn_in['uf'], 'L1_ffn_bf': _L1_ffn_in['bf'], 'L1_ffn_wi': _L1_ffn_in['wi'], 'L1_ffn_ui': _L1_ffn_in['ui'], 'L1_ffn_bi': _L1_ffn_in['bi'], 'L1_ffn_wc': _L1_ffn_in['wc'], 'L1_ffn_uc': _L1_ffn_in['uc'], 'L1_ffn_bc': _L1_ffn_in['bc'], 'L1_ffn_wo': _L1_ffn_in['wo'], 'L1_ffn_uo': _L1_ffn_in['uo'], 'L1_ffn_bo': _L1_ffn_in['bo'], 'L1_ffn_in_c': _L1_ffn_in['in_c']}

def reference(x, ctx_512, g_xattn, g_ffn, L0_xattn_Wq, L0_xattn_bq, L0_xattn_Wk, L0_xattn_bk, L0_xattn_Wv, L0_xattn_bv, L0_xattn_Wo, L0_xattn_bo, L0_ffn_k0, L0_ffn_k1, L0_ffn_k2, L0_ffn_s0, L0_ffn_s1, L0_ffn_s2, L1_xattn_Wq, L1_xattn_Wkv, L1_xattn_Wo, L1_ffn_wf, L1_ffn_uf, L1_ffn_bf, L1_ffn_wi, L1_ffn_ui, L1_ffn_bi, L1_ffn_wc, L1_ffn_uc, L1_ffn_bc, L1_ffn_wo, L1_ffn_uo, L1_ffn_bo, L1_ffn_in_c):
    import jax
    import jax.numpy as jnp

    def _L0_xattn_ref(q, k, v, Wq, bq, Wk, bk, Wv, bv, Wo, bo):
        import jax, jax.numpy as jnp
        import numpy as np
        HEADS = 16
        D_MODEL = 256
        IMG_MODEL = 128
        D_K = D_MODEL // HEADS
        B, LQ, _ = q.shape
        LKV = k.shape[1]
        qh = (q @ Wq + bq).reshape(B, LQ, HEADS, D_K).transpose(0, 2, 1, 3)
        kh = (k @ Wk + bk).reshape(B, LKV, HEADS, D_K).transpose(0, 2, 1, 3)
        vh = (v @ Wv + bv).reshape(B, LKV, HEADS, D_K).transpose(0, 2, 1, 3)
        scale = 1.0 / np.sqrt(D_K)
        scores = jnp.einsum('bhqd,bhkd->bhqk', qh, kh) * scale
        attn = jax.nn.softmax(scores, axis=-1)
        out = jnp.einsum('bhqk,bhkd->bhqd', attn, vh)
        concat = out.transpose(0, 2, 1, 3).reshape(B, LQ, D_MODEL)
        return concat @ Wo + bo

    def _L0_ffn_ref(x, k0, k1, k2, s0, s1, s2):
        import jax, jax.numpy as jnp
        import numpy as np
        import math
        D_IN = 256
        FEATURES = (1024, 1024, 256)
        BATCH, SEQ = (8, 512)

        def _conn_dense(kernel_bool, x):
            w = jnp.where(kernel_bool, jnp.float32(1.0), jnp.float32(-1.0))
            return x @ w
        h = jnp.concatenate([x, -x], axis=-1)
        h = s0 * _conn_dense(k0, h)
        h = jax.nn.relu(h) * 2
        h = s1 * _conn_dense(k1, h)
        h = jax.nn.relu(h) * 2
        h = s2 * _conn_dense(k2, h)
        return h

    def _L1_xattn_ref(x, z, Wq, Wkv, Wo):
        import jax, jax.numpy as jnp
        import numpy as np
        DIM = 256
        LATENT_DIM = 128
        NUM_HEADS = 16
        HEAD_DIM = DIM // NUM_HEADS
        SCALE = HEAD_DIM ** (-0.5)
        B, xN, _ = x.shape
        _, zN, _ = z.shape
        Q = (x @ Wq.T).reshape(B, xN, NUM_HEADS, HEAD_DIM)
        KV = (z @ Wkv.T).reshape(B, zN, 2, NUM_HEADS, HEAD_DIM)
        K = KV[:, :, 0]
        V = KV[:, :, 1]
        attn = jnp.einsum('bqhd,bkhd->bhqk', Q, K) * SCALE
        attn = jax.nn.softmax(attn, axis=-1)
        O = jnp.einsum('bhqk,bkhd->bqhd', attn, V).reshape(B, xN, DIM)
        return O @ Wo.T

    def _L1_ffn_ref(x, wf, uf, bf, wi, ui, bi, wc, uc, bc, wo, uo, bo, in_c):
        import jax, jax.numpy as jnp
        import numpy as np
        from jax import lax
        T, B, I, M, O = (64, 64, 256, 256, 256)

        def _xavier(key, shape):
            fan_out, fan_in = shape
            limit = float(np.sqrt(6.0 / (fan_in + fan_out)))
            return jax.random.uniform(key, shape, jnp.float32, -limit, limit)
        batch = x.shape[1]
        c0 = jnp.broadcast_to(in_c, (batch, in_c.shape[0]))

        def step(c, xt):
            ft = jax.nn.sigmoid(xt @ wf.T + c @ uf.T + bf)
            it = jax.nn.sigmoid(xt @ wi.T + c @ ui.T + bi)
            gt = jnp.tanh(xt @ wc.T + c @ uc.T + bc)
            c = ft * c + it * gt
            return (c, None)
        c_final, _ = lax.scan(step, c0, x)
        h = jnp.tanh(jnp.einsum('tbi,oi->tbo', x, wo) + c_final @ uo.T + bo)
        return h
    x = x + jnp.tanh(g_xattn[0]) * _L0_xattn_ref(_layernorm(x, axis=-1), ctx_512, ctx_512, L0_xattn_Wq, L0_xattn_bq, L0_xattn_Wk, L0_xattn_bk, L0_xattn_Wv, L0_xattn_bv, L0_xattn_Wo, L0_xattn_bo)
    x = x + jnp.tanh(g_ffn[0]) * _L0_ffn_ref(_layernorm(x, axis=-1), L0_ffn_k0, L0_ffn_k1, L0_ffn_k2, L0_ffn_s0, L0_ffn_s1, L0_ffn_s2)
    x = x + jnp.tanh(g_xattn[1]) * _L1_xattn_ref(_layernorm(x, axis=-1), ctx_512, L1_xattn_Wq, L1_xattn_Wkv, L1_xattn_Wo)
    x = x + jnp.tanh(g_ffn[1]) * _L1_ffn_ref(_layernorm(x, axis=-1), L1_ffn_wf, L1_ffn_uf, L1_ffn_bf, L1_ffn_wi, L1_ffn_ui, L1_ffn_bi, L1_ffn_wc, L1_ffn_uc, L1_ffn_bc, L1_ffn_wo, L1_ffn_uo, L1_ffn_bo, L1_ffn_in_c)
    return x

_drawn_inputs = setup_inputs


def setup_inputs(seed=0):
    import zlib

    import numpy as np

    out = dict(_drawn_inputs(seed))
    spreads = {'g_ffn': (-1.0, 0.6),
     'L0_xattn_bq': (0.0, 0.458),
     'L0_xattn_bk': (0.0, 0.8),
     'L0_xattn_bv': (0.0, 0.1),
     'L0_xattn_bo': (0.0, 0.1),
     'L1_ffn_bf': (0.0, 0.8),
     'L1_ffn_bi': (0.0, 0.8),
     'L1_ffn_bc': (0.0, 0.368),
     'L1_ffn_bo': (0.0, 0.323),
     'L1_ffn_in_c': (0.0, 0.8)}
    factors = {'L1_ffn_uf': 3.397}
    for name, (base, spread) in spreads.items():
        noise = np.random.default_rng([zlib.crc32(name.encode()), seed]).standard_normal(out[name].shape)
        drawn = base * np.exp(spread * noise) if base else spread * noise
        out[name] = jnp.asarray(drawn.astype(out[name].dtype))
    for name, factor in factors.items():
        out[name] = (out[name] * factor).astype(out[name].dtype)
    return out
```

```python
import numpy as np
import concourse.bass as bass
from concourse import mybir
from concourse.alu_op_type import AluOpType as ALU
from contextlib import ExitStack

F32 = mybir.dt.float32
F32R = mybir.dt.float32r
U8 = mybir.dt.uint8
ACT = mybir.ActivationFunctionType
AX = mybir.AxisListType

T, B, D = 4, 1024, 256
P = 128
KC = D // P
TILE = 512
SUB = TILE // P
NT = B // TILE
HEADS, DK, KEYS, IMG = 16, 16, 77, 128
HH = HEADS // 2
ROWS = HH * KEYS
RC = -(-ROWS // P)
ROW_N = [min(P, ROWS - c * P) for c in range(RC)]
KP = KEYS + 1
MXH = 4
VW = DK + 1
HID = 1024
HC = HID // P
H2RING = 2
EPS = 1e-5
KSCALE = float(DK) ** -0.5

GENERAL, OUTS, WIDE = (0, 1, 2), (3, 4), (5, 6, 7)
LAYER_NORMS = [("A", 0), ("A", 1), ("B", 0), ("B", 1), ("C", 0), ("C", 1)]


class Job:
    def __init__(self, bank, nth, base):
        self.bank, self.nth, self.base, self.per = bank, nth, base, 0

    def count(self, t):
        return t * self.per + (self.base + self.nth)


def number_jobs(order, base):
    jobs, used, turn = {}, dict.fromkeys(range(8), 0), {}
    for name, ring in order:
        at = turn.get(ring, 0)
        turn[ring] = at + 1
        bank = ring[at % len(ring)]
        used[bank] += 1
        jobs[name] = Job(bank, used[bank], base[bank])
    for job in jobs.values():
        job.per = used[job.bank]
    return jobs, used


def phase1_order():
    out = []

    def add(ring, *names):
        out.extend((n, ring) for n in names)

    def keys_values(l):
        add(GENERAL, ("k", l), *[("v", l, c) for c in range(3)])

    def two(kind, l, i):
        add(GENERAL, (kind, l, i, 0), (kind, l, i, 1))

    def maxima(l, i, a=0, b=16):
        add(WIDE, *[("mx", l, i, n) for n in range(a, b)])

    def scores(l, i, a=0, b=2 * RC):
        add(WIDE, *[("st", l, i, n) for n in range(a, b)])

    def values(l, i):
        add(GENERAL, *[("pv", l, i, s) for s in range(SUB)])

    keys_values("A")
    two("ln", "A", 0), two("q", "A", 0), maxima("A", 0)
    two("ln", "A", 1), two("q", "A", 1)
    add(GENERAL, ("mt", "A", 0))
    for n in range(2 * RC):
        scores("A", 0, n, n + 1)
        maxima("A", 1, n * 16 // 10, (n + 1) * 16 // 10)
    values("A", 0)
    add(GENERAL, ("mt", "A", 1))
    two("ot", "A", 0)
    scores("A", 1, 0, 5), two("wo", "A", 0), scores("A", 1, 5)
    values("A", 1)
    two("ln", "B", 0)
    add(WIDE, *[("h1", 0, m) for m in range(HC)])
    two("ot", "A", 1), keys_values("C"), two("wo", "A", 1)
    for m in range(HC):
        add(WIDE, ("h2", 0, m))
        if m == 1:
            add(OUTS, ("y", 0, 0), ("y", 0, 1))
        if m == 3:
            two("ln", "B", 1)
    add(WIDE, *[("h1", 1, m) for m in range(HC)])
    for m in range(HC):
        add(WIDE, ("h2", 1, m))
        if m == 1:
            add(OUTS, ("y", 1, 0), ("y", 1, 1))
        if m == 3:
            two("ln", "C", 0)
        if m == 4:
            two("q", "C", 0)
        if m == 5:
            maxima("C", 0, 0, 8)
        if m == 6:
            maxima("C", 0, 8)
    add(GENERAL, ("mt", "C", 0))
    scores("C", 0)
    two("ln", "C", 1), two("q", "C", 1), maxima("C", 1)
    values("C", 0)
    add(GENERAL, ("mt", "C", 1))
    two("ot", "C", 0)
    scores("C", 1, 0, 5), two("wo", "C", 0), scores("C", 1, 5)
    values("C", 1)
    two("ot", "C", 1), two("wo", "C", 1)
    return out


def phase2_order():
    out = []
    for i in range(NT):
        out += [(("ln", "D", i, k), GENERAL) for k in range(KC)]
    for i in range(NT):
        out += [(("xo", i, n), GENERAL) for n in range(2)]
        out += [(("gate", i, g, m), OUTS + WIDE) for m in range(KC) for g in range(3)]
    return out


def phase3_order():
    return [(("co", i, n), GENERAL) for i in range(NT) for n in range(2)]


def build(nc, a, out):
    with ExitStack() as ctx:
        def keep(name, shape, dt, scope=ctx):
            return scope.enter_context(nc.sbuf_tensor(name, shape, dt))

        def sem(name):
            return ctx.enter_context(nc.semaphore(name))

        x_sb = keep("x_sb", [P, T * NT, SUB, D], F32)
        ident = keep("ident", [P, P], F32)
        ones_row = keep("ones_row", [2, P], F32R)
        bias_rows = keep("bias_rows", [2, 3, D], F32R)
        not_first = keep("not_first", [2, 1], F32)
        one_f = keep("one_f", [2, P], F32)
        cols = keep("cols", [P, 6, KC], F32)
        bqk, col_b, c0_col = cols[:, 0:2, :], cols[:, 2:5, :], cols[:, 5, :]
        half_b = keep("half_b", [P, 2, KC], F32)
        gates_in = keep("gates_in", [P, 4], F32)
        gates = keep("gates", [P, 4], F32)
        gain_b = keep("gain_b", [P, 1], F32)
        nothing = keep("nothing", [P, 1], F32)
        eps = keep("eps", [P, SUB], F32)
        minus_half = keep("minus_half", [P, SUB], F32)
        scal = keep("scal", [P, 3], F32)
        sgn = keep("sgn", [P, 8], F32)
        token = [keep(f"token{i}", [P, SUB, D], F32) for i in range(NT)]
        act_hi = [keep(f"act_hi{i}", [P, KC, TILE], F32R) for i in range(NT)]
        act_lo = [keep(f"act_lo{i}", [P, KC, TILE], F32R) for i in range(NT)]
        stats = [keep(f"stats{i}", [P, SUB, 6], F32) for i in range(NT)]
        moments = [keep(f"moments{i}", [P, SUB, 2], F32) for i in range(NT)]
        var_eps = [keep(f"var_eps{i}", [P, SUB], F32) for i in range(NT)]
        rstd = [keep(f"rstd{i}", [P, SUB], F32) for i in range(NT)]

        p1 = ExitStack()
        w0 = keep("w0", [P, KC, HID], F32R, p1)
        w1 = keep("w1", [P, HC, HID], F32R, p1)
        w2 = keep("w2", [P, HC, D], F32R, p1)
        WQ, WO, WK, WV = 0, KC * D, 2 * KC * D, 2 * KC * D + D
        WN = WV + D
        wat_hi = [keep(f"wat_hi{l}", [P, WN], F32R, p1) for l in range(2)]
        wat_lo = [keep(f"wat_lo{l}", [P, WN], F32R, p1) for l in range(2)]
        bk4 = keep("bk4", [P, KC], F32, p1)
        head_of_feature = keep("head_of_feature", [P, HH], F32, p1)
        head_of_row = keep("head_of_row", [P, RC, HH], F32, p1)
        row_heads = keep("row_heads", [HEADS, 2, ROWS], F32R, p1)
        ctx_sb = keep("ctx_sb", [IMG, T, KEYS], F32, p1)
        at = ExitStack()
        rep_hi = keep("rep_hi", [IMG, HH, KEYS], F32R, at)
        rep_lo = keep("rep_lo", [IMG, HH, KEYS], F32R, at)
        at.close()
        q_hi = [keep("q_hi0", [P, KC, TILE], F32R, p1)]
        q_lo = [keep("q_lo0", [P, KC, TILE], F32R, p1)]
        k_f = keep("k_f", [P, KC, KEYS], F32, p1)
        k_hi = keep("k_hi", [P, KC, KEYS], F32R, p1)
        k_lo = keep("k_lo", [P, KC, KEYS], F32R, p1)
        kbd_hi = keep("kbd_hi", [P, 2, ROWS], F32R, p1)
        kbd_lo = keep("kbd_lo", [P, 2, ROWS], F32R, p1)
        vbd = keep("vbd", [P, RC, 2, HH, VW], F32, p1)
        neg_max = [keep(f"neg_max{i}", [P, SUB, HEADS], F32, p1) for i in range(NT)]
        neg_max_t = keep("neg_max_t", [HEADS, TILE], F32R, p1)
        inv_sum = keep("inv_sum", [P, SUB, HEADS], F32, p1)
        at = ExitStack()
        row_f = keep("row_f", [2, 3, D], F32, at)
        row_hi = keep("row_hi", [2, 3, D], F32R, at)
        w_raw = [keep(f"w_raw{l}", [P, WN], F32, at) for l in range(2)]
        rh_raw = keep("rh_raw", [HEADS, 2, ROWS], F32, at)
        k2_raw = keep("k2_raw", [P, HC, D], U8, at)
        at.close()
        at = ExitStack()
        probs = keep("probs", [P, 2 * RC, TILE], F32, at)
        q_hi.append(keep("q_hi1", [P, KC, TILE], F32R, at))
        q_lo.append(keep("q_lo1", [P, KC, TILE], F32R, at))
        k0_raw = keep("k0_raw", [P, 2 * KC, HID], U8, at)
        k1_raw = keep("k1_raw", [P, HC, HID], U8, at)
        at.close()
        at = ExitStack()
        h1_hi = keep("h1_hi", [P, HC, TILE], F32R, at)
        h1_lo = keep("h1_lo", [P, HC, TILE], F32R, at)
        h2_hi = keep("h2_hi", [P, H2RING, TILE], F32R, at)
        h2_lo = keep("h2_lo", [P, H2RING, TILE], F32R, at)
        at.close()
        p1.close()

        p2 = ExitStack()
        NW = 8
        wd_hi = keep("wd_hi", [P, NW, KC, D], F32R, p2)
        wd_lo = keep("wd_lo", [P, NW, KC, D], F32R, p2)
        wd_raw = keep("wd_raw", [P, NW, KC, D], F32, p2)
        xo_sb = keep("xo_sb", [P, T * NT, SUB, D], F32, p2)
        c_f = [keep(f"c_f{i}", [P, KC, TILE], F32, p2) for i in range(NT)]
        c_hi = [keep(f"c_hi{i}", [P, KC, TILE], F32R, p2) for i in range(NT)]
        c_lo = [keep(f"c_lo{i}", [P, KC, TILE], F32R, p2) for i in range(NT)]
        gate = [[keep(f"gate{g}_{i}", [P, KC, TILE], F32, p2) for g in range(3)] for i in range(NT)]
        co_sb = [keep(f"co_sb{i}", [P, SUB, D], F32, p2) for i in range(NT)]
        p2.close()

        psum = ctx.enter_context(nc.psum_tensor("psum", [P, 8, 512], F32))

        bank_filled = [sem(f"bank_filled{b}") for b in range(8)]
        bank_drained = [sem(f"bank_drained{b}") for b in range(8)]
        consts_loaded = sem("consts_loaded")
        attn_weights_loaded = sem("attn_weights_loaded")
        bits_loaded = sem("bits_loaded")
        x_loaded = [sem(f"x_loaded{i}") for i in range(NT)]
        wd_loaded = sem("wd_loaded")
        out_stored = sem("out_stored")
        setup_dve = sem("setup_dve")
        setup_act = sem("setup_act")
        setup_pool = sem("setup_pool")
        stats_ready = sem("stats_ready")
        moments_ready = sem("moments_ready")
        var_eps_ready = sem("var_eps_ready")
        rstd_ready = sem("rstd_ready")
        normed_ready = sem("normed_ready")
        rep_hi_ready = sem("rep_hi_ready")
        rep_lo_ready = sem("rep_lo_ready")
        k_parts_ready = sem("k_parts_ready")
        kbd_ready = sem("kbd_ready")
        hi_ready = sem("hi_ready")
        neg_max_ready = sem("neg_max_ready")
        inv_sum_ready = sem("inv_sum_ready")
        heads_ready = sem("heads_ready")
        wd_hi_ready = sem("wd_hi_ready")
        wd_lo_ready = sem("wd_lo_ready")
        fc_ready = sem("fc_ready")
        ig_ready = sem("ig_ready")
        c2_ready = sem("c2_ready")
        c_f_ready = sem("c_f_ready")
        c_hi_ready = sem("c_hi_ready")
        c_lo_ready = sem("c_lo_ready")
        pre_ready = sem("pre_ready")
        h_ready = sem("h_ready")
        out_ready = sem("out_ready")

        zero = dict.fromkeys(range(8), 0)
        jobs, per1 = number_jobs(phase1_order(), zero)
        base2 = {b: T * per1[b] for b in range(8)}
        jobs2, per2 = number_jobs(phase2_order(), base2)
        base3 = {b: base2[b] + T * per2[b] for b in range(8)}
        jobs3, _ = number_jobs(phase3_order(), base3)
        jobs = {**jobs, **jobs2, **jobs3}

        def wait_filled(eng, name, t):
            eng.wait_ge(bank_filled[jobs[name].bank], jobs[name].count(t))

        def wait_drained(eng, name, t):
            eng.wait_ge(bank_drained[jobs[name].bank], jobs[name].count(t) + 1)

        def wait_free(eng, name, t):
            eng.wait_ge(bank_drained[jobs[name].bank], jobs[name].count(t))

        def bank(name):
            return psum[:, jobs[name].bank, :]

        LN1, LN2 = len(LAYER_NORMS), NT

        def ln_count(l, i, t):
            if l == "D":
                return t * LN2 + (T * LN1 + i + 1)
            return t * LN1 + (LAYER_NORMS.index((l, i)) + 1)

        hi1 = []
        for kind, l, i in [("ln", "A", 0), ("q", "A", 0), ("ln", "A", 1), ("q", "A", 1), ("ot", "A", 0),
                           ("ln", "B", 0), ("h1", 0, 0), ("ot", "A", 1)]:
            hi1 += [("h1", 0, m) for m in range(HC)] if kind == "h1" else [(kind, l, i, 0), (kind, l, i, 1)]
        for m in range(HC):
            hi1.append(("h2", 0, m))
            if m == 3:
                hi1 += [("ln", "B", 1, 0), ("ln", "B", 1, 1)]
        hi1 += [("h1", 1, m) for m in range(HC)]
        for m in range(HC):
            hi1.append(("h2", 1, m))
            if m == 3:
                hi1 += [("ln", "C", 0, 0), ("ln", "C", 0, 1)]
            if m == 4:
                hi1 += [("q", "C", 0, 0), ("q", "C", 0, 1)]
        for kind, i in [("ln", 1), ("q", 1), ("ot", 0), ("ot", 1)]:
            hi1 += [(kind, "C", i, 0), (kind, "C", i, 1)]
        HI1 = len(hi1)
        hi2 = [("ln", "D", i, k) for i in range(NT) for k in range(KC)]
        HI2 = len(hi2)

        def hi_count(name, t):
            if name[1] == "D":
                return t * HI2 + (T * HI1 + hi2.index(name) + 1)
            return t * HI1 + (hi1.index(name) + 1)

        ATTN = [("A", 0), ("A", 1), ("C", 0), ("C", 1)]

        def attn_count(l, i, t, each):
            return t * (each * len(ATTN)) + each * (ATTN.index((l, i)) + 1)

        LAYER = {"A": 0, "C": 1}

        def c_count(i, t):
            return t * NT + (2 * NT + i + 1)

        block = ctx.enter_context(nc.Block())

        @block.sync
        def _(sp):
            def weights(l, name, dst, n):
                sp.dma_start(w_raw[l][:, dst:dst + n * D].rearrange("p (c m) -> p c m", c=n),
                             a[name].rearrange("(c p) m -> p c m", p=P)).then_inc(attn_weights_loaded, 16)

            def x_tile(t, i):
                sp.dma_start(x_sb[:, t * NT + i, :, :],
                             a["x"][t * NT + i, :, :, :]).then_inc(x_loaded[i], 16)

            x_tile(0, 0)
            sp.dma_start(ctx_sb[:, :, :], a["ctx_t"].rearrange("b d k -> d b k")).then_inc(consts_loaded, 16)
            sp.dma_start(ident[:, :], a["ident"]).then_inc(consts_loaded, 16)
            for l in range(2):
                weights(l, f"wk{l}", WK, 1)
                weights(l, f"wv{l}", WV, 1)
                weights(l, f"wq{l}", WQ, KC)
                weights(l, f"wo{l}", WO, KC)
                if l == 0:
                    x_tile(0, 1)
            sp.dma_start(k0_raw[:, :, :], a["k0"].rearrange("(c p) m -> p c m", p=P)).then_inc(bits_loaded, 16)
            sp.dma_start(k1_raw[:, :, :], a["k1"].rearrange("(c p) m -> p c m", p=P)).then_inc(bits_loaded, 16)
            sp.dma_start(k2_raw[:, :, :], a["k2"].rearrange("(c p) m -> p c m", p=P)).then_inc(bits_loaded, 16)
            with sp.Fori(1, T) as t:
                for i in range(NT):
                    sp.wait_ge(x_loaded[i], t * 16)
                    x_tile(t, i)
            wait_filled(sp, ("y", 1, 0), T - 1)
            wait_filled(sp, ("y", 1, 1), T - 1)
            for n, name in enumerate(["wf", "wi", "wc", "uf", "ui", "uc", "wo_d", "uo_d"]):
                sp.dma_start(wd_raw[:, n, :, :], a[name].rearrange("(c p) m -> p c m", p=P)).then_inc(wd_loaded, 16)
            with sp.Fori(0, T) as t:
                for i in range(NT):
                    sp.wait_ge(out_ready, t * NT + (i + 1))
                    sp.dma_start(out[t * NT + i, :, :, :], x_sb[:, t * NT + i, :, :]).then_inc(out_stored, 16)
            sp.wait_ge(out_stored, T * NT * 16)

        @block.gpsimd
        def _(pool):
            for first in bank_drained + [k_parts_ready, kbd_ready, c_f_ready]:
                pool.sem_inc(first, 1)
            pool.memset(minus_half[:, :], -0.5).then_inc(setup_pool, 1)
            pool.memset(one_f[:, :], 1.0).then_inc(setup_pool, 1)
            pool.memset(eps[:, :], EPS).then_inc(setup_pool, 1)

            def rstd_of(l, i, t):
                pool.wait_ge(moments_ready, ln_count(l, i, t))
                pool.tensor_tensor(var_eps[i][:, :], moments[i][:, :, 1], eps[:, :], ALU.add).then_inc(var_eps_ready, 1)
                pool.wait_ge(var_eps_ready, ln_count(l, i, t))
                pool.tensor_tensor(rstd[i][:, :], var_eps[i][:, :], minus_half[:, :], ALU.pow).then_inc(rstd_ready, 1)

            def kbd_lo_of(l, t):
                pool.wait_ge(k_parts_ready, t * 4 + (1 + 2 * LAYER[l] + 2))
                for m in range(KC):
                    ins = pool.tensor_tensor(kbd_lo[:, m, :].rearrange("p (h k) -> p h k", h=HH),
                                             k_lo[:, m, :].bitcast(F32).unsqueeze(1).to_broadcast([P, HH, KEYS]),
                                             head_of_feature[:, :].unsqueeze(2).to_broadcast([P, HH, KEYS]), ALU.mult)
                ins.then_inc(kbd_ready, 1)

            pool.wait_ge(setup_pool, 3)
            with pool.Fori(0, T) as t:
                rstd_of("A", 0, t)
                rstd_of("A", 1, t)
                kbd_lo_of("A", t)
                rstd_of("B", 0, t)
                kbd_lo_of("C", t)
                rstd_of("B", 1, t)
                rstd_of("C", 0, t)
                rstd_of("C", 1, t)
            with pool.Fori(0, T) as t:
                rstd_of("D", 0, t)
                rstd_of("D", 1, t)
            with pool.Fori(0, T) as t:
                for i in range(NT):
                    for n in range(2):
                        wait_drained(pool, ("co", i, n), 0)
                    tile = xo_sb[:, t * NT + i, :, :]
                    pool.tensor_tensor(tile, tile, co_sb[i][:, :, :], ALU.add).then_inc(pre_ready, 1)

        @block.scalar
        def _(act):
            for dst, name in [(gates_in[:, :], "g"), (scal[:, :], "s")]:
                act.dma_start(dst, a[name].partition_broadcast(P)).then_inc(consts_loaded, 16)
            act.dma_start(cols[:, :, :], a["cols"]).then_inc(consts_loaded, 16)
            act.dma_start(row_f[:, :, :], a["rows"].partition_broadcast(2)).then_inc(consts_loaded, 16)
            act.dma_start(not_first[:, :], a["not_first"]).then_inc(consts_loaded, 16)
            act.dma_start(head_of_feature[:, :], a["head_of_feature"]).then_inc(consts_loaded, 16)
            act.dma_start(head_of_row[:, :, :], a["head_of_row"]).then_inc(consts_loaded, 16)
            act.dma_start(rh_raw[:, :, :], a["row_heads"]).then_inc(consts_loaded, 16)
            act.wait_ge(consts_loaded, 10 * 16)
            act.activation(gates[:, :], gates_in[:, :], ACT.Tanh).then_inc(setup_act, 1)
            act.activation(row_heads[:, :, :], rh_raw[:, :, :], ACT.Copy).then_inc(setup_act, 1)
            act.wait_ge(attn_weights_loaded, 8 * 16)
            for l in range(2):
                act.activation(wat_hi[l][:, :], w_raw[l][:, :], ACT.Copy).then_inc(setup_act, 1)
            act.wait_ge(bits_loaded, 3 * 16)
            act.wait_ge(setup_dve, 3)
            for h in range(2):
                act.activation(w1[:, h * 4:h * 4 + 4, :], k1_raw[:, h * 4:h * 4 + 4, :], ACT.Identity,
                               scale=sgn[:, 4:5], bias=sgn[:, 5:6]).then_inc(setup_act, 1)

            def hi_of(dst, name, t, func=ACT.Copy, bias=None):
                wait_filled(act, name, t)
                more = {} if bias is None else {"bias": bias}
                act.activation(dst, bank(name), func, **more).then_inc(hi_ready, 1)

            def act_hi_of(kind, l, i, t):
                for k in range(KC):
                    hi_of(act_hi[i][:, k, :], (kind, l, i, k), t)

            def q_hi_of(l, i, t):
                for m in range(KC):
                    if l == "A":
                        hi_of(q_hi[i][:, m, :], ("q", l, i, m), t, ACT.Identity, bqk[:, 0, m:m + 1])
                    else:
                        hi_of(q_hi[i][:, m, :], ("q", l, i, m), t)

            def rep_hi_of(l, t):
                act.activation(rep_hi[:, :, :], ctx_sb[:, t, :].unsqueeze(1).to_broadcast([IMG, HH, KEYS]),
                               ACT.Copy).then_inc(rep_hi_ready, 1)


            def k_of(l, t):
                act.wait_ge(k_parts_ready, t * 4 + (1 + 2 * LAYER[l]))
                wait_filled(act, ("k", l), t)
                pk = bank(("k", l))[:, 0:KC * KP].rearrange("p (c k) -> p c k", c=KC)[:, :, 0:KEYS]
                if l == "A":
                    for m in range(KC):
                        ins = act.activation(k_f[:, m, :], pk[:, m, :], ACT.Identity, scale=KSCALE, bias=bk4[:, m:m + 1])
                else:
                    ins = act.activation(k_f[:, :, :], pk, ACT.Copy, scale=KSCALE)
                ins.then_inc(bank_drained[jobs["k", l].bank], 1)

            def neg_max_of(l, i, t):
                wait_filled(act, ("mt", l, i), t)
                act.activation(neg_max_t[:, :], bank(("mt", l, i))[0:HEADS, :], ACT.Copy)\
                    .then_inc(bank_drained[jobs["mt", l, i].bank], 1)

            def exps(l, i, t, n0, n1, before):
                if before is not None:
                    wait_filled(act, ("pv", *before[0], SUB - 1), before[1])
                for n in range(n0, n1):
                    name, rows = ("st", l, i, n), ROW_N[n % RC]
                    wait_filled(act, name, t)
                    act.activation(probs[0:rows, n, :], bank(name)[0:rows, :], ACT.Exp)\
                        .then_inc(bank_drained[jobs[name].bank], 1)

            def hidden(kind, i, t, ms):
                for m in ms:
                    name = (kind, i, m)
                    if kind == "h2":
                        hi_of(h2_hi[:, m % H2RING, :], name, t, ACT.Relu)
                    else:
                        hi_of(h1_hi[:, m, :], name, t, ACT.Relu)

            with act.Fori(0, T) as t:
                rep_hi_of("A", t)
                k_of("A", t)
                act_hi_of("ln", "A", 0, t)
                q_hi_of("A", 0, t)
                act_hi_of("ln", "A", 1, t)
                q_hi_of("A", 1, t)
                neg_max_of("A", 0, t)
                exps("A", 0, t, 0, 2 * RC, None)
                neg_max_of("A", 1, t)
                act_hi_of("ot", "A", 0, t)
                exps("A", 1, t, 0, 2 * RC, (("A", 0), t))
                act_hi_of("ln", "B", 0, t)
                hidden("h1", 0, t, range(HC))
                rep_hi_of("C", t)
                act_hi_of("ot", "A", 1, t)
                k_of("C", t)
                hidden("h2", 0, t, range(4))
                act_hi_of("ln", "B", 1, t)
                hidden("h2", 0, t, range(4, HC))
                hidden("h1", 1, t, range(HC))
                hidden("h2", 1, t, range(4))
                act_hi_of("ln", "C", 0, t)
                hidden("h2", 1, t, range(4, 5))
                q_hi_of("C", 0, t)
                hidden("h2", 1, t, range(5, HC))
                neg_max_of("C", 0, t)
                exps("C", 0, t, 0, 2 * RC, None)
                act_hi_of("ln", "C", 1, t)
                q_hi_of("C", 1, t)
                neg_max_of("C", 1, t)
                act_hi_of("ot", "C", 0, t)
                exps("C", 1, t, 0, 2 * RC, (("C", 0), t))
                act_hi_of("ot", "C", 1, t)

            act.wait_ge(wd_loaded, NW * 16)
            act.activation(wd_hi[:, :, :, :], wd_raw[:, :, :, :], ACT.Copy).then_inc(wd_hi_ready, 1)

            with act.Fori(0, T) as t:
                for i in range(NT):
                    act_hi_of("ln", "D", i, t)
                for i in range(NT):
                    for n in range(2):
                        wait_filled(act, ("xo", i, n), t)
                        act.activation(xo_sb[:, t * NT + i, 2 * n:2 * n + 2, :],
                                       bank(("xo", i, n)).rearrange("p (s d) -> p s d", s=2), ACT.Copy)\
                            .then_inc(bank_drained[jobs["xo", i, n].bank], 1)
                    act.wait_ge(c_lo_ready, c_count(i, t))
                    for m in range(KC):
                        for g in range(3):
                            name = ("gate", i, g, m)
                            wait_filled(act, name, t)
                            half = 0.5 if g < 2 else 1.0
                            bias = half_b[:, g, m:m + 1] if g < 2 else col_b[:, 2, m:m + 1]
                            act.activation(gate[i][g][:, m, :], bank(name), ACT.Tanh, scale=half, bias=bias)\
                                .then_inc(bank_drained[jobs[name].bank], 1)
                    act.wait_ge(c2_ready, t * NT + (i + 1))
                    act.activation(c_hi[i][:, :, :], gate[i][0][:, :, :], ACT.Copy, scale=0.5).then_inc(c_hi_ready, 1)
                    act.activation(c_f[i][:, :, :], gate[i][0][:, :, :], ACT.Copy, scale=0.5).then_inc(c_f_ready, 1)
            for i in range(NT):
                for n in range(2):
                    name = ("co", i, n)
                    wait_filled(act, name, 0)
                    act.activation(co_sb[i][:, 2 * n:2 * n + 2, :], bank(name).rearrange("p (s d) -> p s d", s=2),
                                   ACT.Copy).then_inc(bank_drained[jobs[name].bank], 1)
            with act.Fori(0, T) as t:
                for i in range(NT):
                    act.wait_ge(pre_ready, t * NT + (i + 1))
                    tile = xo_sb[:, t * NT + i, :, :]
                    act.activation(tile, tile, ACT.Tanh).then_inc(h_ready, 1)

        @block.vector
        def _(dve):
            dve.wait_ge(consts_loaded, 10 * 16)
            dve.wait_ge(setup_pool, 3)
            dve.tensor_scalar(sgn[:, 0:2], scal[:, 0:2], 0.0, None, ALU.is_gt).then_inc(setup_dve, 1)
            dve.tensor_scalar(sgn[:, 2:4], scal[:, 0:2], 0.0, None, ALU.is_lt).then_inc(setup_dve, 1)
            dve.wait_ge(setup_dve, 2)
            dve.tensor_tensor(sgn[:, 6:8], sgn[:, 0:2], sgn[:, 2:4], ALU.subtract)
            dve.tensor_tensor(sgn[:, 5:6], sgn[:, 3:4], sgn[:, 1:2], ALU.subtract)
            dve.tensor_scalar(sgn[:, 4:5], sgn[:, 1:2], sgn[:, 3:4], 2.0, ALU.subtract, ALU.mult).then_inc(setup_dve, 1)
            dve.wait_ge(setup_dve, 3)
            dve.wait_ge(setup_act, 1)
            dve.tensor_tensor(gain_b[:, :], scal[:, 0:1], scal[:, 1:2], ALU.mult).then_inc(setup_dve, 1)
            dve.wait_ge(setup_dve, 4)
            dve.tensor_scalar(gain_b[:, :], gain_b[:, :], scal[:, 2:3], 8.0, ALU.mult, ALU.mult).then_inc(setup_dve, 1)
            dve.wait_ge(setup_dve, 5)
            dve.tensor_scalar(gain_b[:, :], gain_b[:, :], gates[:, 2:3], sgn[:, 6:7], ALU.mult, ALU.mult)\
                .then_inc(setup_dve, 1)
            dve.wait_ge(setup_dve, 6)
            dve.tensor_scalar(gain_b[:, :], gain_b[:, :], sgn[:, 7:8], None, ALU.mult)
            dve.tensor_copy(ones_row[:, :], one_f[:, :])
            dve.tensor_copy(row_hi[:, :, :], row_f[:, :, :]).then_inc(setup_dve, 1)
            dve.tensor_scalar(bk4[:, :], bqk[:, 1, :], KSCALE, None, ALU.mult)
            dve.tensor_scalar(half_b[:, :, :], col_b[:, 0:2, :], 0.5, None, ALU.mult)
            dve.tensor_copy(vbd[:, :, 0, :, DK], head_of_row[:, :, :])
            dve.tensor_copy(vbd[:, :, 1, :, DK], head_of_row[:, :, :])
            dve.wait_ge(setup_dve, 7)
            dve.scalar_tensor_tensor(bias_rows[:, :, :], row_hi[:, :, :].bitcast(F32), not_first[:, 0:1],
                                     row_f[:, :, :], ALU.mult, ALU.add).then_inc(setup_dve, 1)
            for l in range(2):
                dve.wait_ge(setup_act, 3 + l)
                dve.tensor_tensor(wat_lo[l][:, :], w_raw[l][:, :], wat_hi[l][:, :].bitcast(F32), ALU.subtract)\
                    .then_inc(setup_dve, 1)
            dve.wait_ge(bits_loaded, 3 * 16)
            dve.tensor_tensor(w0[:, :, :], k0_raw[:, 0:KC, :], k0_raw[:, KC:2 * KC, :], ALU.subtract).then_inc(setup_dve, 1)
            dve.tensor_scalar(w2[:, :, :], k2_raw[:, :, :], 2.0, -1.0, ALU.mult, ALU.add).then_inc(setup_dve, 1)
            dve.wait_ge(setup_dve, 11)
            dve.tensor_scalar(w0[:, :, :], w0[:, :, :].bitcast(F32), sgn[:, 6:7], None, ALU.mult).then_inc(setup_dve, 1)

            def layer_norm(l, i, t):
                tile = t * NT + i
                if l == "A":
                    dve.wait_ge(x_loaded[i], t * 16 + 16)
                elif l in "BC":
                    for n in range(2):
                        wait_drained(dve, ("wo", "A", i, n) if l == "B" else ("y", i, n), t)
                dve.memset(nothing[:, :], 0.0)
                for s in range(SUB):
                    ins = dve.bn_stats(stats[i][:, s, :], x_sb[:, tile, s, :])
                ins.then_inc(stats_ready, 1)
                dve.wait_ge(stats_ready, ln_count(l, i, t))
                dve.memset(nothing[:, :], 0.0)
                for s in range(SUB):
                    ins = dve.bn_aggr(moments[i][:, s, :], stats[i][:, s, :])
                ins.then_inc(moments_ready, 1)
                dve.wait_ge(moments_ready, ln_count(l, i, t))
                dve.wait_ge(rstd_ready, ln_count(l, i, t))
                for s in range(SUB):
                    ins = dve.tensor_scalar(token[i][:, s, :], x_sb[:, tile, s, :], moments[i][:, s, 0:1],
                                            rstd[i][:, s:s + 1], ALU.subtract, ALU.mult)
                ins.then_inc(normed_ready, 1)

            def act_lo_of(kind, l, i, t):
                for k in range(KC):
                    name = (kind, l, i, k)
                    dve.wait_ge(hi_ready, hi_count(name, t))
                    dve.tensor_tensor(act_lo[i][:, k, :], bank(name), act_hi[i][:, k, :].bitcast(F32), ALU.subtract)\
                        .then_inc(bank_drained[jobs[name].bank], 1)

            def q_lo_of(l, i, t):
                for m in range(KC):
                    name = ("q", l, i, m)
                    dve.wait_ge(hi_ready, hi_count(name, t))
                    if l == "A":
                        ins = dve.scalar_tensor_tensor(q_lo[i][:, m, :], bank(name), bqk[:, 0, m:m + 1],
                                                       q_hi[i][:, m, :].bitcast(F32), ALU.add, ALU.subtract)
                    else:
                        ins = dve.tensor_tensor(q_lo[i][:, m, :], bank(name), q_hi[i][:, m, :].bitcast(F32), ALU.subtract)
                    ins.then_inc(bank_drained[jobs[name].bank], 1)

            def rep_lo_of(l, t):
                dve.wait_ge(rep_hi_ready, t * 2 + (LAYER[l] + 1))
                dve.tensor_tensor(rep_lo[:, :, :], ctx_sb[:, t, :].unsqueeze(1).to_broadcast([IMG, HH, KEYS]),
                                  rep_hi[:, :, :].bitcast(F32), ALU.subtract).then_inc(rep_lo_ready, 1)

            def keys_values(l, t):
                n = 2 * LAYER[l]
                wait_drained(dve, ("k", l), t)
                dve.wait_ge(kbd_ready, t * 4 + (1 + n))
                dve.tensor_copy(k_hi[:, :, :], k_f[:, :, :]).then_inc(k_parts_ready, 1)
                dve.wait_ge(k_parts_ready, t * 4 + (1 + n + 1))
                dve.tensor_tensor(k_lo[:, :, :], k_f[:, :, :], k_hi[:, :, :].bitcast(F32), ALU.subtract)\
                    .then_inc(k_parts_ready, 1)
                for m in range(KC):
                    ins = dve.tensor_tensor(kbd_hi[:, m, :].rearrange("p (h k) -> p h k", h=HH),
                                            k_hi[:, m, :].bitcast(F32).unsqueeze(1).to_broadcast([P, HH, KEYS]),
                                            head_of_feature[:, :].unsqueeze(2).to_broadcast([P, HH, KEYS]), ALU.mult)
                ins.then_inc(kbd_ready, 1)
                for j in range(3):
                    name = ("v", l, j)
                    wait_filled(dve, name, t)
                    for c in range(2 * j, min(2 * j + 2, RC)):
                        rows, o = ROW_N[c], (c % 2) * D
                        ins = dve.tensor_tensor(
                            vbd[0:rows, c, :, :, 0:DK],
                            bank(name)[0:rows, o:o + D].rearrange("p (g h d) -> p g h d", g=2, h=HH),
                            head_of_row[0:rows, c, :].unsqueeze(1).unsqueeze(3).to_broadcast([rows, 2, HH, DK]),
                            ALU.mult)
                    ins.then_inc(bank_drained[jobs[name].bank], 1)

            def maxima(l, i, t, n0=0, n1=16):
                for n in range(n0, n1):
                    s, q = n // 4, n % 4
                    name = ("mx", l, i, n)
                    wait_filled(dve, name, t)
                    ins = dve.tensor_reduce(neg_max[i][:, s, MXH * q:MXH * q + MXH],
                                            bank(name)[:, 0:MXH * KEYS].rearrange("p (h k) -> p h k", h=MXH),
                                            AX.X, ALU.max, negate=True)
                    ins.then_inc(bank_drained[jobs[name].bank], 1)

            def heads(l, i, t):
                for s in range(SUB):
                    name = ("pv", l, i, s)
                    wait_filled(dve, name, t)
                    pv = bank(name)[:, 0:HEADS * VW].rearrange("p (h d) -> p h d", h=HEADS)
                    dve.reciprocal(inv_sum[:, s, :], pv[:, :, DK]).then_inc(inv_sum_ready, 1)
                    dve.wait_ge(inv_sum_ready, attn_count(l, i, t, SUB) - (SUB - 1 - s))
                    ins = dve.tensor_tensor(token[i][:, s, :].rearrange("p (h d) -> p h d", h=HEADS), pv[:, :, 0:DK],
                                            inv_sum[:, s, :].unsqueeze(2).to_broadcast([P, HEADS, DK]), ALU.mult)
                    ins.then_inc(bank_drained[jobs[name].bank], 1)

            def residual(l, i, t):
                gain = {"A": gates[:, 0:1], "B": gain_b[:, 0:1], "C": gates[:, 1:2]}[l]
                for n in range(2):
                    name = ("y", i, n) if l == "B" else ("wo", l, i, n)
                    wait_filled(dve, name, t)
                    part = x_sb[:, t * NT + i, 2 * n:2 * n + 2, :].rearrange("p s d -> p (s d)")
                    dve.scalar_tensor_tensor(part, bank(name), gain, part, ALU.mult, ALU.add)\
                        .then_inc(bank_drained[jobs[name].bank], 1)

            def hidden(kind, i, t, ms):
                for m in ms:
                    name = (kind, i, m)
                    hi, lo = (h1_hi, h1_lo) if kind == "h1" else (h2_hi, h2_lo)
                    at = m if kind == "h1" else m % H2RING
                    dve.wait_ge(hi_ready, hi_count(name, t))
                    dve.scalar_tensor_tensor(lo[:, at, :], bank(name), 0.0, hi[:, at, :].bitcast(F32),
                                             ALU.max, ALU.subtract).then_inc(bank_drained[jobs[name].bank], 1)

            with dve.Fori(0, T) as t:
                rep_lo_of("A", t)
                layer_norm("A", 0, t)
                layer_norm("A", 1, t)
                keys_values("A", t)
                act_lo_of("ln", "A", 0, t)
                q_lo_of("A", 0, t)
                maxima("A", 0, t)
                act_lo_of("ln", "A", 1, t)
                q_lo_of("A", 1, t)
                maxima("A", 1, t)
                heads("A", 0, t)
                act_lo_of("ot", "A", 0, t)
                residual("A", 0, t)
                layer_norm("B", 0, t)
                heads("A", 1, t)
                act_lo_of("ln", "B", 0, t)
                hidden("h1", 0, t, range(HC))
                rep_lo_of("C", t)
                act_lo_of("ot", "A", 1, t)
                keys_values("C", t)
                residual("A", 1, t)
                layer_norm("B", 1, t)
                hidden("h2", 0, t, range(4))
                act_lo_of("ln", "B", 1, t)
                hidden("h2", 0, t, range(4, HC))
                hidden("h1", 1, t, range(1))
                residual("B", 0, t)
                hidden("h1", 1, t, range(1, HC))
                layer_norm("C", 0, t)
                hidden("h2", 1, t, range(4))
                act_lo_of("ln", "C", 0, t)
                hidden("h2", 1, t, range(4, 5))
                q_lo_of("C", 0, t)
                hidden("h2", 1, t, range(5, 6))
                maxima("C", 0, t, 0, 8)
                hidden("h2", 1, t, range(6, 7))
                maxima("C", 0, t, 8, 16)
                hidden("h2", 1, t, range(7, 8))
                residual("B", 1, t)
                layer_norm("C", 1, t)
                act_lo_of("ln", "C", 1, t)
                q_lo_of("C", 1, t)
                maxima("C", 1, t)
                heads("C", 0, t)
                act_lo_of("ot", "C", 0, t)
                residual("C", 0, t)
                heads("C", 1, t)
                act_lo_of("ot", "C", 1, t)
                residual("C", 1, t)

            dve.wait_ge(wd_hi_ready, 1)
            for n in range(2):
                wait_drained(dve, ("wo", "C", 1, n), T - 1)
            dve.tensor_tensor(wd_lo[:, :, :, :], wd_raw[:, :, :, :], wd_hi[:, :, :, :].bitcast(F32), ALU.subtract)\
                .then_inc(wd_lo_ready, 1)
            for i in range(NT):
                dve.tensor_copy(c_f[i][:, :, :], c0_col[:, :].unsqueeze(2).to_broadcast([P, KC, TILE])).then_inc(c_lo_ready, 1)
                dve.tensor_copy(c_hi[i][:, :, :], c0_col[:, :].unsqueeze(2).to_broadcast([P, KC, TILE])).then_inc(c_lo_ready, 1)
                dve.wait_ge(c_lo_ready, 3 * i + 2)
                dve.tensor_tensor(c_lo[i][:, :, :], c_f[i][:, :, :], c_hi[i][:, :, :].bitcast(F32), ALU.subtract)\
                    .then_inc(c_lo_ready, 1)
            with dve.Fori(0, T) as t:
                for i in range(NT):
                    layer_norm("D", i, t)
                for i in range(NT):
                    act_lo_of("ln", "D", i, t)
                for i in range(NT):
                    for m in range(KC):
                        for g in range(3):
                            wait_drained(dve, ("gate", i, g, m), t)
                    dve.wait_ge(c_f_ready, t * NT + 1)
                    dve.scalar_tensor_tensor(gate[i][0][:, :, :], gate[i][0][:, :, :], 1.0, c_f[i][:, :, :],
                                             ALU.add, ALU.mult).then_inc(fc_ready, 1)
                    dve.scalar_tensor_tensor(gate[i][1][:, :, :], gate[i][1][:, :, :], 1.0, gate[i][2][:, :, :],
                                             ALU.add, ALU.mult).then_inc(ig_ready, 1)
                    dve.wait_ge(fc_ready, t * NT + (i + 1))
                    dve.wait_ge(ig_ready, t * NT + (i + 1))
                    dve.tensor_tensor(gate[i][0][:, :, :], gate[i][0][:, :, :], gate[i][1][:, :, :], ALU.add)\
                        .then_inc(c2_ready, 1)
                    dve.wait_ge(c2_ready, t * NT + (i + 1))
                    dve.wait_ge(c_hi_ready, t * NT + (i + 1))
                    dve.scalar_tensor_tensor(c_lo[i][:, :, :], gate[i][0][:, :, :], 0.5, c_hi[i][:, :, :].bitcast(F32),
                                             ALU.mult, ALU.subtract).then_inc(c_lo_ready, 1)
            with dve.Fori(0, T) as t:
                for i in range(NT):
                    dve.wait_ge(h_ready, t * NT + (i + 1))
                    tile = x_sb[:, t * NT + i, :, :].rearrange("p s d -> p (s d)")
                    dve.scalar_tensor_tensor(tile, xo_sb[:, t * NT + i, :, :].rearrange("p s d -> p (s d)"),
                                             gates[:, 3:4], tile, ALU.mult, ALU.add).then_inc(out_ready, 1)

        @block.tensor
        def _(pe):
            def begin(name, t):
                wait_free(pe, name, t)

            def done(ins, name):
                ins.then_inc(bank_filled[jobs[name].bank], 1)

            def terms(dst, lefts, rights, start=True, stop=True):
                n = len(lefts)
                for k, ((lh, ll), (rh, rl)) in enumerate(zip(lefts, rights)):
                    pe.matmul(dst, lh, rh, start=start and k == 0, stop=False, skip_group_check=True)
                    pe.matmul(dst, lh, rl, start=False, stop=False, skip_group_check=True)
                    ins = pe.matmul(dst, ll, rh, start=False, stop=stop and k == n - 1, skip_group_check=True)
                return ins

            def wat(l, at, n, m0=0, m=D):
                j = LAYER[l]
                return [(wat_hi[j][:, at + k * D + m0:at + k * D + m0 + m],
                         wat_lo[j][:, at + k * D + m0:at + k * D + m0 + m]) for k in range(n)]

            def rep(c0, n):
                hi = rep_hi[:, :, :].rearrange("p h k -> p (h k)")
                lo = rep_lo[:, :, :].rearrange("p h k -> p (h k)")
                return hi[:, c0:c0 + n], lo[:, c0:c0 + n]

            def keys_values(l, t):
                pe.wait_ge(rep_lo_ready, t * 2 + (LAYER[l] + 1))
                begin(("k", l), t)
                pk = bank(("k", l))
                for m in range(KC):
                    ins = terms(pk[:, m * KP:m * KP + KP], wat(l, WK, 1, m * P, P), [rep(0, KP)], start=m == 0)
                done(ins, ("k", l))
                for j in range(3):
                    name = ("v", l, j)
                    begin(name, t)
                    for c in range(2 * j, min(2 * j + 2, RC)):
                        rows = ROW_N[c]
                        dst = bank(name)[0:rows, (c % 2) * D:(c % 2) * D + D]
                        first = c % 2 == 0
                        ins = terms(dst, [rep(c * P, rows)], wat(l, WV, 1), start=first, stop=l == "C")
                        if l == "A":
                            ins = pe.matmul(dst, ones_row[0:2, 0:rows], bias_rows[0:2, 0, :], start=False, stop=True,
                                            skip_group_check=True)
                    done(ins, name)

            def transposes(kind, l, i, t):
                if kind == "ln":
                    pe.wait_ge(normed_ready, ln_count(l, i, t))
                else:
                    for s in range(SUB):
                        wait_drained(pe, ("pv", l, i, s), t)
                for k in range(KC):
                    name = (kind, l, i, k)
                    begin(name, t)
                    for s in range(SUB):
                        ins = pe.transpose(bank(name)[:, s * P:s * P + P], token[i][:, s, k * P:k * P + P], ident[:, :])
                    done(ins, name)

            def wait_act(kind, l, i, t):
                for k in range(KC):
                    wait_drained(pe, (kind, l, i, k), t)

            def query(l, i, t):
                wait_act("ln", l, i, t)
                for m in range(KC):
                    name = ("q", l, i, m)
                    begin(name, t)
                    done(terms(bank(name), wat(l, WQ, KC, m * P, P),
                               [(act_hi[i][:, k, :], act_lo[i][:, k, :]) for k in range(KC)]), name)

            def maxima(l, i, t, n0=0, n1=16):
                if n0 == 0:
                    for m in range(KC):
                        wait_drained(pe, ("q", l, i, m), t)
                    pe.wait_ge(kbd_ready, t * 4 + (1 + 2 * LAYER[l] + 2))
                for n in range(n0, n1):
                    s, q = n // 4, n % 4
                    name = ("mx", l, i, n)
                    begin(name, t)
                    at = (q % 2) * MXH * KEYS
                    done(pe.matmul(bank(name)[:, 0:MXH * KEYS], q_hi[i][:, q // 2, s * P:s * P + P],
                                   kbd_hi[:, q // 2, at:at + MXH * KEYS], start=True, stop=True), name)

            def neg_max_rows(l, i, t):
                for n in range(16 - len(WIDE), 16):
                    wait_drained(pe, ("mx", l, i, n), t)
                name = ("mt", l, i)
                begin(name, t)
                for s in range(SUB):
                    ins = pe.transpose(bank(name)[0:HEADS, s * P:s * P + P], neg_max[i][:, s, :], ident[:, :])
                done(ins, name)

            def scores(l, i, t, n0=0, n1=2 * RC):
                if n0 == 0:
                    wait_drained(pe, ("mt", l, i), t)
                for n in range(n0, n1):
                    name = ("st", l, i, n)
                    half, c = n // RC, n % RC
                    rows = ROW_N[c]
                    begin(name, t)
                    dst = bank(name)[0:rows, :]
                    pe.matmul(dst, row_heads[:, half, c * P:c * P + rows], neg_max_t[:, :], start=True, stop=False,
                              skip_group_check=True)
                    done(terms(dst, [(kbd_hi[:, half, c * P:c * P + rows], kbd_lo[:, half, c * P:c * P + rows])],
                               [(q_hi[i][:, half, :], q_lo[i][:, half, :])], start=False), name)

            def values(l, i, t):
                for s in range(SUB):
                    name = ("pv", l, i, s)
                    begin(name, t)
                    for n in range(2 * RC):
                        if s == 0:
                            wait_drained(pe, ("st", l, i, n), t)
                        half, c = n // RC, n % RC
                        rows = ROW_N[c]
                        ins = pe.matmul(bank(name)[:, half * HH * VW:(half + 1) * HH * VW],
                                        probs[0:rows, n, s * P:s * P + P],
                                        vbd[0:rows, c, half, :, :].rearrange("p h d -> p (h d)"),
                                        start=c == 0, stop=c == RC - 1)
                    done(ins, name)

            def by_token(name, t, lefts, weight, start_hi, bias=None):
                for j in range(2):
                    s = 2 * name[-1] + j
                    dst = bank(name)[:, j * D:j * D + D]
                    ins = terms(dst, [(lh[:, k, s * P:s * P + P], ll[:, k, s * P:s * P + P]) for lh, ll in [lefts]
                                      for k in range(KC)], weight, start=start_hi and j == 0, stop=bias is None)
                    if bias is not None:
                        ins = pe.matmul(dst, ones_row[0:2, :], bias_rows[0:2, bias, :], start=False, stop=True,
                                        skip_group_check=True)
                return ins

            def project(l, i, t):
                wait_act("ot", l, i, t)
                for n in range(2):
                    name = ("wo", l, i, n)
                    begin(name, t)
                    done(by_token(name, t, (act_hi[i], act_lo[i]), wat(l, WO, KC), True, 1 if l == "A" else None), name)

            def hidden1(i, t, ms):
                for m in ms:
                    name = ("h1", i, m)
                    if m == 0:
                        wait_act("ln", "B", i, t)
                    begin(name, t)
                    for k in range(KC):
                        w = w0[:, k, m * P:m * P + P]
                        pe.matmul(bank(name), w, act_hi[i][:, k, :], start=k == 0, stop=False)
                        ins = pe.matmul(bank(name), w, act_lo[i][:, k, :], start=False, stop=k == KC - 1)
                    done(ins, name)

            def hidden2(i, t, m):
                name = ("h2", i, m)
                begin(name, t)
                for k in range(HC):
                    if m == 0:
                        wait_drained(pe, ("h1", i, k), t)
                    w = w1[:, k, m * P:m * P + P]
                    pe.matmul(bank(name), w, h1_hi[:, k, :], start=k == 0, stop=False)
                    ins = pe.matmul(bank(name), w, h1_lo[:, k, :], start=False, stop=k == HC - 1)
                done(ins, name)

            def third(i, t, m):
                wait_drained(pe, ("h2", i, m), t)
                if m == 0:
                    begin(("y", i, 0), t)
                    begin(("y", i, 1), t)
                at = m % H2RING
                for s in range(SUB):
                    name = ("y", i, s // 2)
                    dst = bank(name)[:, (s % 2) * D:(s % 2) * D + D]
                    pe.matmul(dst, h2_hi[:, at, s * P:s * P + P], w2[:, m, :], start=m == 0 and s % 2 == 0, stop=False,
                              skip_group_check=True)
                    ins = pe.matmul(dst, h2_lo[:, at, s * P:s * P + P], w2[:, m, :], start=False, stop=m == HC - 1,
                                    skip_group_check=True)
                    if m == HC - 1 and s % 2 == 1:
                        done(ins, name)

            pe.wait_ge(setup_dve, 13)
            pe.wait_ge(setup_act, 6)
            with pe.Fori(0, T) as t:
                keys_values("A", t)
                transposes("ln", "A", 0, t)
                query("A", 0, t)
                maxima("A", 0, t)
                transposes("ln", "A", 1, t)
                query("A", 1, t)
                neg_max_rows("A", 0, t)
                for n in range(2 * RC):
                    scores("A", 0, t, n, n + 1)
                    maxima("A", 1, t, n * 16 // 10, (n + 1) * 16 // 10)
                values("A", 0, t)
                neg_max_rows("A", 1, t)
                transposes("ot", "A", 0, t)
                scores("A", 1, t, 0, 5)
                project("A", 0, t)
                scores("A", 1, t, 5)
                values("A", 1, t)
                transposes("ln", "B", 0, t)
                hidden1(0, t, range(HC))
                transposes("ot", "A", 1, t)
                keys_values("C", t)
                project("A", 1, t)
                for m in range(HC):
                    hidden2(0, t, m)
                    if m >= 1:
                        third(0, t, m - 1)
                    if m == 3:
                        transposes("ln", "B", 1, t)
                hidden1(1, t, range(1))
                third(0, t, HC - 1)
                hidden1(1, t, range(1, HC))
                for m in range(HC):
                    hidden2(1, t, m)
                    if m >= 1:
                        third(1, t, m - 1)
                    if m == 3:
                        transposes("ln", "C", 0, t)
                    if m == 4:
                        query("C", 0, t)
                    if m == 5:
                        maxima("C", 0, t, 0, 8)
                    if m == 6:
                        maxima("C", 0, t, 8)
                third(1, t, HC - 1)
                neg_max_rows("C", 0, t)
                scores("C", 0, t)
                transposes("ln", "C", 1, t)
                query("C", 1, t)
                maxima("C", 1, t)
                values("C", 0, t)
                neg_max_rows("C", 1, t)
                transposes("ot", "C", 0, t)
                scores("C", 1, t, 0, 5)
                project("C", 0, t)
                scores("C", 1, t, 5)
                values("C", 1, t)
                transposes("ot", "C", 1, t)
                project("C", 1, t)

            def wd(n, m0=0, m=D):
                return [(wd_hi[:, n, k, m0:m0 + m], wd_lo[:, n, k, m0:m0 + m]) for k in range(KC)]

            pe.wait_ge(wd_lo_ready, 1)
            with pe.Fori(0, T) as t:
                for i in range(NT):
                    transposes("ln", "D", i, t)
                for i in range(NT):
                    wait_act("ln", "D", i, t)
                    for n in range(2):
                        name = ("xo", i, n)
                        begin(name, t)
                        done(by_token(name, t, (act_hi[i], act_lo[i]), wd(6), True, 2), name)
                    for m in range(KC):
                        for g in range(3):
                            name = ("gate", i, g, m)
                            begin(name, t)
                            terms(bank(name), wd(g, m * P, P),
                                  [(act_hi[i][:, k, :], act_lo[i][:, k, :]) for k in range(KC)], stop=False)
                            if m == 0 and g == 0:
                                pe.wait_ge(c_lo_ready, c_count(i, t))
                            done(terms(bank(name), wd(3 + g, m * P, P),
                                       [(c_hi[i][:, k, :], c_lo[i][:, k, :]) for k in range(KC)], start=False), name)
            for i in range(NT):
                pe.wait_ge(c_lo_ready, c_count(i, T))
                for n in range(2):
                    name = ("co", i, n)
                    begin(name, 0)
                    done(by_token(name, 0, (c_hi[i], c_lo[i]), wd(7), True), name)


def kernel(**inputs):
    import concourse.bacc as bacc
    from concourse.bass_utils import run_bass_kernel_spmd

    v = {k: np.asarray(x) for k, x in inputs.items()}
    wkv = v["L1_xattn_Wkv"]
    row = np.arange(RC * P).reshape(RC, P)
    heads = np.arange(HH)
    arrays = {
        "x": v["x"].reshape(T * NT, P, SUB, D),
        "ctx_t": v["ctx_512"].transpose(0, 2, 1),
        "wq0": v["L0_xattn_Wq"], "wk0": v["L0_xattn_Wk"], "wv0": v["L0_xattn_Wv"], "wo0": v["L0_xattn_Wo"],
        "wq1": v["L1_xattn_Wq"].T, "wk1": wkv[:D].T, "wv1": wkv[D:].T, "wo1": v["L1_xattn_Wo"].T,
        "cols": np.stack([v[n].reshape(KC, P).T for n in ("L0_xattn_bq", "L0_xattn_bk", "L1_ffn_bf", "L1_ffn_bi",
                                                          "L1_ffn_bc", "L1_ffn_in_c")], 1),
        "rows": np.stack([v["L0_xattn_bv"], v["L0_xattn_bo"], v["L1_ffn_bo"]]),
        "g": np.concatenate([v["g_xattn"], v["g_ffn"]]),
        "s": np.stack([v["L0_ffn_s0"], v["L0_ffn_s1"], v["L0_ffn_s2"]]),
        "k0": v["L0_ffn_k0"], "k1": v["L0_ffn_k1"], "k2": v["L0_ffn_k2"],
        "wf": v["L1_ffn_wf"].T, "wi": v["L1_ffn_wi"].T, "wc": v["L1_ffn_wc"].T, "wo_d": v["L1_ffn_wo"].T,
        "uf": v["L1_ffn_uf"].T, "ui": v["L1_ffn_ui"].T, "uc": v["L1_ffn_uc"].T, "uo_d": v["L1_ffn_uo"].T,
        "ident": np.eye(P, dtype=np.float32),
        "not_first": np.array([[0.0], [-1.0]], np.float32),
        "head_of_feature": (np.arange(P)[:, None] // DK == heads).astype(np.float32),
        "head_of_row": (row.T[:, :, None] // KEYS == heads).astype(np.float32),
        "row_heads": (np.arange(2 * ROWS).reshape(2, ROWS) // KEYS == np.arange(HEADS)[:, None, None]).astype(np.float32),
    }
    arrays = {k: np.ascontiguousarray(x) for k, x in arrays.items()}
    nc = bacc.Bacc("TRN2", target_bir_lowering=False, num_devices=1)
    aps = {k: nc.dram_tensor(f"in_{k}", x.shape, mybir.dt.from_np(x.dtype), kind="ExternalInput").ap()
           for k, x in arrays.items()}
    out = nc.dram_tensor("out_x", (T * NT, P, SUB, D), F32, kind="ExternalOutput").ap()
    build(nc, aps, out)
    r = run_bass_kernel_spmd(nc, [{f"in_{k}": x for k, x in arrays.items()}], core_ids=[0])
    return r.results[0]["out_x"].reshape(T, B, D)
```

```python
import numpy as np
import concourse.bass as bass
from concourse import mybir
from concourse.alu_op_type import AluOpType as ALU
from contextlib import ExitStack

F32 = mybir.dt.float32
F32R = mybir.dt.float32r
U8 = mybir.dt.uint8
F16 = mybir.dt.float16
BF16 = mybir.dt.bfloat16
ACT = mybir.ActivationFunctionType
AX = mybir.AxisListType

T, B, D = 4, 1024, 256
P = 128
KC = D // P
TILE = 512
SUB = TILE // P
NT = B // TILE
HEADS, DK, KEYS, IMG = 16, 16, 77, 128
HH = HEADS // 2
ROWS = HH * KEYS
RC = -(-ROWS // P)
ROW_N = [min(P, ROWS - c * P) for c in range(RC)]
KP = KEYS + 1
MXH = 4
VW = DK + 1
WINDOW = 3
FIRST_HEAD = [min(c * P // KEYS, HH - WINDOW) for c in range(RC)]
VPARTS = 3
P_RING = 3
LO_DVE = (4, 9)
LO_POOL = tuple(n for n in range(2 * RC) if n not in LO_DVE)
HID = 1024
HC = HID // P
H2RING = 2
EPS = 1e-5
KSCALE = float(DK) ** -0.5

GENERAL, OUTS, WIDE = (0, 1, 2), (3, 4), (5, 6, 7)
BOTH = OUTS + WIDE
READ, GATES = (2, 3), (4, 5, 6, 7)
LAYER_NORMS = [("A", 0), ("A", 1), ("B", 0), ("B", 1), ("C", 0), ("C", 1)]


HI_KINDS = ("ln", "q", "ot", "h1", "h2")


class Job:
    def __init__(self, bank, nth, hi_nth):
        self.bank, self.nth, self.per, self.hi_nth, self.hi_per = bank, nth, 0, hi_nth, 0

    def count(self, t):
        return t * self.per + self.nth

    def hi_count(self, t):
        return t * self.hi_per + self.hi_nth


def number_jobs(order, base, hi_base):
    jobs, used, his, turn = {}, [0] * 8, [0] * 8, {}
    for name, ring in order:
        at = turn.get(ring, 0)
        turn[ring] = at + 1
        b = ring[at % len(ring)]
        used[b] += 1
        his[b] += name[0] in HI_KINDS
        jobs[name] = Job(b, base[b] + used[b], hi_base[b] + his[b])
    for job in jobs.values():
        job.per, job.hi_per = used[job.bank], his[job.bank]
    return jobs, used, his


def phase1_order():
    out = []

    def add(ring, *names):
        out.extend((n, ring) for n in names)

    def two(kind, l, i, ring=GENERAL):
        add(ring, (kind, l, i, 0), (kind, l, i, 1))

    def maxima(ring, l, i, a=0, b=16):
        add(ring, *[("mx", l, i, n) for n in range(a, b)])

    def scores(l, i, a=0, b=2 * RC):
        add(WIDE, *[("st", l, i, n) for n in range(a, b)])

    def values(l, i, a=0, b=SUB):
        add(GENERAL, *[("pv", l, i, s) for s in range(a, b)])

    add(OUTS, ("k", "A"), *[("v", "A", c) for c in range(3)])
    two("ln", "A", 0, OUTS), two("q", "A", 0, OUTS)
    maxima(BOTH, "A", 0), add(OUTS, ("mt", "A", 0)), scores("A", 0, 0, 2)
    two("ln", "A", 1), two("q", "A", 1), scores("A", 0, 2)
    maxima(OUTS, "A", 1, 0, 8), maxima(BOTH, "A", 1, 8), values("A", 0, 0, 3)
    add(GENERAL, ("mt", "A", 1)), values("A", 0, 3)
    scores("A", 1)
    two("ot", "A", 0), two("wo", "A", 0), values("A", 1), two("ln", "B", 0)
    add(WIDE, *[("h1", 0, m) for m in range(HC)])
    two("ot", "A", 1), add(GENERAL, ("k", "C"), *[("v", "C", c) for c in range(3)]), two("wo", "A", 1)
    add(WIDE, *[("h2", 0, m) for m in range(HC)], *[("h1", 1, m) for m in range(HC)],
        *[("h2", 1, m) for m in range(HC)])
    add(OUTS, ("y", 0, 0), ("y", 0, 1), ("y", 1, 0), ("y", 1, 1))
    two("ln", "B", 1), two("ln", "C", 0), two("q", "C", 0)
    maxima(GENERAL, "C", 0), add(GENERAL, ("mt", "C", 0))
    scores("C", 0), two("ln", "C", 1), two("q", "C", 1)
    maxima(BOTH, "C", 1), values("C", 0)
    two("ot", "C", 0), two("wo", "C", 0), add(GENERAL, ("mt", "C", 1))
    scores("C", 1), values("C", 1), two("ot", "C", 1), two("wo", "C", 1)
    return out


def phase2_order():
    out = [(("ln", "D", i, k), GENERAL[0:2]) for i in range(NT) for k in range(KC)]
    for i in range(NT):
        out += [(("xo", i, n), READ) for n in range(2)]
        out += [(("gate", i, g, m), GATES) for m in range(KC) for g in range(3)]
    return out


def phase3_order():
    return [(("co", i, n), READ) for i in range(NT) for n in range(2)]


def build(nc, a, out):
    with ExitStack() as ctx:
        def keep(name, shape, dt, scope=ctx):
            return scope.enter_context(nc.sbuf_tensor(name, shape, dt))

        def sem(name):
            return ctx.enter_context(nc.semaphore(name))

        x_sb = keep("x_sb", [P, T * NT, SUB, D], F32)
        ident = keep("ident", [P, P], F32)
        ones_row = keep("ones_row", [2, P], F32R)
        bias_rows = keep("bias_rows", [2, 3, D], F32R)
        not_first = keep("not_first", [2, 1], F32)
        one_f = keep("one_f", [2, P], F32)
        cols = keep("cols", [P, 6, KC], F32)
        bqk, col_b, c0_col = cols[:, 0:2, :], cols[:, 2:5, :], cols[:, 5, :]
        half_b = keep("half_b", [P, 2, KC], F32)
        gates_in = keep("gates_in", [P, 4], F32)
        gates = keep("gates", [P, 4], F32)
        gain_b = keep("gain_b", [P, 1], F32)
        nothing = keep("nothing", [P, 1], F32)
        eps = keep("eps", [P, SUB], F32)
        minus_half = keep("minus_half", [P, SUB], F32)
        scal = keep("scal", [P, 3], F32)
        sgn = keep("sgn", [P, 8], F32)
        token = [keep(f"token{i}", [P, SUB, D], F32) for i in range(NT)]
        act_hi = [keep(f"act_hi{i}", [P, KC, TILE], F32R) for i in range(NT)]
        act_lo = [keep(f"act_lo{i}", [P, KC, TILE], F32R) for i in range(NT)]
        stats = [keep(f"stats{i}", [P, SUB, 6], F32) for i in range(NT)]
        moments = [keep(f"moments{i}", [P, SUB, 2], F32) for i in range(NT)]
        var_eps = [keep(f"var_eps{i}", [P, SUB], F32) for i in range(NT)]
        rstd = [keep(f"rstd{i}", [P, SUB], F32) for i in range(NT)]

        p1 = ExitStack()
        w0 = keep("w0", [P, KC, HID], F32R, p1)
        w1 = keep("w1", [P, HC, HID], F32R, p1)
        w2 = keep("w2", [P, HC, D], F32R, p1)
        WQ, WO, WK, WV = 0, KC * D, 2 * KC * D, 2 * KC * D + D
        WN = WV + D
        wat_hi = [keep(f"wat_hi{l}", [P, WN], F32R, p1) for l in range(2)]
        wat_lo = [keep(f"wat_lo{l}", [P, WN], F32R, p1) for l in range(2)]
        bk4 = keep("bk4", [P, KC], F32, p1)
        head_of_feature = keep("head_of_feature", [P, HH], F32, p1)
        head_of_row = keep("head_of_row", [P, RC, HH], F32, p1)
        row_heads = keep("row_heads", [HEADS, 2, ROWS], F32R, p1)
        ctx_sb = keep("ctx_sb", [IMG, T, KEYS], F32, p1)
        at = ExitStack()
        rep_hi = keep("rep_hi", [IMG, HH, KEYS], F32R, at)
        rep_lo = keep("rep_lo", [IMG, HH, KEYS], F32R, at)
        at.close()
        q_hi = [keep("q_hi0", [P, KC, TILE], F32R, p1)]
        q_lo = [keep("q_lo0", [P, KC, TILE], F32R, p1)]
        k_f = keep("k_f", [P, KC, KEYS], F32, p1)
        k_hi = keep("k_hi", [P, KC, KEYS], F32R, p1)
        k_lo = keep("k_lo", [P, KC, KEYS], F32R, p1)
        kbd_hi = {"C": keep("kbd_hi_c", [P, 2, ROWS], F32R, p1)}
        kbd_lo = keep("kbd_lo", [P, 2, ROWS], F32R, p1)
        vbd = keep("vbd", [P, RC, 2, WINDOW, DK], F32, p1)
        v_part = [keep(f"v_part{j}", [P, RC, 2, WINDOW, VW], BF16, p1) for j in range(VPARTS)]
        neg_max = [keep(f"neg_max{i}", [P, SUB, HEADS], F32, p1) for i in range(NT)]
        neg_max_t = keep("neg_max_t", [HEADS, TILE], F32R, p1)
        inv_sum = keep("inv_sum", [P, SUB, HEADS], F32, p1)
        at = ExitStack()
        row_f = keep("row_f", [2, 3, D], F32, at)
        row_hi = keep("row_hi", [2, 3, D], F32R, at)
        w_raw = [keep(f"w_raw{l}", [P, WN], F32, at) for l in range(2)]
        rh_raw = keep("rh_raw", [HEADS, 2, ROWS], F32, at)
        k2_raw = keep("k2_raw", [P, HC, D], U8, at)
        k1_raw = keep("k1_raw", [P, HC, HID], U8, at)
        at.close()
        at = ExitStack()
        p_hi = keep("p_hi", [P, 2 * RC, TILE], F16, at)
        p_lo = keep("p_lo", [P, 2 * RC, TILE], F16, at)
        q_hi.append(keep("q_hi1", [P, KC, TILE], F32R, at))
        q_lo.append(keep("q_lo1", [P, KC, TILE], F32R, at))
        at.close()
        at = ExitStack()
        keep("before_p_f", [P, 2 * RC + 2 * 2 * KC, TILE], F16, at)
        keep("before_p_f2", [P, 2 * RC, TILE], F16, at)
        p_f = keep("p_f", [P, P_RING, TILE], F32, at)
        kbd_hi["A"] = keep("kbd_hi_a", [P, 2, ROWS], F32R, at)
        at.close()
        at = ExitStack()
        h1_hi = keep("h1_hi", [P, HC, TILE], F32R, at)
        h1_lo = keep("h1_lo", [P, HC, TILE], F32R, at)
        h2_hi = keep("h2_hi", [P, H2RING, TILE], F32R, at)
        h2_lo = keep("h2_lo", [P, H2RING, TILE], F32R, at)
        at.close()
        p1.close()

        k0_raw = x_sb[:, T * NT - 1, :, :].bitcast(U8)

        p2 = ExitStack()
        NW = 8
        XO, CO = 0, 7
        wd_hi = keep("wd_hi", [P, NW, KC, D], F32R, p2)
        wd_lo = keep("wd_lo", [P, NW, KC, D], F32R, p2)
        wd_raw = keep("wd_raw", [P, NW, KC, D], F32, p2)
        xo_sb = keep("xo_sb", [P, T * NT, SUB, D], F32, p2)
        c_f = [keep(f"c_f{i}", [P, KC, TILE], F32, p2) for i in range(NT)]
        c_hi = [keep(f"c_hi{i}", [P, KC, TILE], F32R, p2) for i in range(NT)]
        c_lo = [keep(f"c_lo{i}", [P, KC, TILE], F32R, p2) for i in range(NT)]
        gate = [[keep(f"gate{g}_{i}", [P, KC, TILE], F32, p2) for g in range(3)] for i in range(NT)]
        co_sb = [keep(f"co_sb{i}", [P, SUB, D], F32, p2) for i in range(NT)]
        p2.close()

        psum = ctx.enter_context(nc.psum_tensor("psum", [P, 8, 512], F32))

        bank_filled = [sem(f"bank_filled{b}") for b in range(8)]
        bank_drained = [sem(f"bank_drained{b}") for b in range(8)]
        consts_loaded = sem("consts_loaded")
        attn_weights_loaded = [sem(f"attn_weights_loaded{l}") for l in range(2)]
        bits_loaded = sem("bits_loaded")
        x_loaded = [sem(f"x_loaded{i}") for i in range(NT)]
        wd_loaded = [sem(f"wd_loaded{h}") for h in range(2)]
        out_stored = sem("out_stored")
        setup_dve = sem("setup_dve")
        setup_act = sem("setup_act")
        setup_pool = sem("setup_pool")
        stats_ready = sem("stats_ready")
        moments_ready = sem("moments_ready")
        var_eps_ready = sem("var_eps_ready")
        rstd_ready = sem("rstd_ready")
        normed_ready = sem("normed_ready")
        rep_hi_ready = sem("rep_hi_ready")
        rep_lo_ready = sem("rep_lo_ready")
        k_parts_ready = sem("k_parts_ready")
        kbd_hi_ready = sem("kbd_hi_ready")
        kbd_lo_ready = sem("kbd_lo_ready")
        hi_ready = [sem(f"hi_ready{b}") for b in range(8)]
        v_masked = sem("v_masked")
        v_parts_ready = sem("v_parts_ready")
        p_lo_dve = sem("p_lo_dve")
        p_lo_pool = sem("p_lo_pool")
        inv_sum_ready = sem("inv_sum_ready")
        wd_hi_ready = sem("wd_hi_ready")
        wd_lo_ready = sem("wd_lo_ready")
        fc_ready = sem("fc_ready")
        ig_ready = sem("ig_ready")
        c2_ready = sem("c2_ready")
        c_f_ready = sem("c_f_ready")
        c_hi_ready = sem("c_hi_ready")
        c_lo_ready = sem("c_lo_ready")
        pre_ready = [sem("pre_ready_pool"), sem("pre_ready_dve")]
        h_ready = sem("h_ready")
        out_ready = sem("out_ready")

        jobs, per1, his1 = number_jobs(phase1_order(), [0] * 8, [0] * 8)
        base2 = [T * n for n in per1]
        jobs2, per2, _ = number_jobs(phase2_order(), base2, [T * n for n in his1])
        jobs3, _, _ = number_jobs(phase3_order(), [b + T * n for b, n in zip(base2, per2)], [0] * 8)
        jobs = {**jobs, **jobs2, **jobs3}

        def wait_filled(eng, name, t):
            eng.wait_ge(bank_filled[jobs[name].bank], jobs[name].count(t))

        def wait_drained(eng, name, t):
            eng.wait_ge(bank_drained[jobs[name].bank], jobs[name].count(t) + 1)

        def wait_free(eng, name, t):
            eng.wait_ge(bank_drained[jobs[name].bank], jobs[name].count(t))

        def bank(name):
            return psum[:, jobs[name].bank, :]

        LN1, LN2 = len(LAYER_NORMS), NT

        def ln_count(l, i, t):
            if l == "D":
                return t * LN2 + (T * LN1 + i + 1)
            return t * LN1 + (LAYER_NORMS.index((l, i)) + 1)

        def wait_hi(eng, name, t):
            eng.wait_ge(hi_ready[jobs[name].bank], jobs[name].hi_count(t))

        ATTN = [("A", 0), ("A", 1), ("C", 0), ("C", 1)]

        def attn_count(l, i, t, each):
            return t * (each * len(ATTN)) + each * (ATTN.index((l, i)) + 1)

        LAYER = {"A": 0, "C": 1}

        def wait_p_lo(eng, l, i, n, t):
            done_by, mine = (p_lo_dve, LO_DVE) if n in LO_DVE else (p_lo_pool, LO_POOL)
            eng.wait_ge(done_by, attn_count(l, i, t, len(mine)) - (len(mine) - 1 - mine.index(n)))

        def c_count(i, t):
            return t * NT + (2 * NT + i + 1)

        block = ctx.enter_context(nc.Block())

        @block.sync
        def _(sp):
            def weights(l, name, dst, n):
                sp.dma_start(w_raw[l][:, dst:dst + n * D].rearrange("p (c m) -> p c m", c=n),
                             a[name].rearrange("(c p) m -> p c m", p=P)).then_inc(attn_weights_loaded[l], 16)

            def x_tile(t, i):
                sp.dma_start(x_sb[:, t * NT + i, :, :],
                             a["x"][t * NT + i, :, :, :]).then_inc(x_loaded[i], 16)

            x_tile(0, 0)
            sp.dma_start(ctx_sb[:, :, :], a["ctx_t"].rearrange("b d k -> d b k")).then_inc(consts_loaded, 16)
            sp.dma_start(ident[:, :], a["ident"]).then_inc(consts_loaded, 16)
            for l in range(2):
                weights(l, f"wk{l}", WK, 1)
                weights(l, f"wv{l}", WV, 1)
                weights(l, f"wq{l}", WQ, KC)
                weights(l, f"wo{l}", WO, KC)
                if l == 0:
                    x_tile(0, 1)
            sp.dma_start(k0_raw, a["k0"].rearrange("(c p) m -> p c m", p=P)).then_inc(bits_loaded, 16)
            sp.dma_start(k1_raw[:, :, :], a["k1"].rearrange("(c p) m -> p c m", p=P)).then_inc(bits_loaded, 16)
            sp.dma_start(k2_raw[:, :, :], a["k2"].rearrange("(c p) m -> p c m", p=P)).then_inc(bits_loaded, 16)
            sp.wait_ge(setup_dve, 13)
            with sp.Fori(1, T) as t:
                for i in range(NT):
                    sp.wait_ge(x_loaded[i], t * 16)
                    x_tile(t, i)
            wait_filled(sp, ("y", 1, 0), T - 1)
            wait_filled(sp, ("y", 1, 1), T - 1)
            for half, names in enumerate([["wo_d", "wf", "wi", "wc"], ["uf", "ui", "uc", "uo_d"]]):
                for j, name in enumerate(names):
                    sp.dma_start(wd_raw[:, half * NW // 2 + j, :, :],
                                 a[name].rearrange("(c p) m -> p c m", p=P)).then_inc(wd_loaded[half], 16)
            for i in range(NT):
                with sp.Fori(0, T) as t:
                    sp.wait_ge(out_ready, t + (i * T + 1))
                    sp.dma_start(out[t * NT + i, :, :, :], x_sb[:, t * NT + i, :, :]).then_inc(out_stored, 16)
            sp.wait_ge(out_stored, T * NT * 16)

        @block.gpsimd
        def _(pool):
            for first in bank_drained + [k_parts_ready, kbd_lo_ready, c_f_ready]:
                pool.sem_inc(first, 1)
            pool.memset(minus_half[:, :], -0.5).then_inc(setup_pool, 1)
            pool.memset(one_f[:, :], 1.0).then_inc(setup_pool, 1)
            pool.memset(eps[:, :], EPS).then_inc(setup_pool, 1)

            def rstd_of(l, i, t):
                pool.wait_ge(moments_ready, ln_count(l, i, t))
                pool.tensor_tensor(var_eps[i][:, :], moments[i][:, :, 1], eps[:, :], ALU.add).then_inc(var_eps_ready, 1)
                pool.wait_ge(var_eps_ready, ln_count(l, i, t))
                pool.tensor_tensor(rstd[i][:, :], var_eps[i][:, :], minus_half[:, :], ALU.pow).then_inc(rstd_ready, 1)

            def kbd_lo_of(l, t, before=None):
                if before is not None:
                    wait_filled(pool, ("st", "C", 1, 2 * RC - 1), before)
                pool.wait_ge(k_parts_ready, t * 4 + (1 + 2 * LAYER[l] + 2))
                for m in range(KC):
                    ins = pool.tensor_tensor(kbd_lo[:, m, :].rearrange("p (h k) -> p h k", h=HH),
                                             k_lo[:, m, :].bitcast(F32).unsqueeze(1).to_broadcast([P, HH, KEYS]),
                                             head_of_feature[:, :].unsqueeze(2).to_broadcast([P, HH, KEYS]), ALU.mult)
                ins.then_inc(kbd_lo_ready, 1)

            def p_lo_of(l, i, t, n0, n1):
                for n in range(n0, n1):
                    if n in LO_POOL:
                        rows = ROW_N[n % RC]
                        wait_drained(pool, ("st", l, i, n), t)
                        pool.tensor_tensor(p_lo[0:rows, n, :], p_f[0:rows, n % P_RING, :], p_hi[0:rows, n, :],
                                           ALU.subtract).then_inc(p_lo_pool, 1)

            def image(t, last):
                after, ta = ("D", 0) if last else ("A", t + 1)
                p_lo_of("A", 0, t, 2, 2 * RC)
                p_lo_of("A", 1, t, 0, 2 * RC)
                rstd_of("B", 0, t)
                kbd_lo_of("C", t)
                rstd_of("B", 1, t)
                rstd_of("C", 0, t)
                p_lo_of("C", 0, t, 0, 2)
                rstd_of("C", 1, t)
                p_lo_of("C", 0, t, 2, 2 * RC)
                rstd_of(after, 0, ta)
                p_lo_of("C", 1, t, 0, 2 * RC)
                rstd_of(after, 1, ta)
                if not last:
                    kbd_lo_of("A", ta, t)
                    p_lo_of("A", 0, ta, 0, 2)

            pool.wait_ge(setup_pool, 3)
            rstd_of("A", 0, 0)
            kbd_lo_of("A", 0)
            rstd_of("A", 1, 0)
            p_lo_of("A", 0, 0, 0, 2)
            with pool.Fori(0, T - 1) as t:
                image(t, False)
            image(T - 1, True)
            for h in range(2):
                pool.wait_ge(wd_hi_ready, h + 1)
                half = slice(h * NW // 2, (h + 1) * NW // 2)
                pool.tensor_tensor(wd_lo[:, half, :, :], wd_raw[:, half, :, :], wd_hi[:, half, :, :].bitcast(F32),
                                   ALU.subtract).then_inc(wd_lo_ready, 1)
            with pool.Fori(0, T - 1) as t:
                rstd_of("D", 0, t + 1)
                rstd_of("D", 1, t + 1)
            for i in range(NT):
                for n in range(2):
                    wait_drained(pool, ("co", i, n), 0)
                for t in range(T):
                    if t % 2 == 0:
                        tile = xo_sb[:, t * NT + i, :, :]
                        pool.tensor_tensor(tile, tile, co_sb[i][:, :, :], ALU.add).then_inc(pre_ready[0], 1)

        @block.scalar
        def _(act):
            for dst, name in [(gates_in[:, :], "g"), (scal[:, :], "s")]:
                act.dma_start(dst, a[name].partition_broadcast(P)).then_inc(consts_loaded, 16)
            act.dma_start(cols[:, :, :], a["cols"]).then_inc(consts_loaded, 16)
            act.dma_start(row_f[:, :, :], a["rows"].partition_broadcast(2)).then_inc(consts_loaded, 16)
            act.dma_start(not_first[:, :], a["not_first"]).then_inc(consts_loaded, 16)
            act.dma_start(head_of_feature[:, :], a["head_of_feature"]).then_inc(consts_loaded, 16)
            act.dma_start(head_of_row[:, :, :], a["head_of_row"]).then_inc(consts_loaded, 16)
            act.dma_start(rh_raw[:, :, :], a["row_heads"]).then_inc(consts_loaded, 16)
            act.wait_ge(consts_loaded, 10 * 16)
            act.activation(gates[:, :], gates_in[:, :], ACT.Tanh).then_inc(setup_act, 1)
            act.activation(row_heads[:, :, :], rh_raw[:, :, :], ACT.Copy).then_inc(setup_act, 1)
            act.wait_ge(attn_weights_loaded[0], 4 * 16)
            act.activation(wat_hi[0][:, :], w_raw[0][:, :], ACT.Copy).then_inc(setup_act, 1)

            def hi_of(dst, name, t, func=ACT.Copy, bias=None):
                wait_filled(act, name, t)
                more = {} if bias is None else {"bias": bias}
                act.activation(dst, bank(name), func, **more).then_inc(hi_ready[jobs[name].bank], 1)

            def act_hi_of(kind, l, i, t):
                for k in range(KC):
                    hi_of(act_hi[i][:, k, :], (kind, l, i, k), t)

            def q_hi_of(l, i, t):
                for m in range(KC):
                    if l == "A":
                        hi_of(q_hi[i][:, m, :], ("q", l, i, m), t, ACT.Identity, bqk[:, 0, m:m + 1])
                    else:
                        hi_of(q_hi[i][:, m, :], ("q", l, i, m), t)

            def rep_hi_of(l, t):
                act.activation(rep_hi[:, :, :], ctx_sb[:, t, :].unsqueeze(1).to_broadcast([IMG, HH, KEYS]),
                               ACT.Copy).then_inc(rep_hi_ready, 1)


            def k_of(l, t):
                act.wait_ge(k_parts_ready, t * 4 + (1 + 2 * LAYER[l]))
                wait_filled(act, ("k", l), t)
                pk = bank(("k", l))[:, 0:KC * KP].rearrange("p (c k) -> p c k", c=KC)[:, :, 0:KEYS]
                if l == "A":
                    for m in range(KC):
                        ins = act.activation(k_f[:, m, :], pk[:, m, :], ACT.Identity, scale=KSCALE, bias=bk4[:, m:m + 1])
                else:
                    ins = act.activation(k_f[:, :, :], pk, ACT.Copy, scale=KSCALE)
                ins.then_inc(bank_drained[jobs["k", l].bank], 1)

            def neg_max_of(l, i, t):
                wait_filled(act, ("mt", l, i), t)
                act.activation(neg_max_t[:, :], bank(("mt", l, i))[0:HEADS, :], ACT.Copy)\
                    .then_inc(bank_drained[jobs["mt", l, i].bank], 1)

            def exps(l, i, t, n0, n1, before):
                if before is not None:
                    wait_filled(act, ("pv", *before[0], SUB - 1), before[1])
                for n in range(n0, n1):
                    name, rows = ("st", l, i, n), ROW_N[n % RC]
                    wait_filled(act, name, t)
                    act.activation(p_hi[0:rows, n, :], bank(name)[0:rows, :], ACT.Exp)
                    if n >= P_RING:
                        wait_p_lo(act, l, i, n - P_RING, t)
                    act.activation(p_f[0:rows, n % P_RING, :], bank(name)[0:rows, :], ACT.Exp)\
                        .then_inc(bank_drained[jobs[name].bank], 1)

            def hidden(kind, i, t, ms):
                for m in ms:
                    name = (kind, i, m)
                    if kind == "h2":
                        hi_of(h2_hi[:, m % H2RING, :], name, t, ACT.Relu)
                    else:
                        hi_of(h1_hi[:, m, :], name, t, ACT.Relu)

            def image(t, last):
                act_hi_of("ln", "A", 1, t)
                q_hi_of("A", 1, t)
                exps("A", 0, t, 2, 2 * RC, None)
                neg_max_of("A", 1, t)
                exps("A", 1, t, 0, 3, (("A", 0), t))
                act_hi_of("ot", "A", 0, t)
                exps("A", 1, t, 3, 2 * RC, None)
                act_hi_of("ln", "B", 0, t)
                act_hi_of("ot", "A", 1, t)
                rep_hi_of("C", t)
                hidden("h1", 0, t, range(6))
                k_of("C", t)
                hidden("h1", 0, t, range(6, HC))
                hidden("h2", 0, t, range(4))
                act_hi_of("ln", "B", 1, t)
                hidden("h2", 0, t, range(4, HC))
                hidden("h1", 1, t, range(HC))
                hidden("h2", 1, t, range(4))
                act_hi_of("ln", "C", 0, t)
                hidden("h2", 1, t, range(4, 5))
                q_hi_of("C", 0, t)
                hidden("h2", 1, t, range(5, HC))
                neg_max_of("C", 0, t)
                exps("C", 0, t, 0, 7, None)
                act_hi_of("ln", "C", 1, t)
                exps("C", 0, t, 7, 2 * RC, None)
                q_hi_of("C", 1, t)
                if not last:
                    rep_hi_of("A", t + 1)
                act_hi_of("ot", "C", 0, t)
                neg_max_of("C", 1, t)
                if last:
                    exps("C", 1, t, 0, 2 * RC, (("C", 0), t))
                else:
                    k_of("A", t + 1)
                    exps("C", 1, t, 0, 6, (("C", 0), t))
                    act_hi_of("ln", "A", 0, t + 1)
                    exps("C", 1, t, 6, 8, None)
                    q_hi_of("A", 0, t + 1)
                    exps("C", 1, t, 8, 2 * RC, None)
                if last:
                    for h in range(2):
                        act.wait_ge(wd_loaded[h], NW // 2 * 16)
                        half = slice(h * NW // 2, (h + 1) * NW // 2)
                        act.activation(wd_hi[:, half, :, :], wd_raw[:, half, :, :], ACT.Copy).then_inc(wd_hi_ready, 1)
                if not last:
                    neg_max_of("A", 0, t + 1)
                act_hi_of("ot", "C", 1, t)
                if not last:
                    exps("A", 0, t + 1, 0, 2, None)

            rep_hi_of("A", 0)
            k_of("A", 0)
            act_hi_of("ln", "A", 0, 0)
            q_hi_of("A", 0, 0)
            act.wait_ge(attn_weights_loaded[1], 4 * 16)
            act.activation(wat_hi[1][:, :], w_raw[1][:, :], ACT.Copy).then_inc(setup_act, 1)
            act.wait_ge(bits_loaded, 3 * 16)
            act.wait_ge(setup_dve, 3)
            for h in range(2):
                act.activation(w1[:, h * 4:h * 4 + 4, :], k1_raw[:, h * 4:h * 4 + 4, :], ACT.Identity,
                               scale=sgn[:, 4:5], bias=sgn[:, 5:6]).then_inc(setup_act, 1)
            act.wait_ge(setup_dve, 13)
            neg_max_of("A", 0, 0)
            exps("A", 0, 0, 0, 2, None)
            with act.Fori(0, T - 1) as t:
                image(t, False)
            image(T - 1, True)

            def gates_of(i, t, m):
                for g in range(3):
                    name = ("gate", i, g, m)
                    wait_filled(act, name, t)
                    half = 0.5 if g < 2 else 1.0
                    bias = half_b[:, g, m:m + 1] if g < 2 else col_b[:, 2, m:m + 1]
                    act.activation(gate[i][g][:, m, :], bank(name), ACT.Tanh, scale=half, bias=bias)\
                        .then_inc(bank_drained[jobs[name].bank], 1)

            def cell(i, t):
                act.wait_ge(c2_ready, t * NT + (i + 1))
                act.activation(c_hi[i][:, :, :], gate[i][0][:, :, :], ACT.Copy, scale=0.5).then_inc(c_hi_ready, 1)
                act.activation(c_f[i][:, :, :], gate[i][0][:, :, :], ACT.Copy, scale=0.5).then_inc(c_f_ready, 1)

            def x_out(i, t):
                for n in range(2):
                    name = ("xo", i, n)
                    wait_filled(act, name, t)
                    act.activation(xo_sb[:, t * NT + i, 2 * n:2 * n + 2, :],
                                   bank(name).rearrange("p (s d) -> p s d", s=2), ACT.Copy)\
                        .then_inc(bank_drained[jobs[name].bank], 1)

            def c_out(i):
                for n in range(2):
                    name = ("co", i, n)
                    wait_filled(act, name, 0)
                    act.activation(co_sb[i][:, 2 * n:2 * n + 2, :], bank(name).rearrange("p (s d) -> p s d", s=2),
                                   ACT.Copy).then_inc(bank_drained[jobs[name].bank], 1)

            def read_out(i, t):
                act.wait_ge(pre_ready[t % 2], i * (T // 2) + t // 2 + 1)
                tile = xo_sb[:, t * NT + i, :, :]
                act.activation(tile, tile, ACT.Tanh).then_inc(h_ready, 1)

            def step(t, last):
                x_out(0, t)
                act.wait_ge(c_lo_ready, c_count(0, t))
                gates_of(0, t, 0)
                act_hi_of("ln", "D", 1, t)
                gates_of(0, t, 1)
                x_out(1, t)
                act.wait_ge(c_lo_ready, c_count(1, t))
                gates_of(1, t, 0)
                cell(0, t)
                if last:
                    c_out(0)
                else:
                    act_hi_of("ln", "D", 0, t + 1)
                gates_of(1, t, 1)
                cell(1, t)

            act_hi_of("ln", "D", 0, 0)
            with act.Fori(0, T - 1) as t:
                step(t, False)
            step(T - 1, True)
            for t in range(T):
                read_out(0, t)
            c_out(1)
            for t in range(T):
                read_out(1, t)

        @block.vector
        def _(dve):
            dve.wait_ge(consts_loaded, 10 * 16)
            dve.wait_ge(setup_pool, 3)
            dve.tensor_scalar(sgn[:, 0:2], scal[:, 0:2], 0.0, None, ALU.is_gt).then_inc(setup_dve, 1)
            dve.tensor_scalar(sgn[:, 2:4], scal[:, 0:2], 0.0, None, ALU.is_lt).then_inc(setup_dve, 1)
            dve.wait_ge(setup_dve, 2)
            dve.tensor_tensor(sgn[:, 6:8], sgn[:, 0:2], sgn[:, 2:4], ALU.subtract)
            dve.tensor_tensor(sgn[:, 5:6], sgn[:, 3:4], sgn[:, 1:2], ALU.subtract)
            dve.tensor_scalar(sgn[:, 4:5], sgn[:, 1:2], sgn[:, 3:4], 2.0, ALU.subtract, ALU.mult).then_inc(setup_dve, 1)
            dve.wait_ge(setup_dve, 3)
            dve.wait_ge(setup_act, 1)
            dve.tensor_tensor(gain_b[:, :], scal[:, 0:1], scal[:, 1:2], ALU.mult).then_inc(setup_dve, 1)
            dve.wait_ge(setup_dve, 4)
            dve.tensor_scalar(gain_b[:, :], gain_b[:, :], scal[:, 2:3], 8.0, ALU.mult, ALU.mult).then_inc(setup_dve, 1)
            dve.wait_ge(setup_dve, 5)
            dve.tensor_scalar(gain_b[:, :], gain_b[:, :], gates[:, 2:3], sgn[:, 6:7], ALU.mult, ALU.mult)\
                .then_inc(setup_dve, 1)
            dve.wait_ge(setup_dve, 6)
            dve.tensor_scalar(gain_b[:, :], gain_b[:, :], sgn[:, 7:8], None, ALU.mult)
            dve.tensor_copy(ones_row[:, :], one_f[:, :])
            dve.tensor_copy(row_hi[:, :, :], row_f[:, :, :]).then_inc(setup_dve, 1)
            dve.tensor_scalar(bk4[:, :], bqk[:, 1, :], KSCALE, None, ALU.mult)
            dve.tensor_scalar(half_b[:, :, :], col_b[:, 0:2, :], 0.5, None, ALU.mult)
            for j in range(VPARTS):
                dve.memset(v_part[j][:, :, :, :, :], 0.0).then_inc(v_masked, 1)
            dve.memset(vbd[:, :, :, :, :], 0.0)
            dve.wait_ge(v_masked, 1)
            for c in range(RC):
                dve.tensor_copy(v_part[0][:, c, :, :, DK], head_of_row[:, c, FIRST_HEAD[c]:FIRST_HEAD[c] + WINDOW]
                                .unsqueeze(1).to_broadcast([P, 2, WINDOW]))
            dve.wait_ge(setup_dve, 7)
            dve.scalar_tensor_tensor(bias_rows[:, :, :], row_hi[:, :, :].bitcast(F32), not_first[:, 0:1],
                                     row_f[:, :, :], ALU.mult, ALU.add).then_inc(setup_dve, 1)
            def attn_weights(l):
                dve.wait_ge(setup_act, 3 + l)
                dve.tensor_tensor(wat_lo[l][:, :], w_raw[l][:, :], wat_hi[l][:, :].bitcast(F32), ALU.subtract)\
                    .then_inc(setup_dve, 1)

            def sign_weights():
                dve.wait_ge(bits_loaded, 3 * 16)
                dve.tensor_tensor(w0[:, :, :], k0_raw[:, 0:KC, :], k0_raw[:, KC:2 * KC, :], ALU.subtract)\
                    .then_inc(setup_dve, 1)
                dve.tensor_scalar(w2[:, :, :], k2_raw[:, :, :], 2.0, -1.0, ALU.mult, ALU.add).then_inc(setup_dve, 1)
                dve.wait_ge(setup_dve, 11)
                dve.tensor_scalar(w0[:, :, :], w0[:, :, :].bitcast(F32), sgn[:, 6:7], None, ALU.mult)\
                    .then_inc(setup_dve, 1)

            def ln_stats(l, i, t):
                tile = t * NT + i
                if l == "A":
                    dve.wait_ge(x_loaded[i], t * 16 + 16)
                elif l in "BC":
                    for n in range(2):
                        wait_drained(dve, ("wo", "A", i, n) if l == "B" else ("y", i, n), t)
                dve.memset(nothing[:, :], 0.0)
                for s in range(SUB):
                    ins = dve.bn_stats(stats[i][:, s, :], x_sb[:, tile, s, :])
                ins.then_inc(stats_ready, 1)
                dve.wait_ge(stats_ready, ln_count(l, i, t))
                dve.memset(nothing[:, :], 0.0)
                for s in range(SUB):
                    ins = dve.bn_aggr(moments[i][:, s, :], stats[i][:, s, :])
                ins.then_inc(moments_ready, 1)

            def ln_apply(l, i, t):
                tile = t * NT + i
                dve.wait_ge(moments_ready, ln_count(l, i, t))
                dve.wait_ge(rstd_ready, ln_count(l, i, t))
                for s in range(SUB):
                    ins = dve.tensor_scalar(token[i][:, s, :], x_sb[:, tile, s, :], moments[i][:, s, 0:1],
                                            rstd[i][:, s:s + 1], ALU.subtract, ALU.mult)
                ins.then_inc(normed_ready, 1)

            def act_lo_of(kind, l, i, t):
                for k in range(KC):
                    name = (kind, l, i, k)
                    wait_hi(dve, name, t)
                    dve.tensor_tensor(act_lo[i][:, k, :], bank(name), act_hi[i][:, k, :].bitcast(F32), ALU.subtract)\
                        .then_inc(bank_drained[jobs[name].bank], 1)

            def q_lo_of(l, i, t):
                for m in range(KC):
                    name = ("q", l, i, m)
                    wait_hi(dve, name, t)
                    if l == "A":
                        ins = dve.scalar_tensor_tensor(q_lo[i][:, m, :], bank(name), bqk[:, 0, m:m + 1],
                                                       q_hi[i][:, m, :].bitcast(F32), ALU.add, ALU.subtract)
                    else:
                        ins = dve.tensor_tensor(q_lo[i][:, m, :], bank(name), q_hi[i][:, m, :].bitcast(F32), ALU.subtract)
                    ins.then_inc(bank_drained[jobs[name].bank], 1)

            def rep_lo_of(l, t):
                dve.wait_ge(rep_hi_ready, t * 2 + (LAYER[l] + 1))
                dve.tensor_tensor(rep_lo[:, :, :], ctx_sb[:, t, :].unsqueeze(1).to_broadcast([IMG, HH, KEYS]),
                                  rep_hi[:, :, :].bitcast(F32), ALU.subtract).then_inc(rep_lo_ready, 1)

            def key_parts(l, t):
                n = 2 * LAYER[l]
                wait_drained(dve, ("k", l), t)
                dve.wait_ge(kbd_lo_ready, t * 2 + (1 + LAYER[l]))
                dve.tensor_copy(k_hi[:, :, :], k_f[:, :, :]).then_inc(k_parts_ready, 1)
                dve.wait_ge(k_parts_ready, t * 4 + (1 + n + 1))
                dve.tensor_tensor(k_lo[:, :, :], k_f[:, :, :], k_hi[:, :, :].bitcast(F32), ALU.subtract)\
                    .then_inc(k_parts_ready, 1)

            def block_keys(l, t):
                for m in range(KC):
                    ins = dve.tensor_tensor(kbd_hi[l][:, m, :].rearrange("p (h k) -> p h k", h=HH),
                                            k_hi[:, m, :].bitcast(F32).unsqueeze(1).to_broadcast([P, HH, KEYS]),
                                            head_of_feature[:, :].unsqueeze(2).to_broadcast([P, HH, KEYS]), ALU.mult)
                ins.then_inc(kbd_hi_ready, 1)

            def block_values(l, t, j):
                name = ("v", l, j)
                wait_filled(dve, name, t)
                for c in range(2 * j, min(2 * j + 2, RC)):
                    rows, o, h0 = ROW_N[c], (c % 2) * D, FIRST_HEAD[c]
                    ins = dve.tensor_tensor(
                        vbd[0:rows, c, :, :, :],
                        bank(name)[0:rows, o:o + D].rearrange("p (g h d) -> p g h d", g=2, h=HH)[:, :, h0:h0 + WINDOW, :],
                        head_of_row[0:rows, c, h0:h0 + WINDOW].unsqueeze(1).unsqueeze(3)
                        .to_broadcast([rows, 2, WINDOW, DK]), ALU.mult)
                ins.then_inc(bank_drained[jobs[name].bank], 1)

            def value_parts(l, t):
                for j in range(3):
                    wait_drained(dve, ("v", l, j), t)
                if l == "C":
                    wait_filled(dve, ("pv", "A", 1, SUB - 1), t)
                v, n = vbd[:, :, :, :, :].rearrange("p c g h d -> p (c g h) d"), t * 6 + 3 * LAYER[l] + VPARTS
                part = [v_part[j][:, :, :, :, 0:DK].rearrange("p c g h d -> p (c g h) d") for j in range(VPARTS)]
                dve.tensor_copy(part[0], v).then_inc(v_masked, 1)
                dve.wait_ge(v_masked, n + 1)
                dve.tensor_tensor(v, v, part[0], ALU.subtract).then_inc(v_masked, 1)
                dve.wait_ge(v_masked, n + 2)
                dve.tensor_copy(part[1], v).then_inc(v_masked, 1)
                dve.wait_ge(v_masked, n + 3)
                dve.tensor_tensor(part[2], v, part[1], ALU.subtract).then_inc(v_parts_ready, 1)

            def p_lo_of(l, i, t, n):
                rows = ROW_N[n % RC]
                wait_drained(dve, ("st", l, i, n), t)
                dve.tensor_tensor(p_lo[0:rows, n, :], p_f[0:rows, n % P_RING, :], p_hi[0:rows, n, :],
                                  ALU.subtract).then_inc(p_lo_dve, 1)

            def maxima(l, i, t, n0=0, n1=16):
                for n in range(n0, n1):
                    s, q = n // 4, n % 4
                    name = ("mx", l, i, n)
                    wait_filled(dve, name, t)
                    ins = dve.tensor_reduce(neg_max[i][:, s, MXH * q:MXH * q + MXH],
                                            bank(name)[:, 0:MXH * KEYS].rearrange("p (h k) -> p h k", h=MXH),
                                            AX.X, ALU.max, negate=True)
                    ins.then_inc(bank_drained[jobs[name].bank], 1)

            def heads(l, i, t, s0=0, s1=SUB):
                for s in range(s0, s1):
                    name = ("pv", l, i, s)
                    wait_filled(dve, name, t)
                    pv = bank(name)[:, 0:HEADS * VW].rearrange("p (h d) -> p h d", h=HEADS)
                    dve.reciprocal(inv_sum[:, s, :], pv[:, :, DK]).then_inc(inv_sum_ready, 1)
                    dve.wait_ge(inv_sum_ready, attn_count(l, i, t, SUB) - (SUB - 1 - s))
                    ins = dve.tensor_tensor(token[i][:, s, :].rearrange("p (h d) -> p h d", h=HEADS), pv[:, :, 0:DK],
                                            inv_sum[:, s, :].unsqueeze(2).to_broadcast([P, HEADS, DK]), ALU.mult)
                    ins.then_inc(bank_drained[jobs[name].bank], 1)

            def residual(l, i, t):
                gain = {"A": gates[:, 0:1], "B": gain_b[:, 0:1], "C": gates[:, 1:2]}[l]
                for n in range(2):
                    name = ("y", i, n) if l == "B" else ("wo", l, i, n)
                    wait_filled(dve, name, t)
                    part = x_sb[:, t * NT + i, 2 * n:2 * n + 2, :].rearrange("p s d -> p (s d)")
                    dve.scalar_tensor_tensor(part, bank(name), gain, part, ALU.mult, ALU.add)\
                        .then_inc(bank_drained[jobs[name].bank], 1)

            def hidden(kind, i, t, ms):
                for m in ms:
                    name = (kind, i, m)
                    hi, lo = (h1_hi, h1_lo) if kind == "h1" else (h2_hi, h2_lo)
                    at = m if kind == "h1" else m % H2RING
                    wait_hi(dve, name, t)
                    dve.scalar_tensor_tensor(lo[:, at, :], bank(name), 0.0, hi[:, at, :].bitcast(F32),
                                             ALU.max, ALU.subtract).then_inc(bank_drained[jobs[name].bank], 1)

            def image(t, last):
                after, ta = ("D", 0) if last else ("A", t + 1)
                act_lo_of("ln", "A", 1, t)
                q_lo_of("A", 1, t)
                for n in range(2, 2 * RC):
                    maxima("A", 1, t, n - 2, n - 1)
                    if n - 1 in LO_DVE:
                        p_lo_of("A", 0, t, n - 1)
                    if n == 3:
                        value_parts("A", t)
                p_lo_of("A", 0, t, 9)
                maxima("A", 1, t, 8, 11)
                heads("A", 0, t, 0, 1)
                maxima("A", 1, t, 11, 14)
                heads("A", 0, t, 1, 2)
                maxima("A", 1, t, 14, 16)
                heads("A", 0, t, 2, 4)
                act_lo_of("ot", "A", 0, t)
                p_lo_of("A", 1, t, 4)
                residual("A", 0, t)
                ln_stats("B", 0, t)
                p_lo_of("A", 1, t, 9)
                ln_apply("B", 0, t)
                heads("A", 1, t)
                act_lo_of("ln", "B", 0, t)
                act_lo_of("ot", "A", 1, t)
                rep_lo_of("C", t)
                hidden("h1", 0, t, range(6))
                key_parts("C", t)
                block_keys("C", t)
                block_values("C", t, 0)
                hidden("h1", 0, t, range(6, HC))
                for j in range(1, 3):
                    block_values("C", t, j)
                residual("A", 1, t)
                ln_stats("B", 1, t)
                hidden("h2", 0, t, range(1))
                value_parts("C", t)
                ln_apply("B", 1, t)
                hidden("h2", 0, t, range(1, 4))
                act_lo_of("ln", "B", 1, t)
                hidden("h2", 0, t, range(4, HC))
                hidden("h1", 1, t, range(HC))
                residual("B", 0, t)
                ln_stats("C", 0, t)
                hidden("h2", 1, t, range(1))
                ln_apply("C", 0, t)
                hidden("h2", 1, t, range(1, 4))
                act_lo_of("ln", "C", 0, t)
                hidden("h2", 1, t, range(4, 5))
                q_lo_of("C", 0, t)
                for m in range(5, HC):
                    maxima("C", 0, t, 5 * (m - 5), 5 * (m - 4))
                    if m == HC - 1:
                        maxima("C", 0, t, 15, 16)
                    hidden("h2", 1, t, range(m, m + 1))
                residual("B", 1, t)
                ln_stats("C", 1, t)
                ln_apply("C", 1, t)
                p_lo_of("C", 0, t, 4)
                act_lo_of("ln", "C", 1, t)
                q_lo_of("C", 1, t)
                p_lo_of("C", 0, t, 9)
                for s in range(3):
                    heads("C", 0, t, s, s + 1)
                    maxima("C", 1, t, 3 * s, 3 * s + 3)
                heads("C", 0, t, 3, 4)
                maxima("C", 1, t, 9, 12)
                act_lo_of("ot", "C", 0, t)
                maxima("C", 1, t, 12, 16)
                residual("C", 0, t)
                if not last:
                    rep_lo_of("A", ta)
                ln_stats(after, 0, ta)
                if not last:
                    key_parts("A", ta)
                    block_values("A", ta, 0)
                ln_apply(after, 0, ta)
                if not last:
                    block_keys("A", ta)
                    block_values("A", ta, 1)
                p_lo_of("C", 1, t, 4)
                if last:
                    p_lo_of("C", 1, t, 9)
                    ln_stats(after, 1, ta)
                    heads("C", 1, t)
                    act_lo_of("ot", "C", 1, t)
                    ln_apply(after, 1, ta)
                    residual("C", 1, t)
                else:
                    block_values("A", ta, 2)
                    act_lo_of("ln", "A", 0, ta)
                    ln_stats("A", 1, ta)
                    q_lo_of("A", 0, ta)
                    p_lo_of("C", 1, t, 9)
                    maxima("A", 0, ta, 0, 2)
                    for s in range(SUB):
                        maxima("A", 0, ta, 2 + 3 * s, 5 + 3 * s)
                        heads("C", 1, t, s, s + 1)
                    maxima("A", 0, ta, 14, 16)
                    act_lo_of("ot", "C", 1, t)
                    ln_apply("A", 1, ta)
                    residual("C", 1, t)

            ln_stats("A", 0, 0)
            attn_weights(0)
            rep_lo_of("A", 0)
            ln_apply("A", 0, 0)
            key_parts("A", 0)
            block_keys("A", 0)
            for j in range(3):
                block_values("A", 0, j)
            act_lo_of("ln", "A", 0, 0)
            ln_stats("A", 1, 0)
            q_lo_of("A", 0, 0)
            ln_apply("A", 1, 0)
            maxima("A", 0, 0)
            attn_weights(1)
            sign_weights()
            with dve.Fori(0, T - 1) as t:
                image(t, False)
            image(T - 1, True)

            def first_c(i):
                dve.tensor_copy(c_f[i][:, :, :], c0_col[:, :].unsqueeze(2).to_broadcast([P, KC, TILE])).then_inc(c_lo_ready, 1)
                dve.tensor_copy(c_hi[i][:, :, :], c0_col[:, :].unsqueeze(2).to_broadcast([P, KC, TILE])).then_inc(c_lo_ready, 1)
                dve.wait_ge(c_lo_ready, 3 * i + 2)
                dve.tensor_tensor(c_lo[i][:, :, :], c_f[i][:, :, :], c_hi[i][:, :, :].bitcast(F32), ALU.subtract)\
                    .then_inc(c_lo_ready, 1)

            def cell(i, t):
                for m in range(KC):
                    for g in range(3):
                        wait_drained(dve, ("gate", i, g, m), t)
                dve.wait_ge(c_f_ready, t * NT + 1)
                dve.scalar_tensor_tensor(gate[i][0][:, :, :], gate[i][0][:, :, :], 1.0, c_f[i][:, :, :],
                                         ALU.add, ALU.mult).then_inc(fc_ready, 1)
                dve.scalar_tensor_tensor(gate[i][1][:, :, :], gate[i][1][:, :, :], 1.0, gate[i][2][:, :, :],
                                         ALU.add, ALU.mult).then_inc(ig_ready, 1)
                dve.wait_ge(fc_ready, t * NT + (i + 1))
                dve.wait_ge(ig_ready, t * NT + (i + 1))
                dve.tensor_tensor(gate[i][0][:, :, :], gate[i][0][:, :, :], gate[i][1][:, :, :], ALU.add)\
                    .then_inc(c2_ready, 1)

            def cell_lo(i, t):
                dve.wait_ge(c2_ready, t * NT + (i + 1))
                dve.wait_ge(c_hi_ready, t * NT + (i + 1))
                dve.scalar_tensor_tensor(c_lo[i][:, :, :], gate[i][0][:, :, :], 0.5, c_hi[i][:, :, :].bitcast(F32),
                                         ALU.mult, ALU.subtract).then_inc(c_lo_ready, 1)

            def read_out_sum(i, t):
                if t % 2 == 1:
                    for n in range(2):
                        wait_drained(dve, ("co", i, n), 0)
                    tile = xo_sb[:, t * NT + i, :, :]
                    dve.tensor_tensor(tile, tile, co_sb[i][:, :, :], ALU.add).then_inc(pre_ready[1], 1)

            def finish(i, t):
                dve.wait_ge(h_ready, i * T + t + 1)
                tile = x_sb[:, t * NT + i, :, :].rearrange("p s d -> p (s d)")
                dve.scalar_tensor_tensor(tile, xo_sb[:, t * NT + i, :, :].rearrange("p s d -> p (s d)"),
                                         gates[:, 3:4], tile, ALU.mult, ALU.add).then_inc(out_ready, 1)

            def step(t, last):
                if not last:
                    ln_stats("D", 0, t + 1)
                act_lo_of("ln", "D", 1, t)
                if not last:
                    ln_apply("D", 0, t + 1)
                    ln_stats("D", 1, t + 1)
                cell(0, t)
                if not last:
                    ln_apply("D", 1, t + 1)
                cell_lo(0, t)
                if last:
                    for q in range(T):
                        read_out_sum(0, q)
                else:
                    act_lo_of("ln", "D", 0, t + 1)
                cell(1, t)
                cell_lo(1, t)

            act_lo_of("ln", "D", 0, 0)
            for n in range(2):
                wait_drained(dve, ("wo", "C", 1, n), T - 1)
            for i in range(NT):
                first_c(i)
            with dve.Fori(0, T - 1) as t:
                step(t, False)
            step(T - 1, True)
            for i in range(NT):
                if i == 1:
                    for t in range(T):
                        read_out_sum(1, t)
                for t in range(T):
                    finish(i, t)

        @block.tensor
        def _(pe):
            def begin(name, t):
                wait_free(pe, name, t)

            def done(ins, name):
                ins.then_inc(bank_filled[jobs[name].bank], 1)

            def terms(dst, lefts, rights, start=True, stop=True):
                n = len(lefts)
                for k, ((lh, ll), (rh, rl)) in enumerate(zip(lefts, rights)):
                    pe.matmul(dst, lh, rh, start=start and k == 0, stop=False, skip_group_check=True)
                    pe.matmul(dst, lh, rl, start=False, stop=False, skip_group_check=True)
                    ins = pe.matmul(dst, ll, rh, start=False, stop=stop and k == n - 1, skip_group_check=True)
                return ins

            def wat(l, at, n, m0=0, m=D):
                j = LAYER[l]
                return [(wat_hi[j][:, at + k * D + m0:at + k * D + m0 + m],
                         wat_lo[j][:, at + k * D + m0:at + k * D + m0 + m]) for k in range(n)]

            def rep(c0, n):
                hi = rep_hi[:, :, :].rearrange("p h k -> p (h k)")
                lo = rep_lo[:, :, :].rearrange("p h k -> p (h k)")
                return hi[:, c0:c0 + n], lo[:, c0:c0 + n]

            def keys(l, t):
                pe.wait_ge(rep_lo_ready, t * 2 + (LAYER[l] + 1))
                begin(("k", l), t)
                pk = bank(("k", l))
                for m in range(KC):
                    ins = terms(pk[:, m * KP:m * KP + KP], wat(l, WK, 1, m * P, P), [rep(0, KP)], start=m == 0)
                done(ins, ("k", l))

            def new_values(l, t, j):
                name = ("v", l, j)
                begin(name, t)
                for c in range(2 * j, min(2 * j + 2, RC)):
                    rows = ROW_N[c]
                    dst = bank(name)[0:rows, (c % 2) * D:(c % 2) * D + D]
                    first = c % 2 == 0
                    ins = terms(dst, [rep(c * P, rows)], wat(l, WV, 1), start=first, stop=l == "C")
                    if l == "A":
                        ins = pe.matmul(dst, ones_row[0:2, 0:rows], bias_rows[0:2, 0, :], start=False, stop=True,
                                        skip_group_check=True)
                done(ins, name)

            def transposes(kind, l, i, t):
                if kind == "ln":
                    pe.wait_ge(normed_ready, ln_count(l, i, t))
                else:
                    wait_drained(pe, ("pv", l, i, SUB - 1), t)
                for k in range(KC):
                    name = (kind, l, i, k)
                    begin(name, t)
                    for s in range(SUB):
                        ins = pe.transpose(bank(name)[:, s * P:s * P + P], token[i][:, s, k * P:k * P + P], ident[:, :])
                    done(ins, name)

            def wait_act(kind, l, i, t):
                for k in range(KC):
                    wait_drained(pe, (kind, l, i, k), t)

            def query(l, i, t):
                wait_act("ln", l, i, t)
                for m in range(KC):
                    name = ("q", l, i, m)
                    begin(name, t)
                    done(terms(bank(name), wat(l, WQ, KC, m * P, P),
                               [(act_hi[i][:, k, :], act_lo[i][:, k, :]) for k in range(KC)]), name)

            def maxima(l, i, t, n0=0, n1=16):
                if n0 == 0:
                    for m in range(KC):
                        wait_drained(pe, ("q", l, i, m), t)
                    pe.wait_ge(kbd_hi_ready, t * 2 + (LAYER[l] + 1))
                for n in range(n0, n1):
                    s, q = n // 4, n % 4
                    name = ("mx", l, i, n)
                    begin(name, t)
                    at = (q % 2) * MXH * KEYS
                    done(pe.matmul(bank(name)[:, 0:MXH * KEYS], q_hi[i][:, q // 2, s * P:s * P + P],
                                   kbd_hi[l][:, q // 2, at:at + MXH * KEYS], start=True, stop=True), name)

            def neg_max_rows(l, i, t):
                wait_drained(pe, ("mx", l, i, 15), t)
                name = ("mt", l, i)
                begin(name, t)
                for s in range(SUB):
                    ins = pe.transpose(bank(name)[0:HEADS, s * P:s * P + P], neg_max[i][:, s, :], ident[:, :])
                done(ins, name)

            def scores(l, i, t, n0=0, n1=2 * RC):
                if n0 == 0:
                    wait_drained(pe, ("mt", l, i), t)
                    pe.wait_ge(kbd_lo_ready, t * 2 + (1 + LAYER[l] + 1))
                for n in range(n0, n1):
                    name = ("st", l, i, n)
                    half, c = n // RC, n % RC
                    rows = ROW_N[c]
                    begin(name, t)
                    dst = bank(name)[0:rows, :]
                    pe.matmul(dst, row_heads[:, half, c * P:c * P + rows], neg_max_t[:, :], start=True, stop=False,
                              skip_group_check=True)
                    done(terms(dst, [(kbd_hi[l][:, half, c * P:c * P + rows], kbd_lo[:, half, c * P:c * P + rows])],
                               [(q_hi[i][:, half, :], q_lo[i][:, half, :])], start=False), name)

            def values(l, i, t, s0=0, s1=SUB, beside={}):
                if s0 == 0:
                    pe.wait_ge(v_parts_ready, t * 2 + (LAYER[l] + 1))
                for s in range(s0, s1):
                    name = ("pv", l, i, s)
                    begin(name, t)
                    for n in range(2 * RC):
                        if s == 0:
                            wait_p_lo(pe, l, i, n, t)
                        half, c = n // RC, n % RC
                        rows, at = ROW_N[c], (half * HH + FIRST_HEAD[c]) * VW
                        dst = bank(name)[:, at:at + WINDOW * VW]
                        for p, j in ((p_hi, 0), (p_hi, 1), (p_hi, 2), (p_lo, 0), (p_lo, 1)):
                            ins = pe.matmul(dst, p[0:rows, n, s * P:s * P + P],
                                            v_part[j][0:rows, c, half, :, :].rearrange("p h d -> p (h d)"),
                                            start=n == 0 and j == 0 and p is p_hi, stop=n == 2 * RC - 1,
                                            skip_group_check=True)
                        if n == 2 * RC - 1:
                            done(ins, name)
                        if n in beside:
                            maxima(*beside[n])

            def by_token(name, t, lefts, weight, start_hi, bias=None):
                for j in range(2):
                    s = 2 * name[-1] + j
                    dst = bank(name)[:, j * D:j * D + D]
                    ins = terms(dst, [(lh[:, k, s * P:s * P + P], ll[:, k, s * P:s * P + P]) for lh, ll in [lefts]
                                      for k in range(KC)], weight, start=start_hi and j == 0, stop=bias is None)
                    if bias is not None:
                        ins = pe.matmul(dst, ones_row[0:2, :], bias_rows[0:2, bias, :], start=False, stop=True,
                                        skip_group_check=True)
                return ins

            def project(l, i, t, n0=0, n1=2):
                wait_act("ot", l, i, t)
                for n in range(n0, n1):
                    name = ("wo", l, i, n)
                    begin(name, t)
                    done(by_token(name, t, (act_hi[i], act_lo[i]), wat(l, WO, KC), True, 1 if l == "A" else None), name)

            def hidden1(i, t, ms):
                for m in ms:
                    name = ("h1", i, m)
                    if m == 0:
                        wait_act("ln", "B", i, t)
                    begin(name, t)
                    for k in range(KC):
                        w = w0[:, k, m * P:m * P + P]
                        pe.matmul(bank(name), w, act_hi[i][:, k, :], start=k == 0, stop=False)
                        ins = pe.matmul(bank(name), w, act_lo[i][:, k, :], start=False, stop=k == KC - 1)
                    done(ins, name)

            def hidden2(i, t, m, beside=None):
                name = ("h2", i, m)
                begin(name, t)
                for k in range(HC):
                    if m == 0:
                        wait_drained(pe, ("h1", i, k), t)
                    w = w1[:, k, m * P:m * P + P]
                    pe.matmul(bank(name), w, h1_hi[:, k, :], start=k == 0, stop=False)
                    ins = pe.matmul(bank(name), w, h1_lo[:, k, :], start=False, stop=k == HC - 1)
                    if k == HC - 1:
                        done(ins, name)
                    if beside is not None:
                        beside(k)

            def third(i, t, m):
                wait_drained(pe, ("h2", i, m), t)
                if m == 0:
                    begin(("y", i, 0), t)
                    begin(("y", i, 1), t)
                at = m % H2RING
                for s in range(SUB):
                    name = ("y", i, s // 2)
                    dst = bank(name)[:, (s % 2) * D:(s % 2) * D + D]
                    pe.matmul(dst, h2_hi[:, at, s * P:s * P + P], w2[:, m, :], start=m == 0 and s % 2 == 0, stop=False,
                              skip_group_check=True)
                    ins = pe.matmul(dst, h2_lo[:, at, s * P:s * P + P], w2[:, m, :], start=False, stop=m == HC - 1,
                                    skip_group_check=True)
                    if m == HC - 1 and s % 2 == 1:
                        done(ins, name)

            def maxima_beside(t, m):
                def beside(k):
                    if k in (1, 2, 4, 5, 7):
                        n = 5 * (m - 5) + (1, 2, 4, 5, 7).index(k)
                        maxima("C", 0, t, n, n + 1)
                return beside

            def three(l, i, t, n):
                return {at: (l, i, t, n + j, n + j + 1) for j, at in enumerate((2, 5, 8))}

            def image(t, last):
                transposes("ln", "A", 1, t)
                query("A", 1, t)
                for n in range(2, 2 * RC):
                    scores("A", 0, t, n, n + 1)
                    maxima("A", 1, t, n - 2, n - 1)
                values("A", 0, t, 0, 1, three("A", 1, t, 8))
                values("A", 0, t, 1, 2, three("A", 1, t, 11))
                values("A", 0, t, 2, 3, {2: ("A", 1, t, 14, 15), 5: ("A", 1, t, 15, 16)})
                neg_max_rows("A", 1, t)
                values("A", 0, t, 3, 4)
                scores("A", 1, t, 0, 3)
                transposes("ot", "A", 0, t)
                scores("A", 1, t, 3, 6)
                project("A", 0, t)
                scores("A", 1, t, 6)
                values("A", 1, t)
                transposes("ln", "B", 0, t)
                transposes("ot", "A", 1, t)
                pe.wait_ge(setup_dve, 13)
                pe.wait_ge(setup_act, 6)
                hidden1(0, t, range(6))
                keys("C", t)
                new_values("C", t, 0)
                hidden1(0, t, range(6, HC))
                for j in range(1, 3):
                    new_values("C", t, j)
                project("A", 1, t)
                for m in range(HC):
                    hidden2(0, t, m)
                    if m >= 1:
                        third(0, t, m - 1)
                    if m == 3:
                        transposes("ln", "B", 1, t)
                hidden1(1, t, range(HC))
                third(0, t, HC - 1)
                for m in range(HC):
                    hidden2(1, t, m, maxima_beside(t, m) if m >= 5 else None)
                    if m == HC - 1:
                        maxima("C", 0, t, 15, 16)
                    if m >= 1:
                        third(1, t, m - 1)
                    if m == 3:
                        transposes("ln", "C", 0, t)
                    if m == 4:
                        query("C", 0, t)
                neg_max_rows("C", 0, t)
                third(1, t, HC - 1)
                scores("C", 0, t, 0, 7)
                transposes("ln", "C", 1, t)
                scores("C", 0, t, 7)
                query("C", 1, t)
                values("C", 0, t, 0, 1)
                for s in range(1, SUB):
                    values("C", 0, t, s, s + 1, three("C", 1, t, 3 * s - 3))
                maxima("C", 1, t, 9, 12)
                transposes("ot", "C", 0, t)
                maxima("C", 1, t, 12, 16)
                project("C", 0, t)
                neg_max_rows("C", 1, t)
                if last:
                    scores("C", 1, t)
                    values("C", 1, t)
                    transposes("ot", "C", 1, t)
                    project("C", 1, t)
                else:
                    keys("A", t + 1)
                    new_values("A", t + 1, 0)
                    scores("C", 1, t, 0, 3)
                    new_values("A", t + 1, 1)
                    scores("C", 1, t, 3, 5)
                    new_values("A", t + 1, 2)
                    scores("C", 1, t, 5, 6)
                    transposes("ln", "A", 0, t + 1)
                    scores("C", 1, t, 6, 8)
                    query("A", 0, t + 1)
                    scores("C", 1, t, 8, 9)
                    maxima("A", 0, t + 1, 0, 1)
                    scores("C", 1, t, 9, 10)
                    maxima("A", 0, t + 1, 1, 2)
                    for s in range(SUB):
                        values("C", 1, t, s, s + 1, three("A", 0, t + 1, 2 + 3 * s))
                    maxima("A", 0, t + 1, 14, 16)
                    neg_max_rows("A", 0, t + 1)
                    transposes("ot", "C", 1, t)
                    scores("A", 0, t + 1, 0, 2)
                    project("C", 1, t)

            pe.wait_ge(setup_dve, 9)
            pe.wait_ge(setup_act, 3)
            keys("A", 0)
            for j in range(3):
                new_values("A", 0, j)
            transposes("ln", "A", 0, 0)
            query("A", 0, 0)
            maxima("A", 0, 0)
            neg_max_rows("A", 0, 0)
            scores("A", 0, 0, 0, 2)
            with pe.Fori(0, T - 1) as t:
                image(t, False)
            image(T - 1, True)

            def wd(n, m0=0, m=D):
                return [(wd_hi[:, n, k, m0:m0 + m], wd_lo[:, n, k, m0:m0 + m]) for k in range(KC)]

            def x_out(i, t):
                wait_act("ln", "D", i, t)
                for n in range(2):
                    name = ("xo", i, n)
                    begin(name, t)
                    done(by_token(name, t, (act_hi[i], act_lo[i]), wd(XO), True, 2), name)

            def gates_of(i, t, m):
                for g in range(3):
                    name = ("gate", i, g, m)
                    begin(name, t)
                    terms(bank(name), wd(1 + g, m * P, P),
                          [(act_hi[i][:, k, :], act_lo[i][:, k, :]) for k in range(KC)], stop=False)
                    if m == 0 and g == 0:
                        pe.wait_ge(wd_lo_ready, 2)
                        pe.wait_ge(c_lo_ready, c_count(i, t))
                    done(terms(bank(name), wd(4 + g, m * P, P),
                               [(c_hi[i][:, k, :], c_lo[i][:, k, :]) for k in range(KC)], start=False), name)

            def c_out(i):
                pe.wait_ge(c_lo_ready, c_count(i, T))
                for n in range(2):
                    name = ("co", i, n)
                    begin(name, 0)
                    done(by_token(name, 0, (c_hi[i], c_lo[i]), wd(CO), True), name)

            def step(t, last):
                x_out(0, t)
                gates_of(0, t, 0)
                transposes("ln", "D", 1, t)
                gates_of(0, t, 1)
                x_out(1, t)
                gates_of(1, t, 0)
                if last:
                    c_out(0)
                else:
                    transposes("ln", "D", 0, t + 1)
                gates_of(1, t, 1)

            transposes("ln", "D", 0, 0)
            pe.wait_ge(wd_lo_ready, 1)
            with pe.Fori(0, T - 1) as t:
                step(t, False)
            step(T - 1, True)
            c_out(1)


def kernel(**inputs):
    import concourse.bacc as bacc
    from concourse.bass_utils import run_bass_kernel_spmd

    v = {k: np.asarray(x) for k, x in inputs.items()}
    wkv = v["L1_xattn_Wkv"]
    row = np.arange(RC * P).reshape(RC, P)
    heads = np.arange(HH)
    arrays = {
        "x": v["x"].reshape(T * NT, P, SUB, D),
        "ctx_t": v["ctx_512"].transpose(0, 2, 1),
        "wq0": v["L0_xattn_Wq"], "wk0": v["L0_xattn_Wk"], "wv0": v["L0_xattn_Wv"], "wo0": v["L0_xattn_Wo"],
        "wq1": v["L1_xattn_Wq"].T, "wk1": wkv[:D].T, "wv1": wkv[D:].T, "wo1": v["L1_xattn_Wo"].T,
        "cols": np.stack([v[n].reshape(KC, P).T for n in ("L0_xattn_bq", "L0_xattn_bk", "L1_ffn_bf", "L1_ffn_bi",
                                                          "L1_ffn_bc", "L1_ffn_in_c")], 1),
        "rows": np.stack([v["L0_xattn_bv"], v["L0_xattn_bo"], v["L1_ffn_bo"]]),
        "g": np.concatenate([v["g_xattn"], v["g_ffn"]]),
        "s": np.stack([v["L0_ffn_s0"], v["L0_ffn_s1"], v["L0_ffn_s2"]]),
        "k0": v["L0_ffn_k0"], "k1": v["L0_ffn_k1"], "k2": v["L0_ffn_k2"],
        "wf": v["L1_ffn_wf"].T, "wi": v["L1_ffn_wi"].T, "wc": v["L1_ffn_wc"].T, "wo_d": v["L1_ffn_wo"].T,
        "uf": v["L1_ffn_uf"].T, "ui": v["L1_ffn_ui"].T, "uc": v["L1_ffn_uc"].T, "uo_d": v["L1_ffn_uo"].T,
        "ident": np.eye(P, dtype=np.float32),
        "not_first": np.array([[0.0], [-1.0]], np.float32),
        "head_of_feature": (np.arange(P)[:, None] // DK == heads).astype(np.float32),
        "head_of_row": (row.T[:, :, None] // KEYS == heads).astype(np.float32),
        "row_heads": (np.arange(2 * ROWS).reshape(2, ROWS) // KEYS == np.arange(HEADS)[:, None, None]).astype(np.float32),
    }
    arrays = {k: np.ascontiguousarray(x) for k, x in arrays.items()}
    nc = bacc.Bacc("TRN2", target_bir_lowering=False, num_devices=1)
    aps = {k: nc.dram_tensor(f"in_{k}", x.shape, mybir.dt.from_np(x.dtype), kind="ExternalInput").ap()
           for k, x in arrays.items()}
    out = nc.dram_tensor("out_x", (T * NT, P, SUB, D), F32, kind="ExternalOutput").ap()
    build(nc, aps, out)
    r = run_bass_kernel_spmd(nc, [{f"in_{k}": x for k, x in arrays.items()}], core_ids=[0])
    return r.results[0]["out_x"].reshape(T, B, D)
```

```python
import numpy as np
import concourse.bass as bass
from concourse import mybir
from concourse.alu_op_type import AluOpType as ALU
from contextlib import ExitStack

F32 = mybir.dt.float32
F32R = mybir.dt.float32r
U8 = mybir.dt.uint8
F16 = mybir.dt.float16
BF16 = mybir.dt.bfloat16
ACT = mybir.ActivationFunctionType
AX = mybir.AxisListType

T, B, D = 4, 1024, 256
P = 128
KC = D // P
TILE = 512
SUB = TILE // P
NT = B // TILE
HEADS, DK, KEYS, IMG = 16, 16, 77, 128
HH = HEADS // 2
ROWS = HH * KEYS
RC = -(-ROWS // P)
ROW_N = [min(P, ROWS - c * P) for c in range(RC)]
KP = KEYS + 1
MXH = 4
VW = DK + 1
WINDOW = 3
FIRST_HEAD = [min(c * P // KEYS, HH - WINDOW) for c in range(RC)]
VPARTS = 3
P_RING = 3
CUT_BY_DVE = {("A", 0): (4, 9), ("A", 1): (1, 3, 5, 7, 9), ("C", 0): (1, 3, 5, 7, 9), ("C", 1): (4, 9)}
HID = 1024
HC = HID // P
H2RING = 2
EPS = 1e-5
KSCALE = float(DK) ** -0.5

GENERAL, OUTS, WIDE = (0, 1, 2), (3, 4), (5, 6, 7)
BOTH = OUTS + WIDE
READ, GATES, NORMED = (0, 1), (2, 3, 4, 5), (6, 7)
LAYER_NORMS = [("A", 0), ("A", 1), ("B", 0), ("B", 1), ("C", 0), ("C", 1)]


HI_KINDS = ("ln", "q", "ot", "h1", "h2")


class Job:
    def __init__(self, bank, nth, hi_nth):
        self.bank, self.nth, self.per, self.hi_nth, self.hi_per = bank, nth, 0, hi_nth, 0

    def count(self, t):
        return t * self.per + self.nth

    def hi_count(self, t):
        return t * self.hi_per + self.hi_nth


def number_jobs(order, base, hi_base):
    jobs, used, his, turn = {}, [0] * 8, [0] * 8, {}
    for name, ring in order:
        at = turn.get(ring, 0)
        turn[ring] = at + 1
        b = ring[at % len(ring)]
        used[b] += 1
        his[b] += name[0] in HI_KINDS
        jobs[name] = Job(b, base[b] + used[b], hi_base[b] + his[b])
    for job in jobs.values():
        job.per, job.hi_per = used[job.bank], his[job.bank]
    return jobs, used, his


def phase1_order():
    out = []

    def add(ring, *names):
        out.extend((n, ring) for n in names)

    def two(kind, l, i, ring=GENERAL):
        add(ring, (kind, l, i, 0), (kind, l, i, 1))

    def maxima(ring, l, i, a=0, b=16):
        add(ring, *[("mx", l, i, n) for n in range(a, b)])

    def scores(l, i, a=0, b=2 * RC):
        add(WIDE, *[("st", l, i, n) for n in range(a, b)])

    def values(l, i, a=0, b=SUB):
        add(GENERAL, *[("pv", l, i, s) for s in range(a, b)])

    add(OUTS, ("k", "A"), *[("v", "A", c) for c in range(3)])
    two("ln", "A", 0, OUTS), two("q", "A", 0, OUTS)
    maxima(OUTS, "A", 0, 0, 6), maxima(BOTH, "A", 0, 6), add(OUTS, ("mt", "A", 0)), scores("A", 0, 0, 2)
    two("ln", "A", 1), two("q", "A", 1), scores("A", 0, 2)
    maxima(OUTS, "A", 1, 0, 6), maxima(BOTH, "A", 1, 6), values("A", 0, 0, 3)
    add(GENERAL, ("mt", "A", 1)), values("A", 0, 3)
    scores("A", 1)
    two("ot", "A", 0), two("wo", "A", 0), values("A", 1), two("ln", "B", 0)
    add(WIDE, *[("h1", 0, m) for m in range(HC)])
    two("ot", "A", 1), add(GENERAL, ("k", "C"), *[("v", "C", c) for c in range(3)]), two("wo", "A", 1)
    add(WIDE, *[("h2", 0, m) for m in range(HC)], *[("h1", 1, m) for m in range(HC)],
        *[("h2", 1, m) for m in range(HC)])
    add(OUTS, ("y", 0, 0), ("y", 0, 1), ("y", 1, 0), ("y", 1, 1))
    two("ln", "B", 1), two("ln", "C", 0), two("q", "C", 0)
    maxima(GENERAL, "C", 0), add(GENERAL, ("mt", "C", 0))
    scores("C", 0), two("ln", "C", 1), two("q", "C", 1)
    maxima(BOTH, "C", 1), values("C", 0)
    two("ot", "C", 0), add(GENERAL, ("wo", "C", 0, 0), ("mt", "C", 1), ("wo", "C", 0, 1))
    scores("C", 1), values("C", 1), two("ot", "C", 1), two("wo", "C", 1)
    return out


def phase2_order():
    out = [(("ln", "D", i, k), NORMED) for i in range(NT) for k in range(KC)]
    for i in range(NT):
        out += [(("xo", i, n), READ) for n in range(2)]
        out += [(("gate", i, g, m), GATES) for m in range(KC) for g in range(3)]
    return out


def phase3_order():
    return [(("co", i, n), (READ, NORMED)[i]) for i in range(NT) for n in range(2)]


def build(nc, a, out):
    with ExitStack() as ctx:
        def keep(name, shape, dt, scope=ctx):
            return scope.enter_context(nc.sbuf_tensor(name, shape, dt))

        def sem(name):
            return ctx.enter_context(nc.semaphore(name))

        x_sb = keep("x_sb", [P, T * NT, SUB, D], F32)
        ident = keep("ident", [P, P], F32)
        ones_row = keep("ones_row", [2, P], F32R)
        bias_rows = keep("bias_rows", [2, 3, D], F32R)
        not_first = keep("not_first", [2, 1], F32)
        one_f = keep("one_f", [2, P], F32)
        cols = keep("cols", [P, 6, KC], F32)
        bqk, col_b, c0_col = cols[:, 0:2, :], cols[:, 2:5, :], cols[:, 5, :]
        half_b = keep("half_b", [P, 2, KC], F32)
        gates_in = keep("gates_in", [P, 4], F32)
        gates = keep("gates", [P, 4], F32)
        gain_b = keep("gain_b", [P, 1], F32)
        nothing = keep("nothing", [P, NT, 2], F32)
        eps = keep("eps", [P, SUB], F32)
        minus_half = keep("minus_half", [P, SUB], F32)
        scal = keep("scal", [P, 3], F32)
        sgn = keep("sgn", [P, 8], F32)
        token = [keep(f"token{i}", [P, SUB, D], F32) for i in range(NT)]
        act_hi = [keep(f"act_hi{i}", [P, KC, TILE], F32R) for i in range(NT)]
        act_lo = [keep(f"act_lo{i}", [P, KC, TILE], F32R) for i in range(NT)]
        stats = [keep(f"stats{i}", [P, SUB, 6], F32) for i in range(NT)]
        moments = [keep(f"moments{i}", [P, SUB, 2], F32) for i in range(NT)]
        var_eps = [keep(f"var_eps{i}", [P, SUB], F32) for i in range(NT)]
        rstd = [keep(f"rstd{i}", [P, SUB], F32) for i in range(NT)]

        p1 = ExitStack()
        w0 = keep("w0", [P, KC, HID], F32R, p1)
        w1 = keep("w1", [P, HC, HID], F32R, p1)
        w2 = keep("w2", [P, HC, D], F32R, p1)
        WQ, WO, WK, WV = 0, KC * D, 2 * KC * D, 2 * KC * D + D
        WN = WV + D
        wat_hi = [keep(f"wat_hi{l}", [P, WN], F32R, p1) for l in range(2)]
        wat_lo = [keep(f"wat_lo{l}", [P, WN], F32R, p1) for l in range(2)]
        bk4 = keep("bk4", [P, KC], F32, p1)
        head_of_feature = keep("head_of_feature", [P, HH], F32, p1)
        head_of_row = keep("head_of_row", [P, RC, HH], F32, p1)
        row_heads = keep("row_heads", [HEADS, 2, ROWS], F32R, p1)
        ctx_sb = keep("ctx_sb", [IMG, T, KEYS], F32, p1)
        at = ExitStack()
        rep_hi = keep("rep_hi", [IMG, HH, KEYS], F32R, at)
        rep_lo = keep("rep_lo", [IMG, HH, KEYS], F32R, at)
        at.close()
        q_hi = [keep("q_hi0", [P, KC, TILE], F32R, p1)]
        q_lo = [keep("q_lo0", [P, KC, TILE], F32R, p1)]
        k_f = keep("k_f", [P, KC, KEYS], F32, p1)
        k_hi = keep("k_hi", [P, KC, KEYS], F32R, p1)
        k_lo = keep("k_lo", [P, KC, KEYS], F32R, p1)
        kbd_hi = {"C": keep("kbd_hi_c", [P, 2, ROWS], F32R, p1)}
        kbd_lo = keep("kbd_lo", [P, 2, ROWS], F32R, p1)
        vbd = keep("vbd", [P, RC, 2, WINDOW, DK], F32, p1)
        v_part = [keep(f"v_part{j}", [P, RC, 2, WINDOW, VW], BF16, p1) for j in range(VPARTS)]
        neg_max = [keep(f"neg_max{i}", [P, SUB, HEADS], F32, p1) for i in range(NT)]
        neg_max_t = keep("neg_max_t", [HEADS, TILE], F32R, p1)
        inv_sum = keep("inv_sum", [P, SUB, HEADS], F32, p1)
        at = ExitStack()
        row_f = keep("row_f", [2, 3, D], F32, at)
        row_hi = keep("row_hi", [2, 3, D], F32R, at)
        w_raw = [keep("w_raw0", [P, WN], F32, at)[:, :]]
        rh_raw = keep("rh_raw", [HEADS, 2, ROWS], F32, at)
        at.close()
        at = ExitStack()
        p_hi = keep("p_hi", [P, 2 * RC, TILE], F16, at)
        p_lo = keep("p_lo", [P, 2 * RC, TILE], F16, at)
        q_hi.append(keep("q_hi1", [P, KC, TILE], F32R, at))
        q_lo.append(keep("q_lo1", [P, KC, TILE], F32R, at))
        at.close()
        at = ExitStack()
        keep("before_p_f", [P, 2 * RC + 2 * 2 * KC, TILE], F16, at)
        keep("before_p_f2", [P, 2 * RC, TILE], F16, at)
        p_f = keep("p_f", [P, P_RING, TILE], F32, at)
        kbd_hi["A"] = keep("kbd_hi_a", [P, 2, ROWS], F32R, at)
        at.close()
        at = ExitStack()
        h1_hi = keep("h1_hi", [P, HC, TILE], F32R, at)
        h1_lo = keep("h1_lo", [P, HC, TILE], F32R, at)
        h2_hi = keep("h2_hi", [P, H2RING, TILE], F32R, at)
        h2_lo = keep("h2_lo", [P, H2RING, TILE], F32R, at)
        at.close()
        p1.close()

        w_raw.append(x_sb[:, 2:4, :, :].rearrange("p a s d -> p (a s d)")[:, 0:WN])
        k1_raw = x_sb[:, 4:6, :, :].bitcast(U8).rearrange("p a s m -> p (a s) m")
        k2_raw = x_sb[:, 6, 0:2, :].bitcast(U8).rearrange("p s (j d) -> p (s j) d", d=D)
        k0_raw = x_sb[:, 7, :, :].bitcast(U8)

        p2 = ExitStack()
        NW = 8
        XO, CO = 0, 7
        wd_hi = keep("wd_hi", [P, NW, KC, D], F32R, p2)
        wd_lo = keep("wd_lo", [P, NW, KC, D], F32R, p2)
        wd_raw = keep("wd_raw", [P, NW, KC, D], F32, p2)
        xo_sb = keep("xo_sb", [P, T * NT, SUB, D], F32, p2)
        c_f = [keep(f"c_f{i}", [P, KC, TILE], F32, p2) for i in range(NT)]
        c_hi = [keep(f"c_hi{i}", [P, KC, TILE], F32R, p2) for i in range(NT)]
        c_lo = [keep(f"c_lo{i}", [P, KC, TILE], F32R, p2) for i in range(NT)]
        gate = [[keep(f"gate{g}_{i}", [P, KC, TILE], F32, p2) for g in range(3)] for i in range(NT)]
        co_sb = [keep(f"co_sb{i}", [P, SUB, D], F32, p2) for i in range(NT)]
        p2.close()

        psum = ctx.enter_context(nc.psum_tensor("psum", [P, 8, 512], F32))

        bank_filled = [sem(f"bank_filled{b}") for b in range(8)]
        bank_drained = [sem(f"bank_drained{b}") for b in range(8)]
        consts_loaded = sem("consts_loaded")
        ctx_loaded = sem("ctx_loaded")
        attn_weights_loaded = [sem(f"attn_weights_loaded{l}") for l in range(2)]
        bits_loaded = sem("bits_loaded")
        x_loaded = [sem(f"x_loaded{i}") for i in range(NT)]
        wd_loaded = [sem(f"wd_loaded{h}") for h in range(2)]
        out_stored = sem("out_stored")
        setup_dve = sem("setup_dve")
        setup_act = sem("setup_act")
        setup_pool = sem("setup_pool")
        attn_hi_ready = sem("attn_hi_ready")
        attn_lo_ready = [sem(f"attn_lo_ready{l}") for l in range(2)]
        rows_ready = sem("rows_ready")
        w1_ready = sem("w1_ready")
        w0_ready = sem("w0_ready")
        w2_ready = sem("w2_ready")
        stats_ready = sem("stats_ready")
        moments_ready = sem("moments_ready")
        var_eps_ready = sem("var_eps_ready")
        rstd_ready = sem("rstd_ready")
        normed_ready = sem("normed_ready")
        rep_hi_ready = sem("rep_hi_ready")
        rep_lo_ready = sem("rep_lo_ready")
        k_parts_ready = sem("k_parts_ready")
        kbd_hi_ready = sem("kbd_hi_ready")
        kbd_lo_ready = sem("kbd_lo_ready")
        hi_ready = [sem(f"hi_ready{b}") for b in range(8)]
        v_masked = sem("v_masked")
        v_parts_ready = sem("v_parts_ready")
        p_hi_dve = sem("p_hi_dve")
        p_lo_dve = sem("p_lo_dve")
        p_lo_pool = sem("p_lo_pool")
        inv_sum_ready = sem("inv_sum_ready")
        wd_hi_ready = sem("wd_hi_ready")
        wd_lo_ready = sem("wd_lo_ready")
        fc_ready = sem("fc_ready")
        ig_ready = sem("ig_ready")
        c2_ready = sem("c2_ready")
        c_f_ready = sem("c_f_ready")
        c_hi_ready = sem("c_hi_ready")
        c_lo_ready = sem("c_lo_ready")
        pre_ready = [sem("pre_ready_pool"), sem("pre_ready_dve")]
        h_ready = sem("h_ready")
        out_ready = sem("out_ready")

        jobs, per1, his1 = number_jobs(phase1_order(), [0] * 8, [0] * 8)
        base2 = [T * n for n in per1]
        jobs2, per2, _ = number_jobs(phase2_order(), base2, [T * n for n in his1])
        jobs3, _, _ = number_jobs(phase3_order(), [b + T * n for b, n in zip(base2, per2)], [0] * 8)
        jobs = {**jobs, **jobs2, **jobs3}

        def wait_filled(eng, name, t):
            eng.wait_ge(bank_filled[jobs[name].bank], jobs[name].count(t))

        def wait_drained(eng, name, t):
            eng.wait_ge(bank_drained[jobs[name].bank], jobs[name].count(t) + 1)

        def wait_free(eng, name, t):
            eng.wait_ge(bank_drained[jobs[name].bank], jobs[name].count(t))

        def bank(name):
            return psum[:, jobs[name].bank, :]

        LN1, LN2 = len(LAYER_NORMS), NT

        def ln_count(l, i, t):
            if l == "D":
                return t * LN2 + (T * LN1 + i + 1)
            return t * LN1 + (LAYER_NORMS.index((l, i)) + 1)

        def wait_hi(eng, name, t):
            eng.wait_ge(hi_ready[jobs[name].bank], jobs[name].hi_count(t))

        ATTN = [("A", 0), ("A", 1), ("C", 0), ("C", 1)]

        def attn_count(l, i, t, each):
            return t * (each * len(ATTN)) + each * (ATTN.index((l, i)) + 1)

        LAYER = {"A": 0, "C": 1}

        def wait_cut(eng, l, i, n, t):
            by_dve = n in CUT_BY_DVE[l, i]

            def count(tile, upto):
                return sum((c in CUT_BY_DVE[tile]) == by_dve for c in range(upto))

            before = sum(count(tile, 2 * RC) for tile in ATTN[:ATTN.index((l, i))])
            each = sum(count(tile, 2 * RC) for tile in ATTN)
            eng.wait_ge(p_lo_dve if by_dve else p_lo_pool, t * each + (before + count((l, i), n + 1)))

        def c_count(i, t):
            return t * NT + (2 * NT + i + 1)

        block = ctx.enter_context(nc.Block())

        @block.sync
        def _(sp):
            def weights(l, name, dst, n):
                sp.dma_start(w_raw[l][:, dst:dst + n * D].rearrange("p (c m) -> p c m", c=n),
                             a[name].rearrange("(c p) m -> p c m", p=P)).then_inc(attn_weights_loaded[l], 16)

            def x_tile(t, i):
                sp.dma_start(x_sb[:, t * NT + i, :, :],
                             a["x"][t * NT + i, :, :, :]).then_inc(x_loaded[i], 16)

            x_tile(0, 0)
            sp.dma_start(ctx_sb[:, :, :], a["ctx_t"].rearrange("b d k -> d b k")).then_inc(ctx_loaded, 16)
            sp.dma_start(ident[:, :], a["ident"]).then_inc(ctx_loaded, 16)
            for l in range(2):
                weights(l, f"wk{l}", WK, 1)
                weights(l, f"wv{l}", WV, 1)
                weights(l, f"wq{l}", WQ, KC)
                weights(l, f"wo{l}", WO, KC)
                if l == 0:
                    x_tile(0, 1)
            sp.dma_start(k0_raw, a["k0"].rearrange("(c p) m -> p c m", p=P)).then_inc(bits_loaded, 16)
            sp.dma_start(k1_raw, a["k1"].rearrange("(c p) m -> p c m", p=P)).then_inc(bits_loaded, 16)
            sp.dma_start(k2_raw, a["k2"].rearrange("(c p) m -> p c m", p=P)).then_inc(bits_loaded, 16)
            sp.wait_ge(w0_ready, 2)
            sp.wait_ge(w1_ready, 2)
            sp.wait_ge(w2_ready, 1)
            sp.wait_ge(attn_lo_ready[1], 1)
            with sp.Fori(1, T) as t:
                for i in range(NT):
                    sp.wait_ge(x_loaded[i], t * 16)
                    x_tile(t, i)
            wait_filled(sp, ("y", 1, 0), T - 1)
            wait_filled(sp, ("y", 1, 1), T - 1)
            for half, names in enumerate([["wo_d", "wf", "wi", "wc"], ["uf", "ui", "uc", "uo_d"]]):
                for j, name in enumerate(names):
                    sp.dma_start(wd_raw[:, half * NW // 2 + j, :, :],
                                 a[name].rearrange("(c p) m -> p c m", p=P)).then_inc(wd_loaded[half], 16)
            for i in range(NT):
                for nth, t in enumerate((1, 0, 3, 2)):
                    sp.wait_ge(out_ready, i * T + nth + 1)
                    sp.dma_start(out[t * NT + i, :, :, :], x_sb[:, t * NT + i, :, :]).then_inc(out_stored, 16)
            sp.wait_ge(out_stored, T * NT * 16)

        @block.gpsimd
        def _(pool):
            for first in bank_drained + [k_parts_ready, kbd_lo_ready, c_f_ready]:
                pool.sem_inc(first, 1)
            pool.memset(minus_half[:, :], -0.5).then_inc(setup_pool, 1)
            pool.memset(one_f[:, :], 1.0).then_inc(setup_pool, 1)
            pool.memset(eps[:, :], EPS).then_inc(setup_pool, 1)
            for part in v_part + [vbd]:
                pool.memset(part[:, :, :, :, :], 0.0).then_inc(setup_pool, 1)

            def rstd_of(l, i, t):
                pool.wait_ge(moments_ready, ln_count(l, i, t))
                pool.tensor_tensor(var_eps[i][:, :], moments[i][:, :, 1], eps[:, :], ALU.add).then_inc(var_eps_ready, 1)
                pool.wait_ge(var_eps_ready, ln_count(l, i, t))
                pool.tensor_tensor(rstd[i][:, :], var_eps[i][:, :], minus_half[:, :], ALU.pow).then_inc(rstd_ready, 1)

            def kbd_lo_of(l, t, before=None):
                if before is not None:
                    wait_filled(pool, ("st", "C", 1, 2 * RC - 1), before)
                pool.wait_ge(k_parts_ready, t * 4 + (1 + 2 * LAYER[l] + 2))
                for m in range(KC):
                    ins = pool.tensor_tensor(kbd_lo[:, m, :].rearrange("p (h k) -> p h k", h=HH),
                                             k_lo[:, m, :].bitcast(F32).unsqueeze(1).to_broadcast([P, HH, KEYS]),
                                             head_of_feature[:, :].unsqueeze(2).to_broadcast([P, HH, KEYS]), ALU.mult)
                ins.then_inc(kbd_lo_ready, 1)

            def p_lo_of(l, i, t, n0, n1):
                for n in range(n0, n1):
                    if n not in CUT_BY_DVE[l, i]:
                        rows = ROW_N[n % RC]
                        wait_drained(pool, ("st", l, i, n), t)
                        pool.tensor_tensor(p_lo[0:rows, n, :], p_f[0:rows, n % P_RING, :], p_hi[0:rows, n, :],
                                           ALU.subtract).then_inc(p_lo_pool, 1)

            def image(t, last):
                after, ta = ("D", 0) if last else ("A", t + 1)
                p_lo_of("A", 0, t, 2, 2 * RC)
                p_lo_of("A", 1, t, 0, 2 * RC)
                rstd_of("B", 0, t)
                kbd_lo_of("C", t)
                rstd_of("B", 1, t)
                rstd_of("C", 0, t)
                p_lo_of("C", 0, t, 0, 2)
                rstd_of("C", 1, t)
                p_lo_of("C", 0, t, 2, 2 * RC)
                rstd_of(after, 0, ta)
                p_lo_of("C", 1, t, 0, 2 * RC)
                rstd_of(after, 1, ta)
                if not last:
                    kbd_lo_of("A", ta, t)
                    p_lo_of("A", 0, ta, 0, 2)

            pool.wait_ge(setup_pool, 3)
            rstd_of("A", 0, 0)
            kbd_lo_of("A", 0)
            rstd_of("A", 1, 0)
            pool.wait_ge(w0_ready, 1)
            pool.wait_ge(setup_dve, 3)
            pool.tensor_tensor(w0[:, :, :], w0[:, :, :].bitcast(F32),
                               sgn[:, 6:7].unsqueeze(2).to_broadcast([P, KC, HID]), ALU.mult).then_inc(w0_ready, 1)
            pool.wait_ge(attn_hi_ready, 2)
            pool.tensor_tensor(wat_lo[1][:, :], w_raw[1], wat_hi[1][:, :].bitcast(F32), ALU.subtract)\
                .then_inc(attn_lo_ready[1], 1)
            p_lo_of("A", 0, 0, 0, 2)
            with pool.Fori(0, T - 1) as t:
                image(t, False)
            image(T - 1, True)
            for h in range(2):
                pool.wait_ge(wd_hi_ready, h + 1)
                half = slice(h * NW // 2, (h + 1) * NW // 2)
                pool.tensor_tensor(wd_lo[:, half, :, :], wd_raw[:, half, :, :], wd_hi[:, half, :, :].bitcast(F32),
                                   ALU.subtract).then_inc(wd_lo_ready, 1)
            with pool.Fori(0, T - 1) as t:
                rstd_of("D", 0, t + 1)
                rstd_of("D", 1, t + 1)
            for i in range(NT):
                for n in range(2):
                    wait_drained(pool, ("co", i, n), 0)
                for t in range(T):
                    if t % 2 == 0:
                        tile = xo_sb[:, t * NT + i, :, :]
                        pool.tensor_tensor(tile, tile, co_sb[i][:, :, :], ALU.add).then_inc(pre_ready[0], 1)

        @block.scalar
        def _(act):
            for dst, name in [(gates_in[:, :], "g"), (scal[:, :], "s")]:
                act.dma_start(dst, a[name].partition_broadcast(P)).then_inc(consts_loaded, 16)
            act.dma_start(cols[:, :, :], a["cols"]).then_inc(consts_loaded, 16)
            act.dma_start(row_f[:, :, :], a["rows"].partition_broadcast(2)).then_inc(consts_loaded, 16)
            act.dma_start(not_first[:, :], a["not_first"]).then_inc(consts_loaded, 16)
            act.dma_start(head_of_feature[:, :], a["head_of_feature"]).then_inc(consts_loaded, 16)
            act.dma_start(head_of_row[:, :, :], a["head_of_row"]).then_inc(consts_loaded, 16)
            act.dma_start(rh_raw[:, :, :], a["row_heads"]).then_inc(consts_loaded, 16)
            def hi_of(dst, name, t, func=ACT.Copy, bias=None):
                wait_filled(act, name, t)
                more = {} if bias is None else {"bias": bias}
                act.activation(dst, bank(name), func, **more).then_inc(hi_ready[jobs[name].bank], 1)

            def act_hi_of(kind, l, i, t):
                for k in range(KC):
                    hi_of(act_hi[i][:, k, :], (kind, l, i, k), t)

            def q_hi_of(l, i, t):
                for m in range(KC):
                    if l == "A":
                        hi_of(q_hi[i][:, m, :], ("q", l, i, m), t, ACT.Identity, bqk[:, 0, m:m + 1])
                    else:
                        hi_of(q_hi[i][:, m, :], ("q", l, i, m), t)

            def rep_hi_of(l, t):
                act.activation(rep_hi[:, :, :], ctx_sb[:, t, :].unsqueeze(1).to_broadcast([IMG, HH, KEYS]),
                               ACT.Copy).then_inc(rep_hi_ready, 1)


            def k_of(l, t):
                act.wait_ge(k_parts_ready, t * 4 + (1 + 2 * LAYER[l]))
                wait_filled(act, ("k", l), t)
                pk = bank(("k", l))[:, 0:KC * KP].rearrange("p (c k) -> p c k", c=KC)[:, :, 0:KEYS]
                if l == "A":
                    for m in range(KC):
                        ins = act.activation(k_f[:, m, :], pk[:, m, :], ACT.Identity, scale=KSCALE, bias=bk4[:, m:m + 1])
                else:
                    ins = act.activation(k_f[:, :, :], pk, ACT.Copy, scale=KSCALE)
                ins.then_inc(bank_drained[jobs["k", l].bank], 1)

            def neg_max_of(l, i, t):
                wait_filled(act, ("mt", l, i), t)
                act.activation(neg_max_t[:, :], bank(("mt", l, i))[0:HEADS, :], ACT.Copy)\
                    .then_inc(bank_drained[jobs["mt", l, i].bank], 1)

            def exps(l, i, t, n0, n1, before):
                if before is not None:
                    wait_filled(act, ("pv", *before[0], SUB - 1), before[1])
                for n in range(n0, n1):
                    name, rows = ("st", l, i, n), ROW_N[n % RC]
                    wait_filled(act, name, t)
                    if n not in CUT_BY_DVE[l, i]:
                        act.activation(p_hi[0:rows, n, :], bank(name)[0:rows, :], ACT.Exp)
                    if n >= P_RING:
                        wait_cut(act, l, i, n - P_RING, t)
                    act.activation(p_f[0:rows, n % P_RING, :], bank(name)[0:rows, :], ACT.Exp)\
                        .then_inc(bank_drained[jobs[name].bank], 1)

            def hidden(kind, i, t, ms):
                for m in ms:
                    name = (kind, i, m)
                    if kind == "h2":
                        hi_of(h2_hi[:, m % H2RING, :], name, t, ACT.Relu)
                    else:
                        hi_of(h1_hi[:, m, :], name, t, ACT.Relu)

            def wd_hi_of(h):
                act.wait_ge(wd_loaded[h], NW // 2 * 16)
                half = slice(h * NW // 2, (h + 1) * NW // 2)
                act.activation(wd_hi[:, half, :, :], wd_raw[:, half, :, :], ACT.Copy).then_inc(wd_hi_ready, 1)

            def image(t, last):
                act_hi_of("ln", "A", 1, t)
                exps("A", 0, t, 2, 4, None)
                q_hi_of("A", 1, t)
                exps("A", 0, t, 4, 2 * RC, None)
                neg_max_of("A", 1, t)
                exps("A", 1, t, 0, 3, (("A", 0), t))
                act_hi_of("ot", "A", 0, t)
                exps("A", 1, t, 3, 2 * RC, None)
                act_hi_of("ln", "B", 0, t)
                act_hi_of("ot", "A", 1, t)
                rep_hi_of("C", t)
                hidden("h1", 0, t, range(6))
                k_of("C", t)
                hidden("h1", 0, t, range(6, HC))
                hidden("h2", 0, t, range(4))
                act_hi_of("ln", "B", 1, t)
                hidden("h2", 0, t, range(4, HC))
                hidden("h1", 1, t, range(HC))
                hidden("h2", 1, t, range(4))
                act_hi_of("ln", "C", 0, t)
                hidden("h2", 1, t, range(4, 5))
                q_hi_of("C", 0, t)
                hidden("h2", 1, t, range(5, HC))
                neg_max_of("C", 0, t)
                exps("C", 0, t, 0, 8, None)
                act_hi_of("ln", "C", 1, t)
                exps("C", 0, t, 8, 2 * RC, None)
                q_hi_of("C", 1, t)
                if not last:
                    rep_hi_of("A", t + 1)
                act_hi_of("ot", "C", 0, t)
                neg_max_of("C", 1, t)
                if not last:
                    k_of("A", t + 1)
                if last:
                    exps("C", 1, t, 0, 2 * RC, (("C", 0), t))
                else:
                    exps("C", 1, t, 0, 5, (("C", 0), t))
                    act_hi_of("ln", "A", 0, t + 1)
                    exps("C", 1, t, 5, 7, None)
                    q_hi_of("A", 0, t + 1)
                    exps("C", 1, t, 7, 2 * RC, None)
                if last:
                    wd_hi_of(0)
                    act_hi_of("ln", "D", 0, 0)
                if not last:
                    neg_max_of("A", 0, t + 1)
                act_hi_of("ot", "C", 1, t)
                if last:
                    wd_hi_of(1)
                else:
                    exps("A", 0, t + 1, 0, 2, None)

            act.wait_ge(ctx_loaded, 2 * 16)
            rep_hi_of("A", 0)
            act.wait_ge(attn_weights_loaded[0], 4 * 16)
            act.activation(wat_hi[0][:, :], w_raw[0], ACT.Copy).then_inc(attn_hi_ready, 1)
            act.wait_ge(consts_loaded, 8 * 16)
            act.activation(gates[:, :], gates_in[:, :], ACT.Tanh).then_inc(setup_act, 1)
            act.activation(row_heads[:, :, :], rh_raw[:, :, :], ACT.Copy).then_inc(setup_act, 1)
            act.wait_ge(rows_ready, 2)
            k_of("A", 0)
            act_hi_of("ln", "A", 0, 0)
            q_hi_of("A", 0, 0)
            act.wait_ge(attn_weights_loaded[1], 4 * 16)
            act.activation(wat_hi[1][:, :], w_raw[1], ACT.Copy).then_inc(attn_hi_ready, 1)
            act.wait_ge(bits_loaded, 3 * 16)
            act.wait_ge(setup_dve, 3)
            for h in range(2):
                act.activation(w1[:, h * 4:h * 4 + 4, :], k1_raw[:, h * 4:h * 4 + 4, :], ACT.Identity,
                               scale=sgn[:, 4:5], bias=sgn[:, 5:6]).then_inc(w1_ready, 1)
            act.wait_ge(attn_lo_ready[0], 1)
            act.wait_ge(rows_ready, 2)
            neg_max_of("A", 0, 0)
            exps("A", 0, 0, 0, 2, None)
            with act.Fori(0, T - 1) as t:
                image(t, False)
            image(T - 1, True)

            def gates_of(i, t, m):
                for g in range(3):
                    name = ("gate", i, g, m)
                    wait_filled(act, name, t)
                    half = 0.5 if g < 2 else 1.0
                    bias = half_b[:, g, m:m + 1] if g < 2 else col_b[:, 2, m:m + 1]
                    act.activation(gate[i][g][:, m, :], bank(name), ACT.Tanh, scale=half, bias=bias)\
                        .then_inc(bank_drained[jobs[name].bank], 1)

            def cell(i, t, last):
                act.wait_ge(c2_ready, t * NT + (i + 1))
                act.activation(c_hi[i][:, :, :], gate[i][0][:, :, :], ACT.Copy, scale=0.5).then_inc(c_hi_ready, 1)
                if not last:
                    act.activation(c_f[i][:, :, :], gate[i][0][:, :, :], ACT.Copy, scale=0.5).then_inc(c_f_ready, 1)

            def x_out(i, t):
                for n in range(2):
                    name = ("xo", i, n)
                    wait_filled(act, name, t)
                    act.activation(xo_sb[:, t * NT + i, 2 * n:2 * n + 2, :],
                                   bank(name).rearrange("p (s d) -> p s d", s=2), ACT.Copy)\
                        .then_inc(bank_drained[jobs[name].bank], 1)

            def c_out(i):
                for n in range(2):
                    name = ("co", i, n)
                    wait_filled(act, name, 0)
                    act.activation(co_sb[i][:, 2 * n:2 * n + 2, :], bank(name).rearrange("p (s d) -> p s d", s=2),
                                   ACT.Copy).then_inc(bank_drained[jobs[name].bank], 1)

            def read_out(i, t):
                act.wait_ge(pre_ready[t % 2], i * (T // 2) + t // 2 + 1)
                tile = xo_sb[:, t * NT + i, :, :]
                act.activation(tile, tile, ACT.Tanh).then_inc(h_ready, 1)

            def step(t, last):
                x_out(0, t)
                act.wait_ge(c_lo_ready, c_count(0, t))
                gates_of(0, t, 0)
                act_hi_of("ln", "D", 1, t)
                gates_of(0, t, 1)
                x_out(1, t)
                act.wait_ge(c_lo_ready, c_count(1, t))
                gates_of(1, t, 0)
                cell(0, t, last)
                if not last:
                    act_hi_of("ln", "D", 0, t + 1)
                gates_of(1, t, 1)
                cell(1, t, last)

            with act.Fori(0, T - 1) as t:
                step(t, False)
            step(T - 1, True)
            for i in range(NT):
                c_out(i)
                for t in (1, 0, 3, 2):
                    read_out(i, t)

        @block.vector
        def _(dve):
            def ln_stats(l, i, t):
                tile = t * NT + i
                if l == "A":
                    dve.wait_ge(x_loaded[i], t * 16 + 16)
                elif l in "BC":
                    for n in range(2):
                        wait_drained(dve, ("wo", "A", i, n) if l == "B" else ("y", i, n), t)
                dve.memset(nothing[:, i, 0:1], 0.0)
                for s in range(SUB):
                    ins = dve.bn_stats(stats[i][:, s, :], x_sb[:, tile, s, :])
                ins.then_inc(stats_ready, 1)
                dve.wait_ge(stats_ready, ln_count(l, i, t))
                dve.memset(nothing[:, i, 1:2], 0.0)
                for s in range(SUB):
                    ins = dve.bn_aggr(moments[i][:, s, :], stats[i][:, s, :])
                ins.then_inc(moments_ready, 1)

            def ln_apply(l, i, t):
                tile = t * NT + i
                dve.wait_ge(moments_ready, ln_count(l, i, t))
                dve.wait_ge(rstd_ready, ln_count(l, i, t))
                for s in range(SUB):
                    ins = dve.tensor_scalar(token[i][:, s, :], x_sb[:, tile, s, :], moments[i][:, s, 0:1],
                                            rstd[i][:, s:s + 1], ALU.subtract, ALU.mult)
                ins.then_inc(normed_ready, 1)

            def act_lo_of(kind, l, i, t):
                for k in range(KC):
                    name = (kind, l, i, k)
                    wait_hi(dve, name, t)
                    dve.tensor_tensor(act_lo[i][:, k, :], bank(name), act_hi[i][:, k, :].bitcast(F32), ALU.subtract)\
                        .then_inc(bank_drained[jobs[name].bank], 1)

            def q_lo_of(l, i, t):
                for m in range(KC):
                    name = ("q", l, i, m)
                    wait_hi(dve, name, t)
                    if l == "A":
                        ins = dve.scalar_tensor_tensor(q_lo[i][:, m, :], bank(name), bqk[:, 0, m:m + 1],
                                                       q_hi[i][:, m, :].bitcast(F32), ALU.add, ALU.subtract)
                    else:
                        ins = dve.tensor_tensor(q_lo[i][:, m, :], bank(name), q_hi[i][:, m, :].bitcast(F32), ALU.subtract)
                    ins.then_inc(bank_drained[jobs[name].bank], 1)

            def rep_lo_of(l, t):
                dve.wait_ge(rep_hi_ready, t * 2 + (LAYER[l] + 1))
                dve.tensor_tensor(rep_lo[:, :, :], ctx_sb[:, t, :].unsqueeze(1).to_broadcast([IMG, HH, KEYS]),
                                  rep_hi[:, :, :].bitcast(F32), ALU.subtract).then_inc(rep_lo_ready, 1)

            def key_parts(l, t):
                n = 2 * LAYER[l]
                wait_drained(dve, ("k", l), t)
                dve.wait_ge(kbd_lo_ready, t * 2 + (1 + LAYER[l]))
                dve.tensor_copy(k_hi[:, :, :], k_f[:, :, :]).then_inc(k_parts_ready, 1)
                dve.wait_ge(k_parts_ready, t * 4 + (1 + n + 1))
                dve.tensor_tensor(k_lo[:, :, :], k_f[:, :, :], k_hi[:, :, :].bitcast(F32), ALU.subtract)\
                    .then_inc(k_parts_ready, 1)

            def block_keys(l, t):
                for m in range(KC):
                    ins = dve.tensor_tensor(kbd_hi[l][:, m, :].rearrange("p (h k) -> p h k", h=HH),
                                            k_hi[:, m, :].bitcast(F32).unsqueeze(1).to_broadcast([P, HH, KEYS]),
                                            head_of_feature[:, :].unsqueeze(2).to_broadcast([P, HH, KEYS]), ALU.mult)
                ins.then_inc(kbd_hi_ready, 1)

            def block_values(l, t, j):
                name = ("v", l, j)
                wait_filled(dve, name, t)
                for c in range(2 * j, min(2 * j + 2, RC)):
                    rows, o, h0 = ROW_N[c], (c % 2) * D, FIRST_HEAD[c]
                    ins = dve.tensor_tensor(
                        vbd[0:rows, c, :, :, :],
                        bank(name)[0:rows, o:o + D].rearrange("p (g h d) -> p g h d", g=2, h=HH)[:, :, h0:h0 + WINDOW, :],
                        head_of_row[0:rows, c, h0:h0 + WINDOW].unsqueeze(1).unsqueeze(3)
                        .to_broadcast([rows, 2, WINDOW, DK]), ALU.mult)
                ins.then_inc(bank_drained[jobs[name].bank], 1)

            def value_parts(l, t):
                for j in range(3):
                    wait_drained(dve, ("v", l, j), t)
                if l == "C":
                    wait_filled(dve, ("pv", "A", 1, SUB - 1), t)
                v, n = vbd[:, :, :, :, :].rearrange("p c g h d -> p (c g h) d"), t * 6 + 3 * LAYER[l]
                part = [v_part[j][:, :, :, :, 0:DK].rearrange("p c g h d -> p (c g h) d") for j in range(VPARTS)]
                dve.tensor_copy(part[0], v).then_inc(v_masked, 1)
                dve.wait_ge(v_masked, n + 1)
                dve.tensor_tensor(v, v, part[0], ALU.subtract).then_inc(v_masked, 1)
                dve.wait_ge(v_masked, n + 2)
                dve.tensor_copy(part[1], v).then_inc(v_masked, 1)
                dve.wait_ge(v_masked, n + 3)
                dve.tensor_tensor(part[2], v, part[1], ALU.subtract).then_inc(v_parts_ready, 1)

            def cut_of(l, i, t, ns):
                for n in ns:
                    rows = ROW_N[n % RC]
                    wait_drained(dve, ("st", l, i, n), t)
                    dve.tensor_copy(p_hi[0:rows, n, :], p_f[0:rows, n % P_RING, :]).then_inc(p_hi_dve, 1)
                    before = sum(len(CUT_BY_DVE[tile]) for tile in ATTN[:ATTN.index((l, i))])
                    each = sum(len(ns_) for ns_ in CUT_BY_DVE.values())
                    dve.wait_ge(p_hi_dve, t * each + (before + CUT_BY_DVE[l, i].index(n) + 1))
                    dve.tensor_tensor(p_lo[0:rows, n, :], p_f[0:rows, n % P_RING, :], p_hi[0:rows, n, :],
                                      ALU.subtract).then_inc(p_lo_dve, 1)

            def maxima(l, i, t, n0=0, n1=16):
                for n in range(n0, n1):
                    s, q = n // 4, n % 4
                    name = ("mx", l, i, n)
                    wait_filled(dve, name, t)
                    ins = dve.tensor_reduce(neg_max[i][:, s, MXH * q:MXH * q + MXH],
                                            bank(name)[:, 0:MXH * KEYS].rearrange("p (h k) -> p h k", h=MXH),
                                            AX.X, ALU.max, negate=True)
                    ins.then_inc(bank_drained[jobs[name].bank], 1)

            def heads(l, i, t, s0=0, s1=SUB):
                for s in range(s0, s1):
                    name = ("pv", l, i, s)
                    wait_filled(dve, name, t)
                    pv = bank(name)[:, 0:HEADS * VW].rearrange("p (h d) -> p h d", h=HEADS)
                    dve.reciprocal(inv_sum[:, s, :], pv[:, :, DK]).then_inc(inv_sum_ready, 1)
                    dve.wait_ge(inv_sum_ready, attn_count(l, i, t, SUB) - (SUB - 1 - s))
                    ins = dve.tensor_tensor(token[i][:, s, :].rearrange("p (h d) -> p h d", h=HEADS), pv[:, :, 0:DK],
                                            inv_sum[:, s, :].unsqueeze(2).to_broadcast([P, HEADS, DK]), ALU.mult)
                    ins.then_inc(bank_drained[jobs[name].bank], 1)

            def residual(l, i, t, n0=0, n1=2):
                gain = {"A": gates[:, 0:1], "B": gain_b[:, 0:1], "C": gates[:, 1:2]}[l]
                for n in range(n0, n1):
                    name = ("y", i, n) if l == "B" else ("wo", l, i, n)
                    wait_filled(dve, name, t)
                    part = x_sb[:, t * NT + i, 2 * n:2 * n + 2, :].rearrange("p s d -> p (s d)")
                    dve.scalar_tensor_tensor(part, bank(name), gain, part, ALU.mult, ALU.add)\
                        .then_inc(bank_drained[jobs[name].bank], 1)

            def hidden(kind, i, t, ms):
                for m in ms:
                    name = (kind, i, m)
                    hi, lo = (h1_hi, h1_lo) if kind == "h1" else (h2_hi, h2_lo)
                    at = m if kind == "h1" else m % H2RING
                    wait_hi(dve, name, t)
                    dve.scalar_tensor_tensor(lo[:, at, :], bank(name), 0.0, hi[:, at, :].bitcast(F32),
                                             ALU.max, ALU.subtract).then_inc(bank_drained[jobs[name].bank], 1)

            def image(t, last):
                after, ta = ("D", 0) if last else ("A", t + 1)
                act_lo_of("ln", "A", 1, t)
                q_lo_of("A", 1, t)
                value_parts("A", t)
                for n in range(4, 2 * RC):
                    maxima("A", 1, t, n - 4, n - 3)
                    if n in CUT_BY_DVE["A", 0]:
                        cut_of("A", 0, t, (n,))
                maxima("A", 1, t, 6, 9)
                heads("A", 0, t, 0, 1)
                maxima("A", 1, t, 9, 12)
                heads("A", 0, t, 1, 2)
                maxima("A", 1, t, 12, 16)
                heads("A", 0, t, 2, 4)
                cut_of("A", 1, t, (1,))
                act_lo_of("ot", "A", 0, t)
                cut_of("A", 1, t, (3, 5, 7))
                residual("A", 0, t, 0, 1)
                cut_of("A", 1, t, (9,))
                residual("A", 0, t, 1, 2)
                ln_stats("B", 0, t)
                heads("A", 1, t, 0, 2)
                ln_apply("B", 0, t)
                heads("A", 1, t, 2, 4)
                act_lo_of("ln", "B", 0, t)
                act_lo_of("ot", "A", 1, t)
                rep_lo_of("C", t)
                hidden("h1", 0, t, range(6))
                key_parts("C", t)
                block_keys("C", t)
                block_values("C", t, 0)
                hidden("h1", 0, t, range(6, HC))
                for j in range(1, 3):
                    block_values("C", t, j)
                residual("A", 1, t)
                ln_stats("B", 1, t)
                hidden("h2", 0, t, range(1))
                value_parts("C", t)
                ln_apply("B", 1, t)
                hidden("h2", 0, t, range(1, 4))
                act_lo_of("ln", "B", 1, t)
                hidden("h2", 0, t, range(4, HC))
                hidden("h1", 1, t, range(HC))
                residual("B", 0, t)
                ln_stats("C", 0, t)
                hidden("h2", 1, t, range(1))
                ln_apply("C", 0, t)
                hidden("h2", 1, t, range(1, 4))
                act_lo_of("ln", "C", 0, t)
                hidden("h2", 1, t, range(4, 5))
                q_lo_of("C", 0, t)
                for m in range(5, HC):
                    maxima("C", 0, t, 5 * (m - 5), 5 * (m - 4))
                    if m == HC - 1:
                        maxima("C", 0, t, 15, 16)
                    hidden("h2", 1, t, range(m, m + 1))
                residual("B", 1, t)
                ln_stats("C", 1, t)
                cut_of("C", 0, t, (1, 3))
                ln_apply("C", 1, t)
                cut_of("C", 0, t, (5, 7))
                act_lo_of("ln", "C", 1, t)
                cut_of("C", 0, t, (9,))
                q_lo_of("C", 1, t)
                if not last:
                    rep_lo_of("A", ta)
                for s in range(3):
                    heads("C", 0, t, s, s + 1)
                    maxima("C", 1, t, 3 * s, 3 * s + 3)
                heads("C", 0, t, 3, 4)
                maxima("C", 1, t, 9, 12)
                act_lo_of("ot", "C", 0, t)
                maxima("C", 1, t, 12, 16)
                ln_stats(after, 0, ta)
                residual("C", 0, t)
                ln_apply(after, 0, ta)
                if not last:
                    key_parts("A", ta)
                    block_values("A", ta, 0)
                    block_keys("A", ta)
                    block_values("A", ta, 1)
                    block_values("A", ta, 2)
                cut_of("C", 1, t, (4,))
                if last:
                    cut_of("C", 1, t, (9,))
                    ln_stats(after, 1, ta)
                    heads("C", 1, t)
                    act_lo_of("ln", "D", 0, 0)
                    act_lo_of("ot", "C", 1, t)
                    ln_apply(after, 1, ta)
                    residual("C", 1, t)
                else:
                    act_lo_of("ln", "A", 0, ta)
                    ln_stats("A", 1, ta)
                    q_lo_of("A", 0, ta)
                    maxima("A", 0, ta, 0, 6)
                    cut_of("C", 1, t, (9,))
                    heads("C", 1, t, 0, 1)
                    for s in range(1, SUB):
                        maxima("A", 0, ta, 3 + 3 * s, 6 + 3 * s if s < 3 else 16)
                        heads("C", 1, t, s, s + 1)
                    act_lo_of("ot", "C", 1, t)
                    ln_apply("A", 1, ta)
                    residual("C", 1, t)

            ln_stats("A", 0, 0)
            dve.wait_ge(ctx_loaded, 2 * 16)
            rep_lo_of("A", 0)
            dve.wait_ge(attn_hi_ready, 1)
            dve.tensor_tensor(wat_lo[0][:, :], w_raw[0], wat_hi[0][:, :].bitcast(F32), ALU.subtract)\
                .then_inc(attn_lo_ready[0], 1)
            ln_apply("A", 0, 0)
            dve.wait_ge(consts_loaded, 8 * 16)
            dve.wait_ge(setup_pool, 3)
            dve.tensor_copy(ones_row[:, :], one_f[:, :])
            dve.tensor_copy(row_hi[:, :, :], row_f[:, :, :]).then_inc(rows_ready, 1)
            dve.tensor_scalar(bk4[:, :], bqk[:, 1, :], KSCALE, None, ALU.mult)
            dve.tensor_scalar(half_b[:, :, :], col_b[:, 0:2, :], 0.5, None, ALU.mult)
            dve.wait_ge(rows_ready, 1)
            dve.scalar_tensor_tensor(bias_rows[:, :, :], row_hi[:, :, :].bitcast(F32), not_first[:, 0:1],
                                     row_f[:, :, :], ALU.mult, ALU.add).then_inc(rows_ready, 1)
            key_parts("A", 0)
            block_keys("A", 0)
            dve.wait_ge(setup_pool, 3 + VPARTS + 1)
            for c in range(RC):
                dve.tensor_copy(v_part[0][:, c, :, :, DK], head_of_row[:, c, FIRST_HEAD[c]:FIRST_HEAD[c] + WINDOW]
                                .unsqueeze(1).to_broadcast([P, 2, WINDOW]))
            for j in range(3):
                block_values("A", 0, j)
            act_lo_of("ln", "A", 0, 0)
            ln_stats("A", 1, 0)
            q_lo_of("A", 0, 0)
            dve.tensor_scalar(sgn[:, 0:2], scal[:, 0:2], 0.0, None, ALU.is_gt).then_inc(setup_dve, 1)
            dve.tensor_scalar(sgn[:, 2:4], scal[:, 0:2], 0.0, None, ALU.is_lt).then_inc(setup_dve, 1)
            dve.wait_ge(setup_dve, 2)
            dve.tensor_tensor(sgn[:, 6:8], sgn[:, 0:2], sgn[:, 2:4], ALU.subtract)
            dve.tensor_tensor(sgn[:, 5:6], sgn[:, 3:4], sgn[:, 1:2], ALU.subtract)
            dve.tensor_scalar(sgn[:, 4:5], sgn[:, 1:2], sgn[:, 3:4], 2.0, ALU.subtract, ALU.mult).then_inc(setup_dve, 1)
            dve.wait_ge(setup_dve, 3)
            dve.wait_ge(setup_act, 1)
            dve.tensor_tensor(gain_b[:, :], scal[:, 0:1], scal[:, 1:2], ALU.mult).then_inc(setup_dve, 1)
            dve.wait_ge(setup_dve, 4)
            dve.tensor_scalar(gain_b[:, :], gain_b[:, :], scal[:, 2:3], 8.0, ALU.mult, ALU.mult).then_inc(setup_dve, 1)
            dve.wait_ge(setup_dve, 5)
            dve.tensor_scalar(gain_b[:, :], gain_b[:, :], gates[:, 2:3], sgn[:, 6:7], ALU.mult, ALU.mult)\
                .then_inc(setup_dve, 1)
            dve.wait_ge(setup_dve, 6)
            dve.tensor_scalar(gain_b[:, :], gain_b[:, :], sgn[:, 7:8], None, ALU.mult)
            maxima("A", 0, 0)
            ln_apply("A", 1, 0)
            dve.wait_ge(bits_loaded, 3 * 16)
            dve.tensor_tensor(w0[:, :, :], k0_raw[:, 0:KC, :], k0_raw[:, KC:2 * KC, :], ALU.subtract).then_inc(w0_ready, 1)
            dve.tensor_scalar(w2[:, :, :], k2_raw, 2.0, -1.0, ALU.mult, ALU.add).then_inc(w2_ready, 1)
            with dve.Fori(0, T - 1) as t:
                image(t, False)
            image(T - 1, True)

            def first_c(i):
                dve.tensor_copy(c_f[i][:, :, :], c0_col[:, :].unsqueeze(2).to_broadcast([P, KC, TILE])).then_inc(c_lo_ready, 1)
                dve.tensor_copy(c_hi[i][:, :, :], c0_col[:, :].unsqueeze(2).to_broadcast([P, KC, TILE])).then_inc(c_lo_ready, 1)
                dve.wait_ge(c_lo_ready, 3 * i + 2)
                dve.tensor_tensor(c_lo[i][:, :, :], c_f[i][:, :, :], c_hi[i][:, :, :].bitcast(F32), ALU.subtract)\
                    .then_inc(c_lo_ready, 1)

            def cell(i, t):
                for m in range(KC):
                    for g in range(3):
                        wait_drained(dve, ("gate", i, g, m), t)
                dve.wait_ge(c_f_ready, t * NT + 1)
                dve.scalar_tensor_tensor(gate[i][0][:, :, :], gate[i][0][:, :, :], 1.0, c_f[i][:, :, :],
                                         ALU.add, ALU.mult).then_inc(fc_ready, 1)
                dve.scalar_tensor_tensor(gate[i][1][:, :, :], gate[i][1][:, :, :], 1.0, gate[i][2][:, :, :],
                                         ALU.add, ALU.mult).then_inc(ig_ready, 1)
                dve.wait_ge(fc_ready, t * NT + (i + 1))
                dve.wait_ge(ig_ready, t * NT + (i + 1))
                dve.tensor_tensor(gate[i][0][:, :, :], gate[i][0][:, :, :], gate[i][1][:, :, :], ALU.add)\
                    .then_inc(c2_ready, 1)

            def cell_lo(i, t):
                dve.wait_ge(c2_ready, t * NT + (i + 1))
                dve.wait_ge(c_hi_ready, t * NT + (i + 1))
                dve.scalar_tensor_tensor(c_lo[i][:, :, :], gate[i][0][:, :, :], 0.5, c_hi[i][:, :, :].bitcast(F32),
                                         ALU.mult, ALU.subtract).then_inc(c_lo_ready, 1)

            def read_out_sum(i, t):
                if t % 2 == 1:
                    for n in range(2):
                        wait_drained(dve, ("co", i, n), 0)
                    tile = xo_sb[:, t * NT + i, :, :]
                    dve.tensor_tensor(tile, tile, co_sb[i][:, :, :], ALU.add).then_inc(pre_ready[1], 1)

            def finish(i, t, nth):
                dve.wait_ge(h_ready, i * T + nth + 1)
                tile = x_sb[:, t * NT + i, :, :].rearrange("p s d -> p (s d)")
                dve.scalar_tensor_tensor(tile, xo_sb[:, t * NT + i, :, :].rearrange("p s d -> p (s d)"),
                                         gates[:, 3:4], tile, ALU.mult, ALU.add).then_inc(out_ready, 1)

            def step(t, last):
                if not last:
                    ln_stats("D", 0, t + 1)
                act_lo_of("ln", "D", 1, t)
                if not last:
                    ln_apply("D", 0, t + 1)
                    ln_stats("D", 1, t + 1)
                cell(0, t)
                if not last:
                    ln_apply("D", 1, t + 1)
                cell_lo(0, t)
                if not last:
                    act_lo_of("ln", "D", 0, t + 1)
                cell(1, t)
                cell_lo(1, t)

            for n in range(2):
                wait_drained(dve, ("wo", "C", 1, n), T - 1)
            for i in range(NT):
                first_c(i)
            with dve.Fori(0, T - 1) as t:
                step(t, False)
            step(T - 1, True)
            for q in range(T):
                read_out_sum(0, q)
            for nth, t in enumerate((1, 0, 3, 2)):
                finish(0, t, nth)
            for q in range(T):
                read_out_sum(1, q)
            for nth, t in enumerate((1, 0, 3, 2)):
                finish(1, t, nth)

        @block.tensor
        def _(pe):
            def begin(name, t):
                wait_free(pe, name, t)

            def done(ins, name):
                ins.then_inc(bank_filled[jobs[name].bank], 1)

            def terms(dst, lefts, rights, start=True, stop=True):
                n = len(lefts)
                for k, ((lh, ll), (rh, rl)) in enumerate(zip(lefts, rights)):
                    pe.matmul(dst, lh, rh, start=start and k == 0, stop=False, skip_group_check=True)
                    pe.matmul(dst, lh, rl, start=False, stop=False, skip_group_check=True)
                    ins = pe.matmul(dst, ll, rh, start=False, stop=stop and k == n - 1, skip_group_check=True)
                return ins

            def wat(l, at, n, m0=0, m=D):
                j = LAYER[l]
                return [(wat_hi[j][:, at + k * D + m0:at + k * D + m0 + m],
                         wat_lo[j][:, at + k * D + m0:at + k * D + m0 + m]) for k in range(n)]

            def rep(c0, n):
                hi = rep_hi[:, :, :].rearrange("p h k -> p (h k)")
                lo = rep_lo[:, :, :].rearrange("p h k -> p (h k)")
                return hi[:, c0:c0 + n], lo[:, c0:c0 + n]

            def keys(l, t):
                pe.wait_ge(rep_lo_ready, t * 2 + (LAYER[l] + 1))
                begin(("k", l), t)
                pk = bank(("k", l))
                for m in range(KC):
                    ins = terms(pk[:, m * KP:m * KP + KP], wat(l, WK, 1, m * P, P), [rep(0, KP)], start=m == 0)
                done(ins, ("k", l))

            def new_values(l, t, j):
                name = ("v", l, j)
                begin(name, t)
                for c in range(2 * j, min(2 * j + 2, RC)):
                    rows = ROW_N[c]
                    dst = bank(name)[0:rows, (c % 2) * D:(c % 2) * D + D]
                    first = c % 2 == 0
                    ins = terms(dst, [rep(c * P, rows)], wat(l, WV, 1), start=first, stop=l == "C")
                    if l == "A":
                        ins = pe.matmul(dst, ones_row[0:2, 0:rows], bias_rows[0:2, 0, :], start=False, stop=True,
                                        skip_group_check=True)
                done(ins, name)

            def transposes(kind, l, i, t):
                if kind == "ln":
                    pe.wait_ge(normed_ready, ln_count(l, i, t))
                else:
                    wait_drained(pe, ("pv", l, i, SUB - 1), t)
                for k in range(KC):
                    name = (kind, l, i, k)
                    begin(name, t)
                    for s in range(SUB):
                        ins = pe.transpose(bank(name)[:, s * P:s * P + P], token[i][:, s, k * P:k * P + P], ident[:, :])
                    done(ins, name)

            def wait_act(kind, l, i, t):
                for k in range(KC):
                    wait_drained(pe, (kind, l, i, k), t)

            def query(l, i, t):
                wait_act("ln", l, i, t)
                for m in range(KC):
                    name = ("q", l, i, m)
                    begin(name, t)
                    done(terms(bank(name), wat(l, WQ, KC, m * P, P),
                               [(act_hi[i][:, k, :], act_lo[i][:, k, :]) for k in range(KC)]), name)

            def maxima(l, i, t, n0=0, n1=16):
                if n0 == 0:
                    for m in range(KC):
                        wait_drained(pe, ("q", l, i, m), t)
                    pe.wait_ge(kbd_hi_ready, t * 2 + (LAYER[l] + 1))
                for n in range(n0, n1):
                    s, q = n // 4, n % 4
                    name = ("mx", l, i, n)
                    begin(name, t)
                    at = (q % 2) * MXH * KEYS
                    done(pe.matmul(bank(name)[:, 0:MXH * KEYS], q_hi[i][:, q // 2, s * P:s * P + P],
                                   kbd_hi[l][:, q // 2, at:at + MXH * KEYS], start=True, stop=True), name)

            def neg_max_rows(l, i, t):
                wait_drained(pe, ("mx", l, i, 15), t)
                name = ("mt", l, i)
                begin(name, t)
                for s in range(SUB):
                    ins = pe.transpose(bank(name)[0:HEADS, s * P:s * P + P], neg_max[i][:, s, :], ident[:, :])
                done(ins, name)

            def scores(l, i, t, n0=0, n1=2 * RC):
                if n0 == 0:
                    wait_drained(pe, ("mt", l, i), t)
                    pe.wait_ge(kbd_lo_ready, t * 2 + (1 + LAYER[l] + 1))
                for n in range(n0, n1):
                    name = ("st", l, i, n)
                    half, c = n // RC, n % RC
                    rows = ROW_N[c]
                    begin(name, t)
                    dst = bank(name)[0:rows, :]
                    pe.matmul(dst, row_heads[:, half, c * P:c * P + rows], neg_max_t[:, :], start=True, stop=False,
                              skip_group_check=True)
                    done(terms(dst, [(kbd_hi[l][:, half, c * P:c * P + rows], kbd_lo[:, half, c * P:c * P + rows])],
                               [(q_hi[i][:, half, :], q_lo[i][:, half, :])], start=False), name)

            def values(l, i, t, s0=0, s1=SUB, beside={}):
                if s0 == 0:
                    pe.wait_ge(v_parts_ready, t * 2 + (LAYER[l] + 1))
                for s in range(s0, s1):
                    name = ("pv", l, i, s)
                    begin(name, t)
                    for n in range(2 * RC):
                        if s == 0:
                            wait_cut(pe, l, i, n, t)
                        half, c = n // RC, n % RC
                        rows, at = ROW_N[c], (half * HH + FIRST_HEAD[c]) * VW
                        dst = bank(name)[:, at:at + WINDOW * VW]
                        for p, j in ((p_hi, 0), (p_hi, 1), (p_hi, 2), (p_lo, 0), (p_lo, 1)):
                            ins = pe.matmul(dst, p[0:rows, n, s * P:s * P + P],
                                            v_part[j][0:rows, c, half, :, :].rearrange("p h d -> p (h d)"),
                                            start=n == 0 and j == 0 and p is p_hi, stop=n == 2 * RC - 1,
                                            skip_group_check=True)
                        if n == 2 * RC - 1:
                            done(ins, name)
                        if n in beside:
                            maxima(*beside[n])

            def by_token(name, t, lefts, weight, start_hi, bias=None):
                for j in range(2):
                    s = 2 * name[-1] + j
                    dst = bank(name)[:, j * D:j * D + D]
                    ins = terms(dst, [(lh[:, k, s * P:s * P + P], ll[:, k, s * P:s * P + P]) for lh, ll in [lefts]
                                      for k in range(KC)], weight, start=start_hi and j == 0, stop=bias is None)
                    if bias is not None:
                        ins = pe.matmul(dst, ones_row[0:2, :], bias_rows[0:2, bias, :], start=False, stop=True,
                                        skip_group_check=True)
                return ins

            def project(l, i, t, n0=0, n1=2):
                wait_act("ot", l, i, t)
                for n in range(n0, n1):
                    name = ("wo", l, i, n)
                    begin(name, t)
                    done(by_token(name, t, (act_hi[i], act_lo[i]), wat(l, WO, KC), True, 1 if l == "A" else None), name)

            def hidden1(i, t, ms):
                for m in ms:
                    name = ("h1", i, m)
                    if m == 0:
                        wait_act("ln", "B", i, t)
                    begin(name, t)
                    for k in range(KC):
                        w = w0[:, k, m * P:m * P + P]
                        pe.matmul(bank(name), w, act_hi[i][:, k, :], start=k == 0, stop=False)
                        ins = pe.matmul(bank(name), w, act_lo[i][:, k, :], start=False, stop=k == KC - 1)
                    done(ins, name)

            def hidden2(i, t, m, beside=None):
                name = ("h2", i, m)
                begin(name, t)
                for k in range(HC):
                    if m == 0:
                        wait_drained(pe, ("h1", i, k), t)
                    w = w1[:, k, m * P:m * P + P]
                    pe.matmul(bank(name), w, h1_hi[:, k, :], start=k == 0, stop=False)
                    ins = pe.matmul(bank(name), w, h1_lo[:, k, :], start=False, stop=k == HC - 1)
                    if k == HC - 1:
                        done(ins, name)
                    if beside is not None:
                        beside(k)

            def third(i, t, m):
                wait_drained(pe, ("h2", i, m), t)
                if m == 0:
                    begin(("y", i, 0), t)
                    begin(("y", i, 1), t)
                at = m % H2RING
                for s in range(SUB):
                    name = ("y", i, s // 2)
                    dst = bank(name)[:, (s % 2) * D:(s % 2) * D + D]
                    pe.matmul(dst, h2_hi[:, at, s * P:s * P + P], w2[:, m, :], start=m == 0 and s % 2 == 0, stop=False,
                              skip_group_check=True)
                    ins = pe.matmul(dst, h2_lo[:, at, s * P:s * P + P], w2[:, m, :], start=False, stop=m == HC - 1,
                                    skip_group_check=True)
                    if m == HC - 1 and s % 2 == 1:
                        done(ins, name)

            def maxima_beside(t, m):
                def beside(k):
                    if k in (1, 2, 4, 5, 7):
                        n = 5 * (m - 5) + (1, 2, 4, 5, 7).index(k)
                        maxima("C", 0, t, n, n + 1)
                return beside

            def three(l, i, t, n):
                return {at: (l, i, t, n + j, n + j + 1) for j, at in enumerate((2, 5, 8) if n < 12 else (1, 3, 5, 7))}

            def image(t, last):
                transposes("ln", "A", 1, t)
                scores("A", 0, t, 2, 4)
                query("A", 1, t)
                for n in range(4, 2 * RC):
                    scores("A", 0, t, n, n + 1)
                    maxima("A", 1, t, n - 4, n - 3)
                values("A", 0, t, 0, 1, three("A", 1, t, 6))
                values("A", 0, t, 1, 2, three("A", 1, t, 9))
                values("A", 0, t, 2, 3, three("A", 1, t, 12))
                neg_max_rows("A", 1, t)
                values("A", 0, t, 3, 4)
                scores("A", 1, t, 0, 3)
                transposes("ot", "A", 0, t)
                scores("A", 1, t, 3, 7)
                project("A", 0, t, 0, 1)
                scores("A", 1, t, 7)
                project("A", 0, t, 1, 2)
                values("A", 1, t)
                transposes("ln", "B", 0, t)
                transposes("ot", "A", 1, t)
                pe.wait_ge(w0_ready, 2)
                pe.wait_ge(w1_ready, 2)
                pe.wait_ge(w2_ready, 1)
                pe.wait_ge(attn_lo_ready[1], 1)
                hidden1(0, t, range(6))
                keys("C", t)
                new_values("C", t, 0)
                hidden1(0, t, range(6, HC))
                for j in range(1, 3):
                    new_values("C", t, j)
                project("A", 1, t)
                for m in range(HC):
                    hidden2(0, t, m)
                    if m >= 1:
                        third(0, t, m - 1)
                    if m == 3:
                        transposes("ln", "B", 1, t)
                hidden1(1, t, range(HC))
                third(0, t, HC - 1)
                for m in range(HC):
                    hidden2(1, t, m, maxima_beside(t, m) if m >= 5 else None)
                    if m == HC - 1:
                        maxima("C", 0, t, 15, 16)
                    if m >= 1:
                        third(1, t, m - 1)
                    if m == 3:
                        transposes("ln", "C", 0, t)
                    if m == 4:
                        query("C", 0, t)
                neg_max_rows("C", 0, t)
                third(1, t, HC - 1)
                scores("C", 0, t, 0, 8)
                transposes("ln", "C", 1, t)
                scores("C", 0, t, 8)
                query("C", 1, t)
                values("C", 0, t, 0, 1)
                for s in range(1, SUB):
                    values("C", 0, t, s, s + 1, three("C", 1, t, 3 * s - 3))
                maxima("C", 1, t, 9, 12)
                transposes("ot", "C", 0, t)
                maxima("C", 1, t, 12, 16)
                project("C", 0, t, 0, 1)
                neg_max_rows("C", 1, t)
                project("C", 0, t, 1, 2)
                if last:
                    scores("C", 1, t)
                    values("C", 1, t)
                    transposes("ln", "D", 0, 0)
                    transposes("ot", "C", 1, t)
                    project("C", 1, t)
                else:
                    keys("A", t + 1)
                    new_values("A", t + 1, 0)
                    scores("C", 1, t, 0, 2)
                    new_values("A", t + 1, 1)
                    scores("C", 1, t, 2, 4)
                    new_values("A", t + 1, 2)
                    scores("C", 1, t, 4, 5)
                    transposes("ln", "A", 0, t + 1)
                    scores("C", 1, t, 5, 7)
                    query("A", 0, t + 1)
                    for n in range(7, 2 * RC):
                        scores("C", 1, t, n, n + 1)
                        maxima("A", 0, t + 1, 2 * (n - 7), 2 * (n - 6))
                    values("C", 1, t, 0, 1)
                    for s in range(1, SUB):
                        values("C", 1, t, s, s + 1, three("A", 0, t + 1, 3 + 3 * s))
                    neg_max_rows("A", 0, t + 1)
                    transposes("ot", "C", 1, t)
                    scores("A", 0, t + 1, 0, 2)
                    project("C", 1, t)

            pe.wait_ge(ctx_loaded, 2 * 16)
            pe.wait_ge(attn_lo_ready[0], 1)
            keys("A", 0)
            pe.wait_ge(rows_ready, 2)
            pe.wait_ge(setup_act, 2)
            for j in range(3):
                new_values("A", 0, j)
            transposes("ln", "A", 0, 0)
            query("A", 0, 0)
            maxima("A", 0, 0)
            neg_max_rows("A", 0, 0)
            scores("A", 0, 0, 0, 2)
            with pe.Fori(0, T - 1) as t:
                image(t, False)
            image(T - 1, True)

            def wd(n, m0=0, m=D):
                return [(wd_hi[:, n, k, m0:m0 + m], wd_lo[:, n, k, m0:m0 + m]) for k in range(KC)]

            def x_out(i, t):
                wait_act("ln", "D", i, t)
                for n in range(2):
                    name = ("xo", i, n)
                    begin(name, t)
                    done(by_token(name, t, (act_hi[i], act_lo[i]), wd(XO), True, 2), name)

            def gates_of(i, t, m):
                for g in range(3):
                    name = ("gate", i, g, m)
                    begin(name, t)
                    terms(bank(name), wd(1 + g, m * P, P),
                          [(act_hi[i][:, k, :], act_lo[i][:, k, :]) for k in range(KC)], stop=False)
                    if m == 0 and g == 0:
                        pe.wait_ge(wd_lo_ready, 2)
                        pe.wait_ge(c_lo_ready, c_count(i, t))
                    done(terms(bank(name), wd(4 + g, m * P, P),
                               [(c_hi[i][:, k, :], c_lo[i][:, k, :]) for k in range(KC)], start=False), name)

            def c_out(i):
                pe.wait_ge(c_lo_ready, c_count(i, T))
                for n in range(2):
                    name = ("co", i, n)
                    begin(name, 0)
                    done(by_token(name, 0, (c_hi[i], c_lo[i]), wd(CO), True), name)

            def step(t, last):
                x_out(0, t)
                gates_of(0, t, 0)
                transposes("ln", "D", 1, t)
                gates_of(0, t, 1)
                x_out(1, t)
                gates_of(1, t, 0)
                if not last:
                    transposes("ln", "D", 0, t + 1)
                gates_of(1, t, 1)

            pe.wait_ge(wd_lo_ready, 1)
            with pe.Fori(0, T - 1) as t:
                step(t, False)
            step(T - 1, True)
            for i in range(NT):
                c_out(i)


def kernel(**inputs):
    import concourse.bacc as bacc
    from concourse.bass_utils import run_bass_kernel_spmd

    v = {k: np.asarray(x) for k, x in inputs.items()}
    wkv = v["L1_xattn_Wkv"]
    row = np.arange(RC * P).reshape(RC, P)
    heads = np.arange(HH)
    arrays = {
        "x": v["x"].reshape(T * NT, P, SUB, D),
        "ctx_t": v["ctx_512"].transpose(0, 2, 1),
        "wq0": v["L0_xattn_Wq"], "wk0": v["L0_xattn_Wk"], "wv0": v["L0_xattn_Wv"], "wo0": v["L0_xattn_Wo"],
        "wq1": v["L1_xattn_Wq"].T, "wk1": wkv[:D].T, "wv1": wkv[D:].T, "wo1": v["L1_xattn_Wo"].T,
        "cols": np.stack([v[n].reshape(KC, P).T for n in ("L0_xattn_bq", "L0_xattn_bk", "L1_ffn_bf", "L1_ffn_bi",
                                                          "L1_ffn_bc", "L1_ffn_in_c")], 1),
        "rows": np.stack([v["L0_xattn_bv"], v["L0_xattn_bo"], v["L1_ffn_bo"]]),
        "g": np.concatenate([v["g_xattn"], v["g_ffn"]]),
        "s": np.stack([v["L0_ffn_s0"], v["L0_ffn_s1"], v["L0_ffn_s2"]]),
        "k0": v["L0_ffn_k0"], "k1": v["L0_ffn_k1"], "k2": v["L0_ffn_k2"],
        "wf": v["L1_ffn_wf"].T, "wi": v["L1_ffn_wi"].T, "wc": v["L1_ffn_wc"].T, "wo_d": v["L1_ffn_wo"].T,
        "uf": v["L1_ffn_uf"].T, "ui": v["L1_ffn_ui"].T, "uc": v["L1_ffn_uc"].T, "uo_d": v["L1_ffn_uo"].T,
        "ident": np.eye(P, dtype=np.float32),
        "not_first": np.array([[0.0], [-1.0]], np.float32),
        "head_of_feature": (np.arange(P)[:, None] // DK == heads).astype(np.float32),
        "head_of_row": (row.T[:, :, None] // KEYS == heads).astype(np.float32),
        "row_heads": (np.arange(2 * ROWS).reshape(2, ROWS) // KEYS == np.arange(HEADS)[:, None, None]).astype(np.float32),
    }
    arrays = {k: np.ascontiguousarray(x) for k, x in arrays.items()}
    nc = bacc.Bacc("TRN2", target_bir_lowering=False, num_devices=1)
    aps = {k: nc.dram_tensor(f"in_{k}", x.shape, mybir.dt.from_np(x.dtype), kind="ExternalInput").ap()
           for k, x in arrays.items()}
    out = nc.dram_tensor("out_x", (T * NT, P, SUB, D), F32, kind="ExternalOutput").ap()
    build(nc, aps, out)
    r = run_bass_kernel_spmd(nc, [{f"in_{k}": x for k, x in arrays.items()}], core_ids=[0])
    return r.results[0]["out_x"].reshape(T, B, D)
```
